# Optimizing a Trainium2 kernel written in Bass

```python
import numpy as np
import jax
import jax.numpy as jnp

def _softmax(x, axis=-1):
    return jax.nn.softmax(x, axis=axis)

def _gelu(x):
    return jax.nn.gelu(x, approximate=True)

def _silu(x):
    return jax.nn.silu(x)

def _sigmoid(x):
    return jax.nn.sigmoid(x)

def _layernorm(x, axis=-1, eps=1e-05):
    m = jnp.mean(x, axis=axis, keepdims=True)
    v = jnp.var(x, axis=axis, keepdims=True)
    return (x - m) / jnp.sqrt(v + eps)

def _scatter_add(tgt, idx, src, axis=0):
    return tgt.at[idx].add(src)

def _segment_sum(src, seg, n):
    return jax.ops.segment_sum(src, seg, n)
kernel_name = 'mk_gnn_ffn_d1_gnn_r8_ab3d14'

def setup_inputs(seed: int=0):
    np.random.seed(seed)
    _w = jnp.asarray

    def _rec_inputs():
        import jax
        import jax.numpy as jnp
        _gk = jax.random.key(seed)
        x = -0.0003713 + 1 * jax.random.normal(jax.random.fold_in(_gk, 1), (12500, 256), jnp.float32)
        _s = jax.random.randint(jax.random.fold_in(_gk, 2), (100000,), 0, 12500, jnp.int32)
        _d = jax.random.randint(jax.random.fold_in(_gk, 3), (100000,), 0, 12500, jnp.int32)
        _loop = jnp.arange(12500, dtype=jnp.int32)
        src = jnp.concatenate([_s, _d, _loop])
        dst = jnp.concatenate([_d, _s, _loop])
        _o = jnp.argsort(dst, stable=True)
        src = src[_o]
        dst = dst[_o]
        return (x, src, dst)
    x, src, dst = _rec_inputs()

    def _L0_gnn_setup():
        import jax, jax.numpy as jnp
        import numpy as np
        N, F_IN, H, C = (6250, 256, 4, 64)
        E = 100000
        NEG_SLOPE = 0.2
        LN_EPS = 1e-05
        key = jax.random.key(seed)
        ks = jax.random.split(key, 8)
        x = jax.random.normal(ks[0], (N, F_IN), dtype=jnp.float32)
        edge_index = jax.random.randint(ks[1], (2, E), 0, N, dtype=jnp.int32)
        W = jax.random.normal(ks[2], (F_IN, H * C), dtype=jnp.float32) * (1.0 / np.sqrt(F_IN))
        att_src = jax.random.normal(ks[3], (H, C), dtype=jnp.float32) * (1.0 / np.sqrt(C))
        att_dst = jax.random.normal(ks[4], (H, C), dtype=jnp.float32) * (1.0 / np.sqrt(C))
        bias = jnp.zeros((H * C,), dtype=jnp.float32)
        ln_gamma = jnp.ones((H * C,), dtype=jnp.float32)
        ln_beta = jnp.zeros((H * C,), dtype=jnp.float32)
        return {'x': x, 'edge_index': edge_index, 'W': W, 'att_src': att_src, 'att_dst': att_dst, 'bias': bias, 'ln_gamma': ln_gamma, 'ln_beta': ln_beta}
    _L0_gnn_all = _L0_gnn_setup()
    _L0_gnn_in = {k: v for k, v in _L0_gnn_all.items() if k in ('W', 'att_src', 'att_dst', 'bias', 'ln_gamma', 'ln_beta')}
    del _L0_gnn_all

    def _L0_ffn_setup():
        import math
        import jax, jax.numpy as jnp
        import numpy as np
        CAPACITY_FACTOR = 1.25
        TOP_K = 2
        LN_EPS = 1e-05

        def _layer_norm(x, gamma, beta):
            mu = jnp.mean(x, axis=-1, keepdims=True)
            var = jnp.var(x, axis=-1, keepdims=True)
            return (x - mu) * jax.lax.rsqrt(var + LN_EPS) * gamma + beta
        key = jax.random.key(seed)
        ks = jax.random.split(key, 4)
        B, S, D, F, E = (8, 512, 256, 512, 8)
        x = jax.random.normal(ks[0], (B, S, D), dtype=jnp.float32)
        Wr = jax.random.normal(ks[1], (D, E), dtype=jnp.float32) / np.sqrt(D)
        br = jnp.zeros((E,), jnp.float32)
        W1 = jax.random.normal(ks[2], (E, D, F), dtype=jnp.float32) / np.sqrt(D)
        b1 = jnp.zeros((E, F), jnp.float32)
        W2 = jax.random.normal(ks[3], (E, F, D), dtype=jnp.float32) / np.sqrt(F)
        b2 = jnp.zeros((E, D), jnp.float32)
        gamma = jnp.ones((D,), jnp.float32)
        beta = jnp.zeros((D,), jnp.float32)
        return {'x': x, 'Wr': Wr, 'br': br, 'W1': W1, 'b1': b1, 'W2': W2, 'b2': b2, 'gamma': gamma, 'beta': beta}
    _L0_ffn_all = _L0_ffn_setup()
    _L0_ffn_in = {k: v for k, v in _L0_ffn_all.items() if k in ('Wr', 'br', 'W1', 'b1', 'W2', 'b2', 'gamma', 'beta')}
    del _L0_ffn_all
    return {'x': x, 'src': src, 'dst': dst, 'L0_gnn_W': _L0_gnn_in['W'], 'L0_gnn_att_src': _L0_gnn_in['att_src'], 'L0_gnn_att_dst': _L0_gnn_in['att_dst'], 'L0_gnn_bias': _L0_gnn_in['bias'], 'L0_gnn_ln_gamma': _L0_gnn_in['ln_gamma'], 'L0_gnn_ln_beta': _L0_gnn_in['ln_beta'], 'L0_ffn_Wr': _L0_ffn_in['Wr'], 'L0_ffn_br': _L0_ffn_in['br'], 'L0_ffn_W1': _L0_ffn_in['W1'], 'L0_ffn_b1': _L0_ffn_in['b1'], 'L0_ffn_W2': _L0_ffn_in['W2'], 'L0_ffn_b2': _L0_ffn_in['b2'], 'L0_ffn_gamma': _L0_ffn_in['gamma'], 'L0_ffn_beta': _L0_ffn_in['beta']}

def reference(x, src, dst, L0_gnn_W, L0_gnn_att_src, L0_gnn_att_dst, L0_gnn_bias, L0_gnn_ln_gamma, L0_gnn_ln_beta, L0_ffn_Wr, L0_ffn_br, L0_ffn_W1, L0_ffn_b1, L0_ffn_W2, L0_ffn_b2, L0_ffn_gamma, L0_ffn_beta):
    import jax
    import jax.numpy as jnp

    def _L0_gnn_ref(x, edge_index, W, att_src, att_dst, bias, ln_gamma, ln_beta):
        import jax, jax.numpy as jnp
        import numpy as np
        N, F_IN, H, C = (6250, 256, 4, 64)
        E = 100000
        NEG_SLOPE = 0.2
        LN_EPS = 1e-05
        n = x.shape[0]
        loops = jnp.arange(n, dtype=edge_index.dtype)
        src = jnp.concatenate([edge_index[0], loops])
        dst = jnp.concatenate([edge_index[1], loops])
        h = (x @ W).reshape(n, H, C)
        a_src = jnp.einsum('nhc,hc->nh', h, att_src)
        a_dst = jnp.einsum('nhc,hc->nh', h, att_dst)
        alpha = a_src[src] + a_dst[dst]
        alpha = jax.nn.leaky_relu(alpha, NEG_SLOPE)
        amax = jax.ops.segment_max(alpha, dst, num_segments=n)
        alpha = jnp.exp(alpha - amax[dst])
        asum = jax.ops.segment_sum(alpha, dst, num_segments=n)
        alpha = alpha / (asum[dst] + 1e-16)
        msg = alpha[:, :, None] * h[src]
        out = jax.ops.segment_sum(msg, dst, num_segments=n)
        out = out.reshape(n, H * C) + bias
        mu = out.mean(axis=-1, keepdims=True)
        var = out.var(axis=-1, keepdims=True)
        out = (out - mu) * jax.lax.rsqrt(var + LN_EPS) * ln_gamma + ln_beta
        return jax.nn.relu(out)

    def _L0_ffn_ref(x, Wr, br, W1, b1, W2, b2, gamma, beta):
        import math
        import jax, jax.numpy as jnp
        import numpy as np
        CAPACITY_FACTOR = 1.25
        TOP_K = 2
        LN_EPS = 1e-05

        def _layer_norm(x, gamma, beta):
            mu = jnp.mean(x, axis=-1, keepdims=True)
            var = jnp.var(x, axis=-1, keepdims=True)
            return (x - mu) * jax.lax.rsqrt(var + LN_EPS) * gamma + beta
        B, S, D = x.shape
        E = Wr.shape[1]
        N = B * S
        K = TOP_K
        logits = jnp.mean(x, axis=1) @ Wr + br
        routing_weights = jax.nn.softmax(logits, axis=-1)
        capacity = float(math.ceil(N * CAPACITY_FACTOR / E))
        expected_loads = routing_weights.sum(axis=0) * (N / B)
        scale = jnp.where(expected_loads > capacity, capacity / expected_loads, 1.0)
        routing_weights = jax.nn.softmax(routing_weights * scale, axis=-1)
        rw_tok = jnp.broadcast_to(routing_weights[:, None, :], (B, S, E)).reshape(N, E)
        top_w, top_i = jax.lax.top_k(rw_tok, K)
        top_w = jax.nn.softmax(top_w, axis=-1)
        xf = x.reshape(N, D)
        h = jax.nn.gelu(jnp.einsum('nd,edf->enf', xf, W1) + b1[:, None, :], approximate=False)
        y = jnp.einsum('enf,efd->end', h, W2) + b2[:, None, :]
        w_dense = jnp.zeros((N, E), x.dtype).at[jnp.arange(N)[:, None], top_i].add(top_w)
        out = jnp.einsum('ne,end->nd', w_dense, y).reshape(B, S, D)
        out = _layer_norm(out + x, gamma, beta)
        return out
    edge_index = jnp.stack([src, dst])
    x = x + _L0_gnn_ref(_layernorm(x, axis=-1), edge_index, L0_gnn_W, L0_gnn_att_src, L0_gnn_att_dst, L0_gnn_bias, L0_gnn_ln_gamma, L0_gnn_ln_beta)
    x = x + _L0_ffn_ref(_layernorm(x, axis=-1)[None], L0_ffn_Wr, L0_ffn_br, L0_ffn_W1, L0_ffn_b1, L0_ffn_W2, L0_ffn_b2, L0_ffn_gamma, L0_ffn_beta)[0]
    return x

_drawn_inputs = setup_inputs


def setup_inputs(seed=0):
    import zlib

    import numpy as np

    out = dict(_drawn_inputs(seed))
    spreads = {'L0_gnn_bias': (0.0, 0.1),
     'L0_gnn_ln_gamma': (1.0, 0.2),
     'L0_gnn_ln_beta': (0.0, 0.1),
     'L0_ffn_br': (0.0, 0.8),
     'L0_ffn_b1': (0.0, 0.406),
     'L0_ffn_b2': (0.0, 0.277),
     'L0_ffn_gamma': (1.0, 0.2),
     'L0_ffn_beta': (0.0, 0.1)}
    factors = {}
    for name, (base, spread) in spreads.items():
        noise = np.random.default_rng([zlib.crc32(name.encode()), seed]).standard_normal(out[name].shape)
        drawn = base * np.exp(spread * noise) if base else spread * noise
        out[name] = jnp.asarray(drawn.astype(out[name].dtype))
    for name, factor in factors.items():
        out[name] = (out[name] * factor).astype(out[name].dtype)
    return out
```

```python
from contextlib import ExitStack
import math

import concourse.bass as bass
from concourse import mybir

F32 = mybir.dt.float32
I32 = mybir.dt.int32
U32 = mybir.dt.uint32
ALU = mybir.AluOpType
ACT = mybir.ActivationFunctionType
X = mybir.AxisListType.X

P = 128
TILES = 14
CHUNK = TILES * P
ROWS_RING = 4
NEG_SLOPE, LN_EPS, DEN_EPS = 0.2, 1e-5, 1e-16
BIG = 1e30
CAPACITY_FACTOR = 1.25
GROUP = 512


def sizes(N, E):
    chunks = -(-E // CHUNK)
    steps = chunks + N // P + 1 + 1
    steps += 1 - steps % 2
    blocks = -(-(N + 3 * P) // P)
    blocks = -(-blocks // ROWS_RING) * ROWS_RING
    groups = -(-N // GROUP)
    return chunks, steps, blocks, groups


class At:

    def __init__(self, k, mul, off):
        self.k, self.mul, self.off = k, mul, off

    def number(self, lead=0):
        return self.k * self.mul + (self.off + lead)

    def slot(self, lead=0):
        return (self.off + lead) % self.mul

    def landed(self, dmas, lead=0):
        return self.k * (16 * dmas) + 16 * dmas * ((self.off + lead) // self.mul + 1)


class Ticks:

    def __init__(self, sem, names, back):
        self.sem, self.names, self.back, self.at = sem, names.split(), back, 0
        assert len(set(self.names)) == len(self.names)

    def mark(self, name, ins):
        assert self.names[self.at % len(self.names)] == name, (name, self.names[self.at % len(self.names)])
        self.at += 1
        ins.then_inc(self.sem, 1)

    def value(self, name, at, lead=0):
        n = len(self.names)
        return at.k * (n * at.mul) + ((at.off + lead + self.back) * n + self.names.index(name) + 1)

    def wait(self, eng, name, at, lead=0):
        eng.wait_ge(self.sem, self.value(name, at, lead))

    def skip(self, eng, names, at):
        i = self.names.index(names[0])
        assert self.names[i:i + len(names)] == list(names) and self.at % len(self.names) == i
        eng.wait_ge(self.sem, self.value(names[0], at) - 1)
        eng.sem_inc(self.sem, len(names))
        self.at += len(names)

    def credit(self, eng, ahead=()):
        eng.sem_inc(self.sem, len(self.names) * (self.back - bool(ahead)))

    def rest(self, eng, ahead):
        n, a = len(self.names), len(ahead)
        assert self.names[:a] == list(ahead) and self.at == a
        eng.wait_ge(self.sem, n * (self.back - 1) + a)
        eng.sem_inc(self.sem, n - a)
        self.at = 0


def build(nc, x, src_t, dst, dst_t, W, att_src, att_dst, g_bias, g_gamma, g_beta, Wr, br, W1, b1, W2, b2,
          f_gamma, f_beta, out, N, E):
    D = x.shape[1]
    H, C = att_src.shape
    NE, _, F = W1.shape
    KD, KF = D // P, F // P
    chunks, STEPS, BLOCKS, GROUPS = sizes(N, E)
    HC1 = H * (C + 1)
    ONE, AS, AD = HC1, HC1 + 1, HC1 + 1 + H
    TW = AD + H
    R5 = 1 + H
    SR = R5 * TILES
    SHIFT, HAS = HC1, HC1 + H
    AW = HAS + 1
    SCHED = 256
    assert STEPS + 3 <= SCHED and SR <= P and D == H * C
    QB = GROUP // P
    XO_ROWS = (GROUPS + 1) * GROUP

    with ExitStack() as ctx:
        def sb(name, shape, dt=F32):
            return ctx.enter_context(nc.sbuf_tensor(name, shape, dt))

        def sem(name):
            return ctx.enter_context(nc.semaphore(name))

        bank = [ctx.enter_context(nc.psum_tensor(f"bank{i}", [P, 512], F32)) for i in range(8)]
        table = nc.dram_tensor("table", [BLOCKS * P, TW], F32, kind="Internal").ap()
        x_mid = nc.dram_tensor("x_mid", [XO_ROWS, D], F32, kind="Internal").ap()
        sched = nc.dram_tensor("sched", [2, SCHED], I32, kind="Internal").ap()

        ident = sb("ident", [P, P])
        iota_row = sb("iota_row", [P, P])
        iota_col = sb("iota_col", [P, 1])
        ones = sb("ones", [P, P])
        eps = sb("eps", [P, 1])
        zeros = sb("zeros", [P, D])
        g_aff = sb("g_aff", [P, 3, D])
        f_aff = sb("f_aff", [P, 2, D])

        wx = sb("wx", [P, KD, D + 2 * H])
        att = sb("att", [P, 2, D])
        att_tmp = sb("att_tmp", [P, D])
        x_in = sb("x_in", [P, ROWS_RING, D])
        xT = sb("xT", [P, 2, KD, P])
        st1 = sb("st1", [P, ROWS_RING, 6])
        mv1 = sb("mv1", [P, ROWS_RING, 2])
        y1 = sb("y1", [P, ROWS_RING, 2])
        row_out = sb("row_out", [P, ROWS_RING, TW])

        first = sb("first", [1, 257], I32)
        gap = sb("gap", [1, 256], I32)
        lows = sb("lows", [1, 3, 256])
        s_both = sb("s_both", [P, 2, 256])
        s_cmp = sb("s_cmp", [P, 2, 256])
        s_col = sb("s_col", [P, 2, 4])
        s_out_i = sb("s_out_i", [P, 2, 2], I32)
        step_tab = sb("step_tab", [P, 2, SCHED], I32)
        w_tab = sb("w_tab", [P, SCHED])
        tot_i = sb("tot_i", [1, 2], I32)

        idx = [sb(f"idx{i}", [P, TILES], I32) for i in range(2)]
        dst_e = sb("dst_e", [P, 2, TILES], I32)
        dst_s = sb("dst_s", [SR, 2, P], I32)
        dst_b = sb("dst_b", [P, 2, CHUNK], I32)
        tab_w = sb("tab_w", [P, 2, TW])
        x_w = sb("x_w", [P, 2, D])
        rows = sb("rows", [P, 2, TILES, TW])
        msg = sb("msg", [P, 2, TILES, HC1])
        oh = sb("oh", [P, 2, TILES, P])
        ohT = sb("ohT", [P, 2, TILES, P])
        wcur = sb("wcur", [P, 2, 2])
        node = sb("node", [P, 2])
        drel = sb("drel", [P, 2, TILES])
        sel = sb("sel", [P, 2])
        mask = sb("mask", [P, 2])
        newseg = sb("newseg", [SR, 2, P + 1])
        pen = sb("pen", [SR, 2, P])
        asrc = sb("asrc", [P, SR])
        runmax = sb("runmax", [SR, P])
        lastmax = sb("lastmax", [SR, P])
        lastmax_e = sb("lastmax_e", [P, SR])
        nohas = sb("nohas", [P, TILES])
        mtile = sb("mtile", [P, TILES, H])
        mnode = sb("mnode", [P, H])
        zn = sb("zn", [P, H])
        adsh = sb("adsh", [P, 2, 2 * H])
        ze = sb("ze", [P, TILES, H])
        le = sb("le", [P, TILES, H])
        we = sb("we", [P, 2, TILES, H])
        acc = sb("acc", [P, AW])
        carry = sb("carry", [1, AW])
        r_t = sb("r_t", [1, 1])
        r_sc = sb("r_sc", [1, H])
        r_mn = sb("r_mn", [1, H])
        r_d = sb("r_d", [1, 2 * H])
        r_f = sb("r_f", [1, 2 * H])
        r_c = sb("r_c", [1, HC1])
        zs = sb("zs", [P, H])
        ws = sb("ws", [P, H])
        num = sb("num", [P, HC1])
        rden = sb("rden", [P, H])
        o = sb("o", [P, D])
        st2 = sb("st2", [P, 6])
        mv2 = sb("mv2", [P, 4])
        ln2 = sb("ln2", [P, 4])
        vv = sb("vv", [P, 2])
        nt = sb("nt", [P, 3])
        m_lhs = sb("m_lhs", [P, 2])
        x_o = sb("x_o", [P, 2, D + 1])

        zrow = sb("zrow", [1, D + 1])
        zcol = sb("zcol", [P, KD])
        wr_sb = sb("wr_sb", [P, KD, NE])
        rt = sb("rt", [1, 16, NE])
        top_i = sb("top_i", [1, NE], U32)
        top_ii = sb("top_ii", [1, NE], I32)
        wtop = sb("wtop", [P, 2])
        w1_sb = sb("w1_sb", [P, 2, KD, F])
        w2_sb = sb("w2_sb", [P, 2, KF, D])
        b1_sb = sb("b1_sb", [P, 2, KF])
        b2_sb = sb("b2_sb", [P, 2, D])
        b2_w = sb("b2_w", [P, D])
        fx = sb("fx", [P, 3, QB, D])
        fst = sb("fst", [P, QB, 6])
        fmv = sb("fmv", [P, QB, 2])
        fln = sb("fln", [P, QB])
        fy = sb("fy", [P, QB])
        fv = sb("fv", [P, QB])
        ft = sb("ft", [P, QB])
        fxn = msg[:, :, :, :].rearrange("p a t c -> p (a t c)")[:, 0:2 * QB * D]\
            .rearrange("p (a q d) -> p a q d", a=2, q=QB)
        fxT = oh[:, :, :, :].rearrange("p a t c -> p (a t c)")[:, 0:2 * KD * GROUP]\
            .rearrange("p (a k n) -> p a k n", a=2, k=KD)
        hT = rows[:, :, :, :].rearrange("p a t c -> p (a t c)")[:, 0:2 * KF * GROUP]\
            .rearrange("p (f n) -> p f n", f=2 * KF)
        fo = sb("fo", [P, 2, QB, D])

        s_w = sem("s_w")
        s_x = [sem(f"s_x{i}") for i in range(ROWS_RING)]
        s_tab = [sem(f"s_tab{i}") for i in range(ROWS_RING)]
        s_pad = sem("s_pad")
        s_sched = sem("s_sched")
        s_idx = [sem(f"s_idx{i}") for i in range(2)]
        s_dst = [sem(f"s_dst{i}") for i in range(2)]
        s_rows = [sem(f"s_rows{i}") for i in range(2)]
        s_win = [sem(f"s_win{i}") for i in range(2)]
        s_mid = sem("s_mid")
        s_fwr = sem("s_fwr")
        s_fw = sem("s_fw")
        s_fx = [sem(f"s_fx{i}") for i in range(3)]
        s_out = sem("s_out")
        s_const = sem("s_const")
        s_pool = sem("s_pool")
        s_setup = sem("s_setup")
        s_once = sem("s_once")
        s_exp = sem("s_exp")
        s_granted = sem("s_granted")
        s_dve_held = sem("s_dve_held")
        s_sp_held = sem("s_sp_held")

        p1_pe = Ticks(sem("p1_pe"), "xT rows", 4)
        p1_dve = Ticks(sem("p1_dve"), "stats mv xT logits", 4)
        p1_act = Ticks(sem("p1_act"), "ln rstd rows", 4)
        DVE_A = "wcur node drel newseg pen ohT oh".split()
        DVE_F1 = "r_t r_sc r_mn r_d1 r_d".split()
        DVE_F2 = "accshift mergescale carrypart merged mergedshift self_z self_l self_d".split()
        DVE_F3 = "carry selfmsg num den rden attn biased st mv v".split()
        DVE_F4 = "n1 n2 rstd normed gam bet xmid st_m mv_m v_m".split()
        DVE_F5 = "m1 m2 m_rstd lhs mu".split()
        MSGS = [f"msg{i}" for i in range(TILES // 2)]
        dve2 = Ticks(sem("dve2"), " ".join(
            DVE_A + ["runmax", "lastmax", "sel", "mask"] + DVE_F1
            + "nohas mtile mnode maxself ad zn shift".split() + DVE_F2 + "ze le d dmin".split() + DVE_F3
            + MSGS[:4] + DVE_F4 + MSGS[4:] + DVE_F5), 3)
        act2 = Ticks(sem("act2"), "asrc acc lastT rexp wself we ln1 y1 ln2 y2", 3)
        pe2 = Ticks(sem("pe2"), "lT lastT nodemax expand carry agg router", 3)
        sp2 = Ticks(sem("sp2"), "stored", 3)
        DVE3_A = "st mv v n1 n2 rstd xn xT".split()
        HID = [f"h{i}" for i in range(2 * KF)]
        dve3 = Ticks(sem("dve3"), " ".join(DVE3_A) + " res b2 st2 mv2 v2 m1 m2 rstd2 yn gam bet out", 2)
        act3 = Ticks(sem("act3"), "ln y " + " ".join(HID) + " ln2 y2", 2)
        pe3 = Ticks(sem("pe3"), "xT " + " ".join(HID) + " out", 2)
        sp3 = Ticks(sem("sp3"), "stored", 3)

        psX = [bank[i][:, 0:KD * P].rearrange("p (k n) -> p k n", k=KD) for i in (0, 1)]
        psH = [bank[i][:, 0:D + 2 * H] for i in (2, 3)]
        psW = bank[4][:, 0:D + 2 * H]
        psS = bank[5]
        psT, psR, psM = bank[0][0:SR, 0:P], bank[1][:, 0:SR], bank[2][:, 0:SR]
        psE = bank[3][:, 0:2 * H * TILES]
        psA = [bank[i][:, 0:HC1] for i in (4, 5)]
        psC, psZ = bank[6][0:1, 0:AW], bank[7][0:1, 0:D + 1]
        psF = [bank[i][:, :] for i in (0, 1)]
        psU = [bank[i][:, :] for i in (2, 3, 4, 5)]
        psY = [bank[i][:, :].rearrange("p (q d) -> p q d", d=D) for i in (6, 7)]

        N_ATT = 1 + 4 * KD
        N_WX = N_ATT + KD
        N_LOWS = N_WX + 8
        N_SETUP = N_LOWS + 1 + 2 * 9
        N_MEAN = N_SETUP + 1 + 2
        N_EXP = [N_MEAN + 4, N_MEAN + 13, N_MEAN + 20]
        N_TOP = N_EXP[2] + 3
        N_EXPERT = N_TOP + 5
        WTOP = 9

        block = ctx.enter_context(nc.Block())

        def row(v):
            return v.rearrange("(a d) -> a d", a=1)

        def head_cols(ap):
            return ap.rearrange("p (h c) -> p h c", h=H)

        def over(ap, n):
            return ap.unsqueeze(len(ap.shape)).to_broadcast([*ap.shape, n])

        def hold(eng, counted):
            eng.sem_inc(counted, 1)

        def walk(eng, total, step):
            step(At(0, 2, 0), False)
            with eng.Fori(0, (STEPS - 1) // 2) as k:
                for j in (1, 2):
                    at = At(k, 2, j)
                    with eng.If(at.number() < total):
                        step(at, True)

        def steps_to_run(eng):
            eng.wait_ge(s_sched, 64)
            return eng.value_load(tot_i[0:1, 0:1], min_val=2, max_val=STEPS)

        @block.sync
        def _(sp):
            sp.dma_start(wx[:, :, 0:D], W.rearrange("(k p) n -> p k n", p=P)).then_inc(s_w, 16)
            for i, v in enumerate((att_src, att_dst)):
                sp.dma_start(att[:, i, :], v.rearrange("(a h) c -> a (h c)", a=1).to_broadcast([P, D])).then_inc(s_w, 16)
            for b in range(3):
                sp.dma_start(x_in[:, b, :], x[b * P:(b + 1) * P, :]).then_inc(s_x[b], 16)
            for i, v in enumerate((g_bias, g_gamma, g_beta)):
                sp.dma_start(g_aff[:, i, :], row(v).to_broadcast([P, D])).then_inc(s_w, 16)
            sp.wait_ge(s_setup, 1)
            sp.dma_start(first[:, 0:chunks],
                         dst[0:chunks * CHUNK].rearrange("(a c e) -> a c e", a=1, e=CHUNK)[:, :, 0],
                         allow_slow_non_contiguous=True).then_inc(s_sched, 16)
            sp.wait_ge(s_const, 7)
            pads = [(r, min(P, XO_ROWS - r)) for r in range(N, XO_ROWS, P)]
            for i, (r, n) in enumerate(pads):
                sp.dma_start(x_mid[r:r + n, :], zeros[0:n, :]).then_inc(s_tab[i] if i < ROWS_RING else s_pad, 16)
            with sp.Fori(0, BLOCKS // ROWS_RING) as k:
                for j in range(ROWS_RING):
                    at = At(k, ROWS_RING, j)
                    p1_dve.wait(sp, "stats", at, -1)
                    hold(sp, s_sp_held)
                    p1_pe.wait(sp, "xT", at, -2)
                    hold(sp, s_sp_held)
                    sp.dma_start(x_in[:, at.slot(3), :], x[bass.ds(at.number(3) * P, P), :])\
                      .then_inc(s_x[at.slot(3)], 16)
                    p1_act.wait(sp, "rows", at)
                    hold(sp, s_sp_held)
                    p1_dve.wait(sp, "logits", at)
                    hold(sp, s_sp_held)
                    sp.dma_start(table[bass.ds(at.number() * P, P), :], row_out[:, j, :]).then_inc(s_tab[j], 16)
            for j in range(ROWS_RING):
                sp.wait_ge(s_tab[j], 16 * (BLOCKS // ROWS_RING + 1))
                sp.wait_ge(s_x[j], 16 * (BLOCKS // ROWS_RING + (j < 3)))
            sp.wait_ge(s_pad, 16 * (len(pads) - ROWS_RING))
            sp.wait_ge(s_setup, N_SETUP)
            for i in range(2):
                sp.dma_start(sched[i, :].rearrange("(b p) -> p b", p=P), s_out_i[:, i, :],
                             allow_slow_non_contiguous=True).then_inc(s_sched, 16)
            sp.wait_ge(s_sched, 48)
            sp.dma_start(step_tab[:, :, :].rearrange("p a s -> p (a s)"),
                         sched.rearrange("(o a) s -> o (a s)", o=1).to_broadcast([P, 2 * SCHED])).then_inc(s_sched, 16)
            total = steps_to_run(sp)

            def load_edges(at, lead):
                slot = at.slot(lead)
                c = sp.value_load(step_tab[0:1, 1, bass.ds(at.number(lead), 1)], min_val=0, max_val=chunks - 1)
                sp.dma_start(idx[slot][:, :], src_t[bass.ds(c * P, P), :]).then_inc(s_idx[slot], 16)
                sp.dma_start(dst_e[:, slot, :], dst_t[bass.ds(c * P, P), :]).then_inc(s_dst[slot], 16)
                sp.dma_start(dst_s[:, slot, :], dst.rearrange("(t o e) -> t o e", o=1, e=P)
                             [bass.ds(c * TILES, TILES), :, :].to_broadcast([TILES, R5, P])).then_inc(s_dst[slot], 16)
                sp.dma_start(dst_b[:, slot, :], dst.rearrange("(a e) -> a e", e=CHUNK)
                             [bass.ds(c, 1), :].to_broadcast([P, CHUNK])).then_inc(s_dst[slot], 16)

            def load_window(at, lead):
                slot = at.slot(lead)
                w = sp.value_load(step_tab[0:1, 0, bass.ds(at.number(lead), 1)], min_val=0, max_val=N + P)
                sp.dma_start(tab_w[:, slot, :], table[bass.ds(w, P), :]).then_inc(s_win[slot], 16)
                sp.dma_start(x_w[:, slot, :], x[bass.ds(w, P), :]).then_inc(s_win[slot], 16)

            def step(at, follows):
                sp.wait_ge(s_rows[at.slot()], at.landed(TILES))
                hold(sp, s_sp_held)
                dve2.wait(sp, "oh", at, -1)
                hold(sp, s_sp_held)
                load_edges(at, 2)
                if not follows:
                    load_window(at, 1)
                    sp2.skip(sp, ["stored"], at)
                    return
                dve2.wait(sp, "xmid", at)
                hold(sp, s_sp_held)
                w = sp.value_load(step_tab[0:1, 0, bass.ds(at.number(-1), 1)], min_val=0, max_val=N)
                sp.dma_start(x_mid[bass.ds(w, P), :], x_o[:, at.slot(-1), 0:D]).then_inc(s_mid, 16)
                load_window(at, 1)
                sp.wait_ge(s_mid, at.k * (16 * at.mul) + 16 * at.off)
                hold(sp, s_sp_held)
                sp2.skip(sp, ["stored"], at)

            sp2.credit(sp)
            load_edges(At(0, 2, 0), 0)
            load_edges(At(0, 2, 0), 1)
            load_window(At(0, 2, 0), 0)
            walk(sp, total, step)
            for slot in range(2):
                edges, windows = (total + (3 - slot)) // 2, (total + (2 - slot)) // 2
                for s, n in ((s_idx, edges * 16), (s_dst, edges * 48), (s_win, windows * 32)):
                    sp.wait_ge(s[slot], n)
                    hold(sp, s_sp_held)

            sp.dma_start(wr_sb[:, :, :], Wr.rearrange("(k p) e -> p k e", p=P)).then_inc(s_fwr, 16)
            sp.dma_start(rt[:, 0, :], row(br)).then_inc(s_fwr, 16)
            for i, v in enumerate((f_gamma, f_beta)):
                sp.dma_start(f_aff[:, i, :], row(v).to_broadcast([P, D])).then_inc(s_fwr, 16)

            def load_group(at, lead):
                sp.dma_start(fx[:, at.slot(lead), :, :],
                             x_mid[bass.ds(at.number(lead) * GROUP, GROUP), :].rearrange("(q p) d -> p q d", p=P))\
                  .then_inc(s_fx[at.slot(lead)], 16)

            load_group(At(0, 3, 0), 0)
            load_group(At(0, 3, 0), 1)
            sp.wait_ge(s_setup, N_TOP)
            for i in range(2):
                e = sp.value_load(top_ii[0:1, i:i + 1], min_val=0, max_val=NE - 1)
                sp.dma_start(w1_sb[:, i, :, :],
                             W1[bass.ds(e, 1), :, :].rearrange("o (k p) f -> p (o k) f", p=P)).then_inc(s_fw, 16)
                sp.dma_start(w2_sb[:, i, :, :],
                             W2[bass.ds(e, 1), :, :].rearrange("o (k p) f -> p (o k) f", p=P)).then_inc(s_fw, 16)
                sp.dma_start(b1_sb[:, i, :], b1[bass.ds(e, 1), :].rearrange("o (k p) -> p (o k)", p=P),
                             allow_slow_non_contiguous=True).then_inc(s_fw, 16)
                sp.dma_start(b2_sb[:, i, :], b2[bass.ds(e, 1), :].to_broadcast([P, D])).then_inc(s_fw, 16)
            sp3.credit(sp)
            with sp.Fori(0, (GROUPS - 1) // 6) as k:
                for j in range(6):
                    at3, at2 = At(k * 2, 3, j), At(k * 3, 2, j)
                    dve3.wait(sp, "out", at2, -1)
                    hold(sp, s_sp_held)
                    load_group(at3, 2)
                    dve3.wait(sp, "out", at2)
                    hold(sp, s_sp_held)
                    sp.dma_start(out[bass.ds(at2.number() * GROUP, GROUP), :].rearrange("(q p) d -> p q d", p=P),
                                 fo[:, at2.slot(), :, :]).then_inc(s_out, 16)
                    sp.wait_ge(s_out, at2.k * 32 + 16 * (j + 1))
                    hold(sp, s_sp_held)
                    sp3.skip(sp, ["stored"], at2)
            last = At(0, 2, GROUPS - 1)
            dve3.wait(sp, "out", last)
            hold(sp, s_sp_held)
            tail = [(r, min(P, N - r)) for r in range((GROUPS - 1) * GROUP, N, P)]
            for q, (r, n) in enumerate(tail):
                sp.dma_start(out[r:r + n, :], fo[0:n, last.slot(), q, :]).then_inc(s_out, 16)
            sp.wait_ge(s_out, 16 * (GROUPS - 1 + len(tail)))
            for j in range(3):
                sp.wait_ge(s_fx[j], 16 * len([g for g in range(GROUPS + 1) if g % 3 == j]))

        @block.gpsimd
        def _(pool):
            pool.iota(iota_row[:, :], [[1, P]], base=0, channel_multiplier=0,
                      allow_small_or_imprecise_dtypes=True).then_inc(s_const, 1)
            pool.iota(iota_col[:, :], [[0, 1]], base=0, channel_multiplier=1,
                      allow_small_or_imprecise_dtypes=True).then_inc(s_const, 1)
            pool.memset(ones[:, :], 1.0).then_inc(s_const, 1)
            pool.memset(eps[:, :], LN_EPS).then_inc(s_const, 1)
            pool.memset(zeros[:, :], 0.0).then_inc(s_const, 1)
            pool.memset(ident[:, :], 0.0).then_inc(s_const, 1)
            pool.wait_ge(s_const, 6)
            pool.affine_select(out=ident[:, :], in_=ident[:, :], compare_op=ALU.not_equal, fill=1.0, base=0,
                               pattern=[[-1, P]], channel_multiplier=1).then_inc(s_const, 1)
            pool.memset(row_out[:, :, :], 1.0).then_inc(s_pool, 1)
            pool.memset(newseg[:, :, :], 1.0).then_inc(s_pool, 1)
            pool.memset(acc[:, :], 1.0).then_inc(s_pool, 1)
            pool.memset(carry[:, :], 0.0).then_inc(s_pool, 1)
            for j in range(ROWS_RING):
                pool.wait_ge(s_tab[j], 16 * (BLOCKS // ROWS_RING + 1))
            total = steps_to_run(pool)
            bound = pool.to_reg(BLOCKS * P - 1)

            def gather(at, follows):
                slot = at.slot()
                pool.wait_ge(s_idx[slot], at.landed(1))
                dve2.wait(pool, MSGS[-1], at, -2)
                act2.wait(pool, "asrc", at, -2)
                hold(pool, s_granted)
                for t in range(TILES):
                    pool.indirect_dma_start(rows[:, slot, t, :], None, table,
                                            bass.IndirectOffsetOnAxis(ap=idx[slot][:, t:t + 1], axis=0),
                                            bounds_check=bound, oob_is_err=False).then_inc(s_rows[slot], 16)

            walk(pool, total, gather)

        @block.tensor
        def _(pe):
            pe.wait_ge(s_setup, N_ATT)
            for k in range(KD):
                mm = pe.matmul(psW, ones[:, :], wx[:, k, :], start=(k == 0), stop=(k == KD - 1))
            mm.then_inc(s_once, 1)
            p1_pe.credit(pe, ahead=["xT"])

            def transpose_x(at, lead):
                pe.wait_ge(s_x[at.slot(lead)], at.landed(1, lead))
                p1_dve.wait(pe, "xT", at, lead - 2)
                for k in range(KD):
                    mm = pe.transpose(psX[(at.off + lead) % 2][:, k, :], x_in[:, at.slot(lead), k * P:(k + 1) * P],
                                      ident[:, :])
                p1_pe.mark("xT", mm)

            transpose_x(At(0, ROWS_RING, 0), 0)
            p1_pe.rest(pe, ["xT"])
            pe.wait_ge(s_setup, N_WX)
            with pe.Fori(0, BLOCKS // ROWS_RING) as k:
                for j in range(ROWS_RING):
                    at = At(k, ROWS_RING, j)
                    transpose_x(at, 1)
                    p1_dve.wait(pe, "xT", at)
                    p1_act.wait(pe, "rows", at, -2)
                    p1_dve.wait(pe, "logits", at, -2)
                    for kk in range(KD):
                        mm = pe.matmul(psH[j % 2], xT[:, j % 2, kk, :], wx[:, kk, :], start=(kk == 0),
                                       stop=(kk == KD - 1))
                    p1_pe.mark("rows", mm)
            pe.wait_ge(s_setup, N_LOWS)
            pe.matmul(psS[:, 0:256], ones[0:1, :], lows[0:1, 1, :], start=True, stop=True)
            pe.matmul(psS[:, 256:512], ones[0:1, :], lows[0:1, 2, :], start=True, stop=True).then_inc(s_once, 1)
            pe.matmul(bank[7][0:1, 0:D], zeros[:, 0:1], zeros[:, :], start=True, stop=False, skip_group_check=True)
            pe.matmul(bank[7][0:1, D:D + 1], zeros[:, 0:1], zeros[:, 0:1], start=False, stop=False,
                      skip_group_check=True)
            pe2.credit(pe)
            p1_end = At(BLOCKS // ROWS_RING - 1, ROWS_RING, ROWS_RING - 1)
            p1_act.wait(pe, "rows", p1_end)
            p1_dve.wait(pe, "logits", p1_end)
            total = steps_to_run(pe)

            def step(at, follows):
                s, q = at.slot(), at.slot(-1)
                act2.wait(pe, "asrc", at)
                dve2.wait(pe, "runmax", at, -1)
                pe2.mark("lT", pe.matmul(psT, asrc[:, :], ident[:, :], start=True, stop=True))
                dve2.wait(pe, "lastmax", at)
                act2.wait(pe, "lastT", at, -1)
                pe2.mark("lastT", pe.matmul(psR, lastmax[:, :], ident[0:SR, 0:SR], start=True, stop=True))
                act2.wait(pe, "lastT", at)
                dve2.wait(pe, "oh", at, -1)
                dve2.wait(pe, "mtile", at, -1)
                for t in range(TILES):
                    mm = pe.matmul(psM[:, t * R5:(t + 1) * R5], oh[:, s, t, :], lastmax_e[:, t * R5:(t + 1) * R5],
                                   start=True, stop=True)
                pe2.mark("nodemax", mm)
                dve2.wait(pe, "shift", at)
                dve2.wait(pe, "d", at, -1)
                for t in range(TILES):
                    mm = pe.matmul(psE[:, t * 2 * H:(t + 1) * 2 * H], ohT[:, s, t, :], adsh[:, s, :],
                                   start=True, stop=True)
                pe2.mark("expand", mm)
                if follows:
                    dve2.wait(pe, "mergedshift", at)
                    dve2.wait(pe, "carry", at, -1)
                    pe2.mark("carry", pe.matmul(psC, sel[:, q:q + 1], acc[:, :], start=True, stop=True))
                else:
                    pe2.skip(pe, ["carry"], at)
                act2.wait(pe, "acc", at, -1)
                for t in range(TILES):
                    if t % 2 == 0:
                        dve2.wait(pe, MSGS[t // 2], at)
                    mm = pe.matmul(psA[s], oh[:, s, t, :], msg[:, s, t, :], start=(t == 0), stop=(t == TILES - 1))
                pe2.mark("agg", mm)
                if follows:
                    dve2.wait(pe, "mu", at)
                    pe2.mark("router", pe.matmul(psZ, m_lhs[:, q:q + 1], x_o[:, q, :], start=False, stop=False,
                                                 skip_group_check=True))
                else:
                    pe2.skip(pe, ["router"], at)

            walk(pe, total, step)
            pe.drain().then_inc(s_once, 1)
            pe.wait_ge(s_setup, N_MEAN)
            for k in range(KD):
                mm = pe.matmul(bank[0][:, k:k + 1], zrow[0:1, k * P:(k + 1) * P], ones[0:1, 0:1], start=True, stop=True)
            mm.then_inc(s_once, 1)
            pe.wait_ge(s_setup, N_MEAN + 1)
            pe.wait_ge(s_fwr, 64)
            for k in range(KD):
                mm = pe.matmul(bank[1][0:1, 0:NE], zcol[:, k:k + 1], wr_sb[:, k, :], start=(k == 0), stop=(k == KD - 1))
            mm.then_inc(s_once, 1)
            pe.wait_ge(s_setup, N_TOP)
            pe.matmul(bank[2][:, 0:2], ones[0:1, :], rt[0:1, WTOP, 0:2], start=True, stop=True).then_inc(s_once, 1)

            pe3.credit(pe, ahead=["xT"])

            def transpose_rows(at, lead):
                dve3.wait(pe, "xn", at, lead - 1)
                dve3.wait(pe, "xT", at, lead - 2)
                for k in range(KD):
                    for q in range(QB):
                        mm = pe.transpose(psF[k][:, q * P:(q + 1) * P],
                                          fxn[:, at.slot(lead), q, k * P:(k + 1) * P], ident[:, :])
                pe3.mark("xT", mm)

            def group(at):
                transpose_rows(at, 1)
                dve3.wait(pe, "xT", at, -1)
                for f in range(2 * KF):
                    e, fk = divmod(f, KF)
                    u = psU[f % len(psU)]
                    g = f - len(psU)
                    act3.wait(pe, HID[g], at, 0 if g >= 0 else -1)
                    for k in range(KD):
                        mm = pe.matmul(u, w1_sb[:, e, k, fk * P:(fk + 1) * P], fxT[:, at.slot(), k, :],
                                       start=(k == 0), stop=(k == KD - 1))
                    pe3.mark(HID[f], mm)
                dve3.wait(pe, "res", at, -1)
                for q in range(QB):
                    for f in range(2 * KF):
                        e, fk = divmod(f, KF)
                        if q == 0:
                            act3.wait(pe, HID[f], at)
                        mm = pe.matmul(psY[q // 2][:, q % 2, :], hT[:, f, q * P:(q + 1) * P], w2_sb[:, e, fk, :],
                                       start=(f == 0), stop=(f == 2 * KF - 1))
                pe3.mark("out", mm)

            pe.wait_ge(s_setup, N_EXPERT)
            transpose_rows(At(0, 2, 0), 0)
            pe3.rest(pe, ["xT"])
            with pe.Fori(0, (GROUPS - 1) // 2) as k:
                for j in range(2):
                    group(At(k, 2, j))
            group(At(0, 2, GROUPS - 1))

        @block.scalar
        def _(act):
            p1_act.credit(act)
            act.wait_ge(s_const, 7)
            act.wait_ge(s_pool, 4)
            with act.Fori(0, BLOCKS // ROWS_RING) as k:
                for j in range(ROWS_RING):
                    at = At(k, ROWS_RING, j)
                    p1_dve.wait(act, "mv", at)
                    p1_mark = p1_act.mark
                    p1_mark("ln", act.activation(y1[:, j, 0:1], mv1[:, j, 1:2], ACT.Ln, bias=eps[:, 0:1]))
                    p1_act.wait(act, "ln", at)
                    p1_dve.wait(act, "logits", at, -4)
                    p1_mark("rstd", act.activation(y1[:, j, 1:2], y1[:, j, 0:1], ACT.Exp, scale=-0.5))
                    p1_act.wait(act, "rstd", at)
                    p1_pe.wait(act, "rows", at)
                    act.wait_ge(s_tab[j], at.k * 16 + 16)
                    p1_mark("rows", act.activation(head_cols(row_out[:, j, 0:HC1])[:, :, 0:C],
                                                   head_cols(psH[j % 2][:, 0:D]), ACT.Copy, scale=y1[:, j, 1:2]))
            act2.credit(act)
            total = steps_to_run(act)

            def step(at, follows):
                s, q = at.slot(), at.slot(-1)
                act.wait_ge(s_rows[s], at.landed(TILES))
                pe2.wait(act, "lT", at, -1)
                act2.mark("asrc", act.activation(asrc[:, :].rearrange("p (t r) -> p t r", r=R5),
                                                 rows[:, s, :, ONE:AD], ACT.Copy))
                if follows:
                    pe2.wait(act, "agg", at, -1)
                    dve2.wait(act, "num", at, -1)
                    pe2.wait(act, "carry", at, -1)
                    act2.mark("acc", act.activation(acc[:, 0:HC1], psA[q], ACT.Copy))
                else:
                    act2.skip(act, ["acc"], at)
                pe2.wait(act, "lastT", at)
                pe2.wait(act, "nodemax", at, -1)
                act2.mark("lastT", act.activation(lastmax_e[:, :], psR, ACT.Copy))
                if follows:
                    dve2.wait(act, "r_d", at)
                    act2.mark("rexp", act.activation(r_f[:, :], r_d[:, :], ACT.Exp))
                    dve2.wait(act, "self_d", at)
                    act2.mark("wself", act.activation(ws[:, :], zs[:, :], ACT.Exp))
                else:
                    act2.skip(act, ["rexp", "wself"], at)
                dve2.wait(act, "dmin", at)
                act2.mark("we", act.activation(we[:, s, :, :], le[:, :, :], ACT.Exp))
                if follows:
                    for n, src in (("1", "mv"), ("2", "mv_m")):
                        c = 2 * int(n) - 2
                        dve2.wait(act, src, at)
                        act2.mark("ln" + n, act.activation(ln2[:, c:c + 1], mv2[:, c + 1:c + 2], ACT.Ln,
                                                           bias=eps[:, 0:1]))
                        act2.wait(act, "ln" + n, at)
                        act2.mark("y" + n, act.activation(ln2[:, c + 1:c + 2], ln2[:, c:c + 1], ACT.Exp, scale=-0.5))
                else:
                    act2.skip(act, ["ln1", "y1", "ln2", "y2"], at)

            walk(act, total, step)

            for n in N_EXP:
                act.wait_ge(s_setup, n)
                act.activation(rt[:, 13, :], rt[:, 14, :], ACT.Exp).then_inc(s_exp, 1)

            act3.credit(act, ahead=["ln", "y"])

            def rstd(at, lead):
                dve3.wait(act, "mv", at, lead - 1)
                act3.mark("ln", act.activation(fln[:, :], fmv[:, :, 1], ACT.Ln, bias=eps[:, 0:1]))
                act3.wait(act, "ln", at, lead - 1)
                act3.mark("y", act.activation(fy[:, :], fln[:, :], ACT.Exp, scale=-0.5))

            def group(at):
                rstd(at, 1)
                for f in range(2 * KF):
                    e, fk = divmod(f, KF)
                    pe3.wait(act, HID[f], at)
                    if f == 0:
                        pe3.wait(act, "out", at, -1)
                    act3.mark(HID[f], act.activation(hT[:, f, :], psU[f % len(psU)], ACT.Gelu,
                                                     bias=b1_sb[:, e, fk:fk + 1]))
                dve3.wait(act, "mv2", at)
                act3.mark("ln2", act.activation(fln[:, :], fmv[:, :, 1], ACT.Ln, bias=eps[:, 0:1]))
                act3.wait(act, "ln2", at)
                act3.mark("y2", act.activation(fy[:, :], fln[:, :], ACT.Exp, scale=-0.5))

            rstd(At(0, 2, 0), 0)
            act3.rest(act, ["ln", "y"])
            act.wait_ge(s_fw, 128)
            with act.Fori(0, (GROUPS - 1) // 2) as k:
                for j in range(2):
                    group(At(k, 2, j))
            group(At(0, 2, GROUPS - 1))

        @block.vector
        def _(dve):
            done = [0]

            def link(ins):
                done[0] += 1
                ins.then_inc(s_setup, 1)
                dve.wait_ge(s_setup, done[0])

            link(dve.memset(first[:, :], N))
            dve.wait_ge(s_w, 96)
            dve.wait_ge(s_const, 7)
            for k in range(KD):
                for i in range(2):
                    link(dve.tensor_tensor(att_tmp[:, :], wx[:, k, 0:D], att[:, i, :], ALU.mult))
                    link(dve.tensor_reduce(wx[:, k, D + i * H:D + (i + 1) * H], head_cols(att_tmp[:, :]), X, ALU.add))
            assert done[0] == N_ATT
            dve.wait_ge(s_once, 1)
            for k in range(KD):
                link(dve.scalar_tensor_tensor(out=wx[:, k, :], in0=psW, scalar=-1.0 / D, in1=wx[:, k, :],
                                              op0=ALU.mult, op1=ALU.add))
            assert done[0] == N_WX
            p1_dve.credit(dve)
            with dve.Fori(0, BLOCKS // ROWS_RING) as k:
                for j in range(ROWS_RING):
                    at = At(k, ROWS_RING, j)
                    dve.wait_ge(s_x[j], at.landed(1))
                    p1_dve.mark("stats", dve.bn_stats(st1[:, j, :], x_in[:, j, :]))
                    p1_dve.wait(dve, "stats", at)
                    p1_act.wait(dve, "ln", at, -4)
                    hold(dve, s_dve_held)
                    p1_dve.mark("mv", dve.bn_aggr(mv1[:, j, :], st1[:, j, :]))
                    p1_pe.wait(dve, "xT", at, -1)
                    p1_pe.wait(dve, "rows", at, -2)
                    p1_dve.mark("xT", dve.tensor_copy(xT[:, j % 2, :, :], psX[j % 2]))
                    p1_pe.wait(dve, "rows", at)
                    p1_act.wait(dve, "rows", at)
                    dve.wait_ge(s_tab[j], at.k * 16 + 16)
                    p1_dve.mark("logits", dve.tensor_scalar(row_out[:, j, AS:TW], psH[j % 2][:, D:D + 2 * H],
                                                            y1[:, j, 1:2], None, ALU.mult))
            dve.wait_ge(s_sched, 16)
            link(dve.memset(first[:, 0:1], 0))
            link(dve.tensor_tensor(gap[:, :], first[:, 1:257], first[:, 0:256], ALU.subtract))
            link(dve.tensor_scalar(gap[:, :], gap[:, :], 7, None, ALU.arith_shift_right))
            link(dve.tensor_scalar(lows[:, 0, :], gap[:, :], 1.0, None, ALU.add))
            link(dve.memset(lows[:, 1, 0:1], 0.0))
            link(dve.tensor_tensor_scan(lows[:, 1, 1:256], lows[:, 0, 0:255], zeros[0:1, 0:255], 0.0, ALU.add, ALU.add))
            link(dve.scalar_tensor_tensor(out=lows[:, 2, :], in0=lows[:, 1, :], scalar=-float(P), in1=first[:, 0:256],
                                          op0=ALU.mult, op1=ALU.add))
            link(dve.tensor_scalar(tot_i[:, 0:1], lows[:, 1, chunks:chunks + 1], 1.0, None, ALU.add))
            assert done[0] == N_LOWS
            dve.wait_ge(s_once, 2)
            link(dve.tensor_copy(s_both[:, :, :], psS[:, :].rearrange("p (a s) -> p a s", a=2)))
            for half in range(2):
                col = s_col[:, half, :]
                link(dve.tensor_scalar(col[:, 0:1], iota_col[:, :], float(half * P), None, ALU.add))
                link(dve.tensor_scalar(s_cmp[:, half, 0:chunks], s_both[:, 0, 0:chunks], col[:, 0:1], None, ALU.is_le))
                link(dve.tensor_reduce(col[:, 1:2], s_cmp[:, half, 0:chunks], X, ALU.add))
                link(dve.tensor_scalar(s_out_i[:, 1, half:half + 1], col[:, 1:2], -1.0, None, ALU.add))
                link(dve.tensor_scalar(s_cmp[:, half, 0:chunks + 1], s_both[:, 0, 0:chunks + 1], col[:, 0:1], 1e9,
                                       ALU.is_gt, ALU.mult))
                link(dve.tensor_tensor(s_cmp[:, half, 0:chunks + 1], s_cmp[:, half, 0:chunks + 1],
                                       s_both[:, 1, 0:chunks + 1], ALU.add))
                link(dve.tensor_reduce(col[:, 2:3], s_cmp[:, half, 0:chunks + 1], X, ALU.min))
                link(dve.scalar_tensor_tensor(out=col[:, 3:4], in0=col[:, 0:1], scalar=float(P), in1=col[:, 2:3],
                                              op0=ALU.mult, op1=ALU.add))
                link(dve.tensor_scalar(s_out_i[:, 0, half:half + 1], col[:, 3:4], float(N + P), None, ALU.min))
            assert done[0] == N_SETUP
            total = steps_to_run(dve)
            link(dve.tensor_copy(w_tab[:, :], step_tab[:, 0, :]))
            dve2.credit(dve, ahead=DVE_A)

            def one_hots(at, lead):
                s, b = at.slot(lead), lead - 1
                dve2.mark("wcur", dve.tensor_copy(wcur[:, s, :], w_tab[:, bass.ds(at.number(lead), 2)]))
                dve2.wait(dve, "wcur", at, b)
                dve2.mark("node", dve.tensor_tensor(node[:, s:s + 1], iota_col[:, :], wcur[:, s, 0:1], ALU.add))
                dve.wait_ge(s_dst[s], at.landed(3, lead))
                dve2.mark("drel", dve.tensor_scalar(drel[:, s, :], dst_e[:, s, :], wcur[:, s, 0:1], None, ALU.subtract))
                dve2.mark("newseg", dve.tensor_tensor(newseg[:, s, 1:P], dst_s[:, s, 1:P], dst_s[:, s, 0:P - 1],
                                                      ALU.not_equal))
                dve2.wait(dve, "newseg", at, b)
                dve2.mark("pen", dve.tensor_scalar(pen[:, s, :], newseg[:, s, 0:P], -BIG, None, ALU.mult))
                pe2.wait(dve, "expand", at, b - 1)
                dve2.mark("ohT", dve.tensor_scalar(ohT[:, s, :, :].rearrange("p t n -> p (t n)"), dst_b[:, s, :],
                                                   node[:, s:s + 1], None, ALU.is_equal))
                pe2.wait(dve, "agg", at, b - 1)
                dve2.mark("oh", dve.tensor_tensor(oh[:, s, :, :], over(drel[:, s, :], P),
                                                  iota_row[:, :].unsqueeze(1).to_broadcast([P, TILES, P]), ALU.is_equal))

            def step(at, follows):
                s, q = at.slot(), at.slot(-1)
                mark = dve2.mark

                def own(name, lead=0):
                    dve2.wait(dve, name, at, lead)

                one_hots(at, 1)
                pe2.wait(dve, "lT", at)
                mark("runmax", dve.tensor_tensor_scan(runmax[:, :], pen[:, s, :], psT, -BIG, ALU.add, ALU.max))
                own("runmax")
                mark("lastmax", dve.tensor_tensor(lastmax[:, :], runmax[:, :], newseg[:, s, 1:P + 1], ALU.mult))
                mark("sel", dve.tensor_tensor(sel[:, s:s + 1], node[:, s:s + 1], wcur[:, s, 1:2], ALU.is_equal))
                mark("mask", dve.tensor_tensor(mask[:, s:s + 1], node[:, s:s + 1], wcur[:, s, 1:2], ALU.is_lt))
                if follows:
                    mark("r_t", dve.tensor_scalar(r_t[:, :], carry[:, HAS:HAS + 1], BIG, -BIG, ALU.mult, ALU.add))
                    own("r_t")
                    mark("r_sc", dve.tensor_scalar(r_sc[:, :], carry[:, SHIFT:HAS], r_t[:, 0:1], None, ALU.add))
                    own("r_sc")
                    mark("r_mn", dve.tensor_tensor(r_mn[:, :], r_sc[:, :], adsh[0:1, q, H:], ALU.max))
                    own("r_mn")
                    mark("r_d1", dve.tensor_tensor(r_d[:, 0:H], r_sc[:, :], r_mn[:, :], ALU.subtract))
                    mark("r_d", dve.tensor_tensor(r_d[:, H:], adsh[0:1, q, H:], r_mn[:, :], ALU.subtract))
                else:
                    dve2.skip(dve, DVE_F1, at)
                pe2.wait(dve, "nodemax", at)
                psm = psM.rearrange("p (t r) -> p t r", r=R5)
                mark("nohas", dve.tensor_scalar(nohas[:, :], psm[:, :, 0], BIG, -BIG, ALU.mult, ALU.add))
                own("nohas")
                mark("mtile", dve.tensor_tensor(mtile[:, :, :], psm[:, :, 1:R5], over(nohas[:, :], H), ALU.add))
                own("mtile")
                mark("mnode", dve.tensor_reduce(mnode[:, :], mtile[:, :, :].rearrange("p t h -> p h t"), X, ALU.max))
                dve.wait_ge(s_win[s], at.landed(2))
                own("mnode")
                mark("maxself", dve.tensor_tensor(mnode[:, :], mnode[:, :], tab_w[:, s, AS:AD], ALU.max))
                mark("ad", dve.tensor_copy(adsh[:, s, 0:H], tab_w[:, s, AD:TW]))
                own("maxself")
                mark("zn", dve.tensor_tensor(zn[:, :], mnode[:, :], tab_w[:, s, AD:TW], ALU.add))
                own("zn")
                mark("shift", dve.scalar_tensor_tensor(out=adsh[:, s, H:], in0=zn[:, :], scalar=NEG_SLOPE, in1=zn[:, :],
                                                       op0=ALU.mult, op1=ALU.max))
                if follows:
                    act2.wait(dve, "acc", at)
                    mark("accshift", dve.tensor_copy(acc[:, SHIFT:HAS], adsh[:, q, H:]))
                    act2.wait(dve, "rexp", at)
                    mark("mergescale", dve.tensor_tensor(head_cols(acc[0:1, 0:HC1]), head_cols(acc[0:1, 0:HC1]),
                                                         over(r_f[:, H:], C + 1), ALU.mult))
                    mark("carrypart", dve.tensor_tensor(head_cols(r_c[:, :]), head_cols(carry[:, 0:HC1]),
                                                        over(r_f[:, 0:H], C + 1), ALU.mult))
                    own("carrypart")
                    mark("merged", dve.tensor_tensor(acc[0:1, 0:HC1], acc[0:1, 0:HC1], r_c[:, :], ALU.add))
                    mark("mergedshift", dve.tensor_copy(acc[0:1, SHIFT:HAS], r_mn[:, :]))
                    mark("self_z", dve.tensor_tensor(zs[:, :], tab_w[:, q, AS:AD], tab_w[:, q, AD:TW], ALU.add))
                    own("self_z")
                    mark("self_l", dve.scalar_tensor_tensor(out=zs[:, :], in0=zs[:, :], scalar=NEG_SLOPE,
                                                            in1=zs[:, :], op0=ALU.mult, op1=ALU.max))
                    own("self_l")
                    mark("self_d", dve.tensor_tensor(zs[:, :], zs[:, :], acc[:, SHIFT:HAS], ALU.subtract))
                else:
                    dve2.skip(dve, DVE_F2, at)
                pe2.wait(dve, "expand", at)
                act2.wait(dve, "we", at, -1)
                pse = psE.rearrange("p (t r) -> p t r", r=2 * H)
                mark("ze", dve.tensor_tensor(ze[:, :, :], rows[:, s, :, AS:AD], pse[:, :, 0:H], ALU.add))
                own("ze")
                mark("le", dve.scalar_tensor_tensor(out=ze[:, :, :], in0=ze[:, :, :], scalar=NEG_SLOPE,
                                                    in1=ze[:, :, :], op0=ALU.mult, op1=ALU.max))
                own("le")
                mark("d", dve.tensor_tensor(le[:, :, :], ze[:, :, :], pse[:, :, H:], ALU.subtract))
                own("d")
                mark("dmin", dve.tensor_scalar(le[:, :, :], le[:, :, :], 0.0, None, ALU.min))
                if follows:
                    pe2.wait(dve, "carry", at)
                    mark("carry", dve.tensor_copy(carry[:, :], psC))
                    act2.wait(dve, "wself", at)
                    mark("selfmsg", dve.tensor_tensor(head_cols(num[:, :]), head_cols(tab_w[:, q, 0:HC1]),
                                                      over(ws[:, :], C + 1), ALU.mult))
                    own("selfmsg")
                    mark("num", dve.tensor_tensor(num[:, :], num[:, :], acc[:, 0:HC1], ALU.add))
                    own("num")
                    numh = head_cols(num[:, :])
                    mark("den", dve.tensor_scalar(rden[:, :], numh[:, :, C], DEN_EPS, None, ALU.add))
                    own("den")
                    mark("rden", dve.reciprocal(rden[:, :], rden[:, :]))
                    own("rden")
                    mark("attn", dve.tensor_tensor(head_cols(o[:, :]), numh[:, :, 0:C], over(rden[:, :], C), ALU.mult))
                    own("attn")
                    mark("biased", dve.tensor_tensor(o[:, :], o[:, :], g_aff[:, 0, :], ALU.add))
                    own("biased")
                    mark("st", dve.bn_stats(st2[:, :], o[:, :]))
                    own("st")
                    hold(dve, s_dve_held)
                    mark("mv", dve.bn_aggr(mv2[:, 0:2], st2[:, :]))
                    own("mv")
                    mark("v", dve.tensor_scalar(vv[:, 0:1], mv2[:, 1:2], LN_EPS, None, ALU.add))
                else:
                    dve2.skip(dve, DVE_F3, at)

                def messages(names):
                    for name in names:
                        t = 2 * MSGS.index(name)
                        w = we[:, s, t:t + 2, :]
                        mark(name, dve.tensor_tensor(
                            msg[:, s, t:t + 2, :].rearrange("p t (h c) -> p t h c", h=H),
                            rows[:, s, t:t + 2, 0:HC1].rearrange("p t (h c) -> p t h c", h=H),
                            over(w, C + 1), ALU.mult))

                act2.wait(dve, "we", at)
                messages(MSGS[:4])
                if follows:
                    def refine(y, v, names):
                        mark(names[0], dve.scalar_tensor_tensor(out=nt[:, 0:1], in0=y, scalar=v, in1=y,
                                                                op0=ALU.mult, op1=ALU.mult))
                        own(names[0])
                        mark(names[1], dve.tensor_scalar(nt[:, 1:2], nt[:, 0:1], -0.5, 1.5, ALU.mult, ALU.add))
                        own(names[1])
                        mark(names[2], dve.tensor_tensor(nt[:, 2:3], nt[:, 1:2], y, ALU.mult))
                        own(names[2])

                    act2.wait(dve, "y1", at)
                    own("v")
                    refine(ln2[:, 1:2], vv[:, 0:1], ("n1", "n2", "rstd"))
                    mark("normed", dve.tensor_scalar(o[:, :], o[:, :], mv2[:, 0:1], nt[:, 2:3], ALU.subtract, ALU.mult))
                    own("normed")
                    mark("gam", dve.tensor_tensor(o[:, :], o[:, :], g_aff[:, 1, :], ALU.mult))
                    own("gam")
                    mark("bet", dve.tensor_tensor(o[:, :], o[:, :], g_aff[:, 2, :], ALU.add))
                    own("bet")
                    sp2.wait(dve, "stored", at, -1)
                    pe2.wait(dve, "router", at, -2)
                    mark("xmid", dve.scalar_tensor_tensor(out=x_o[:, q, 0:D], in0=o[:, :], scalar=0.0,
                                                          in1=x_w[:, q, :], op0=ALU.max, op1=ALU.add))
                    own("xmid")
                    mark("st_m", dve.bn_stats(st2[:, :], x_o[:, q, 0:D]))
                    own("st_m")
                    hold(dve, s_dve_held)
                    mark("mv_m", dve.bn_aggr(mv2[:, 2:4], st2[:, :]))
                    own("mv_m")
                    mark("v_m", dve.tensor_scalar(vv[:, 1:2], mv2[:, 3:4], LN_EPS, None, ALU.add))
                else:
                    dve2.skip(dve, DVE_F4, at)
                messages(MSGS[4:])
                if follows:
                    act2.wait(dve, "y2", at)
                    own("v_m")
                    refine(ln2[:, 3:4], vv[:, 1:2], ("m1", "m2", "m_rstd"))
                    mark("lhs", dve.tensor_tensor(m_lhs[:, q:q + 1], nt[:, 2:3], mask[:, q:q + 1], ALU.mult))
                    mark("mu", dve.tensor_copy(x_o[:, q, D:D + 1], mv2[:, 2:3]))
                else:
                    dve2.skip(dve, DVE_F5, at)

            one_hots(At(0, 2, 0), 0)
            dve2.rest(dve, DVE_A)
            walk(dve, total, step)

            dve.wait_ge(s_once, 3)
            link(dve.tensor_copy(zrow[:, :], psZ))
            link(dve.tensor_scalar(zrow[:, 0:D], zrow[:, 0:D], zrow[:, D:D + 1], 1.0 / N, ALU.subtract, ALU.mult))
            assert done[0] == N_MEAN
            dve.wait_ge(s_once, 4)
            link(dve.tensor_copy(zcol[:, :], bank[0][:, 0:KD]))
            dve.wait_ge(s_once, 5)
            link(dve.tensor_tensor(rt[:, 1, :], bank[1][0:1, 0:NE], rt[:, 0, :], ALU.add))

            exps = [0]

            def softmax(src, to):
                link(dve.tensor_reduce(rt[:, 15, 0:1], rt[:, src, :], X, ALU.max))
                link(dve.tensor_scalar(rt[:, 14, :], rt[:, src, :], rt[:, 15, 0:1], None, ALU.subtract))
                assert done[0] == N_EXP[exps[0]]
                exps[0] += 1
                dve.wait_ge(s_exp, exps[0])
                link(dve.tensor_reduce(rt[:, 15, 1:2], rt[:, 13, :], X, ALU.add))
                link(dve.reciprocal(rt[:, 15, 2:3], rt[:, 15, 1:2]))
                link(dve.tensor_scalar(rt[:, to, :], rt[:, 13, :], rt[:, 15, 2:3], None, ALU.mult))

            softmax(1, 2)
            capacity = float(math.ceil(N * CAPACITY_FACTOR / NE))
            link(dve.tensor_scalar(rt[:, 3, :], rt[:, 2, :], float(N), 1e-30, ALU.mult, ALU.max))
            link(dve.reciprocal(rt[:, 4, :], rt[:, 3, :]))
            link(dve.tensor_scalar(rt[:, 5, :], rt[:, 4, :], capacity, 1.0, ALU.mult, ALU.min))
            link(dve.tensor_tensor(rt[:, 6, :], rt[:, 5, :], rt[:, 2, :], ALU.mult))
            softmax(6, 7)
            link(dve.max(rt[:, 8, :], rt[:, 7, :]))
            link(dve.max_index(top_i[:, :], rt[:, 8, :], rt[:, 7, :]))
            link(dve.tensor_copy(top_ii[:, :], top_i[:, :]))
            link(dve.tensor_scalar(rt[:, 14, :], rt[:, 8, :], rt[:, 8, 0:1], None, ALU.subtract))
            assert done[0] == N_EXP[exps[0]]
            dve.wait_ge(s_exp, exps[0] + 1)
            link(dve.tensor_reduce(rt[:, 15, 1:2], rt[:, 13, 0:2], X, ALU.add))
            link(dve.reciprocal(rt[:, 15, 2:3], rt[:, 15, 1:2]))
            link(dve.tensor_scalar(rt[:, WTOP, 0:2], rt[:, 13, 0:2], rt[:, 15, 2:3], None, ALU.mult))
            assert done[0] == N_TOP
            dve.wait_ge(s_once, 6)
            link(dve.tensor_copy(wtop[:, :], bank[2][:, 0:2]))
            dve.wait_ge(s_fw, 128)
            for i in range(2):
                flat = w2_sb[:, i, :, :].rearrange("p k d -> p (k d)")
                link(dve.tensor_scalar(flat, flat, wtop[:, i:i + 1], None, ALU.mult))
            link(dve.tensor_scalar(b2_w[:, :], b2_sb[:, 0, :], wtop[:, 0:1], None, ALU.mult))
            link(dve.scalar_tensor_tensor(out=b2_w[:, :], in0=b2_sb[:, 1, :], scalar=wtop[:, 1:2], in1=b2_w[:, :],
                                          op0=ALU.mult, op1=ALU.add))
            assert done[0] == N_EXPERT
            dve3.credit(dve, ahead=DVE3_A)

            def normalise(at, at3, lead):
                s = at.slot(lead)
                dve.wait_ge(s_fx[at3.slot(lead)], at3.landed(1, lead))
                rstd_of(at, lead - 1, "st mv v n1 n2 rstd".split(), lambda q: fx[:, at3.slot(lead), q, :],
                        lambda: act3.wait(dve, "y", at, lead - 1))
                for q in range(QB):
                    ins = dve.tensor_scalar(fxn[:, s, q, :], fx[:, at3.slot(lead), q, :], fmv[:, q, 0:1],
                                            ft[:, q:q + 1], ALU.subtract, ALU.mult)
                dve3.mark("xn", ins)
                pe3.wait(dve, "xT", at, lead - 1)
                for k in range(KD):
                    ins = dve.tensor_copy(fxT[:, s, k, :], psF[k])
                dve3.mark("xT", ins)

            def rstd_of(at, lead, names, rows_of, wait_y):
                def own(name):
                    dve3.wait(dve, name, at, lead)

                for q in range(QB):
                    ins = dve.bn_stats(fst[:, q, :], rows_of(q))
                dve3.mark(names[0], ins)
                own(names[0])
                hold(dve, s_dve_held)
                for q in range(QB):
                    ins = dve.bn_aggr(fmv[:, q, :], fst[:, q, :])
                dve3.mark(names[1], ins)
                own(names[1])
                dve3.mark(names[2], dve.tensor_scalar(fv[:, :], fmv[:, :, 1], LN_EPS, -0.5, ALU.add, ALU.mult))
                own(names[2])
                wait_y()
                for q in range(QB):
                    ins = dve.scalar_tensor_tensor(out=ft[:, q:q + 1], in0=fy[:, q:q + 1], scalar=fv[:, q:q + 1],
                                                   in1=fy[:, q:q + 1], op0=ALU.mult, op1=ALU.mult)
                dve3.mark(names[3], ins)
                own(names[3])
                dve3.mark(names[4], dve.tensor_scalar(ft[:, :], ft[:, :], 1.5, None, ALU.add))
                own(names[4])
                dve3.mark(names[5], dve.tensor_tensor(ft[:, :], ft[:, :], fy[:, :], ALU.mult))
                own(names[5])

            def group(at, at3):
                s = at.slot()
                y = fo[:, s, :, :]

                def own(name):
                    dve3.wait(dve, name, at)

                normalise(at, at3, 1)
                pe3.wait(dve, "out", at)
                sp3.wait(dve, "stored", at, -2)
                for i in range(2):
                    ins = dve.tensor_tensor(y[:, 2 * i:2 * i + 2, :], psY[i], fxn[:, s, 2 * i:2 * i + 2, :], ALU.add)
                dve3.mark("res", ins)
                own("res")
                dve3.mark("b2", dve.tensor_tensor(y, y, b2_w[:, :].unsqueeze(1).to_broadcast([P, QB, D]), ALU.add))
                own("b2")
                rstd_of(at, 0, "st2 mv2 v2 m1 m2 rstd2".split(), lambda q: y[:, q, :],
                        lambda: act3.wait(dve, "y2", at))
                for q in range(QB):
                    ins = dve.tensor_scalar(y[:, q, :], y[:, q, :], fmv[:, q, 0:1], ft[:, q:q + 1],
                                            ALU.subtract, ALU.mult)
                dve3.mark("yn", ins)
                own("yn")
                dve3.mark("gam", dve.tensor_tensor(y, y, f_aff[:, 0, :].unsqueeze(1).to_broadcast([P, QB, D]), ALU.mult))
                own("gam")
                dve3.mark("bet", dve.tensor_tensor(y, y, f_aff[:, 1, :].unsqueeze(1).to_broadcast([P, QB, D]), ALU.add))
                own("bet")
                dve3.mark("out", dve.tensor_tensor(y, y, fx[:, at3.slot(), :, :], ALU.add))

            normalise(At(0, 2, 0), At(0, 3, 0), 0)
            dve3.rest(dve, DVE3_A)
            with dve.Fori(0, (GROUPS - 1) // 6) as k:
                for j in range(6):
                    group(At(k * 3, 2, j), At(k * 2, 3, j))
            group(At(0, 2, GROUPS - 1), At(0, 3, GROUPS - 1))


def kernel(**inputs):
    import numpy as _np
    import concourse.bacc as _bacc
    from concourse.bass_utils import run_bass_kernel_spmd as _run

    N, E = inputs["x"].shape[0], inputs["src"].shape[0]
    chunks, _, blocks, _ = sizes(N, E)
    padded = chunks * CHUNK
    host = {k: _np.ascontiguousarray(v) for k, v in inputs.items()}
    rows = _np.zeros(((blocks + ROWS_RING - 1) * P, host["x"].shape[1]), host["x"].dtype)
    rows[:N] = host["x"]
    src = _np.zeros(padded, host["src"].dtype)
    src[:E] = host["src"]
    dst = _np.full(padded, PAD_NODE, host["dst"].dtype)
    dst[:E] = host["dst"]

    def tiles(a):
        return _np.ascontiguousarray(a.reshape(chunks, TILES, P).transpose(0, 2, 1)).reshape(chunks * P, TILES)

    arrays = {"x_rows": rows, "src_tiles": tiles(src), "dst": dst, "dst_tiles": tiles(dst)}
    arrays.update((k, host[k]) for k in _WEIGHTS)
    nc = _bacc.Bacc("TRN2", target_bir_lowering=False, num_devices=1)
    args = [nc.dram_tensor(f"in_{k}", a.shape, mybir.dt.from_np(a.dtype), kind="ExternalInput").ap()
            for k, a in arrays.items()]
    args.append(nc.dram_tensor("out_0", (N, rows.shape[1]), F32, kind="ExternalOutput").ap())
    build(nc, *args, N, E)
    r = _run(nc, [{f"in_{k}": a for k, a in arrays.items()}], core_ids=[0])
    return r.results[0]["out_0"]


PAD_NODE = 1 << 20
_WEIGHTS = ["L0_gnn_W", "L0_gnn_att_src", "L0_gnn_att_dst", "L0_gnn_bias", "L0_gnn_ln_gamma", "L0_gnn_ln_beta",
            "L0_ffn_Wr", "L0_ffn_br", "L0_ffn_W1", "L0_ffn_b1", "L0_ffn_W2", "L0_ffn_b2", "L0_ffn_gamma",
            "L0_ffn_beta"]
```

```python
from contextlib import ExitStack
import math

import concourse.bass as bass
from concourse import mybir

F32 = mybir.dt.float32
BF16 = mybir.dt.bfloat16
I32 = mybir.dt.int32
U32 = mybir.dt.uint32
ALU = mybir.AluOpType
ACT = mybir.ActivationFunctionType
X = mybir.AxisListType.X

P = 128
TILES = 14
CHUNK = TILES * P
ROWS_RING = 4
NEG_SLOPE, LN_EPS, DEN_EPS = 0.2, 1e-5, 1e-16
ROOT_SEED = 1597463007.0
BIG = 1e30
CAPACITY_FACTOR = 1.25
GROUP = 512


def sizes(N, E):
    chunks = -(-E // CHUNK)
    steps = chunks + N // P + 1 + 1
    steps += 1 - steps % 2
    blocks = -(-(N + 3 * P) // P)
    blocks = -(-blocks // ROWS_RING) * ROWS_RING
    groups = -(-N // GROUP)
    return chunks, steps, blocks, groups


class At:

    def __init__(self, k, mul, off):
        self.k, self.mul, self.off = k, mul, off

    def number(self, lead=0):
        return self.k * self.mul + (self.off + lead)

    def slot(self, lead=0):
        return (self.off + lead) % self.mul

    def landed(self, dmas, lead=0):
        return self.k * (16 * dmas) + 16 * dmas * ((self.off + lead) // self.mul + 1)


class Ticks:

    def __init__(self, sem, names, back):
        self.sem, self.names, self.back, self.at = sem, names.split(), back, 0
        assert len(set(self.names)) == len(self.names)

    def mark(self, name, ins):
        assert self.names[self.at % len(self.names)] == name, (name, self.names[self.at % len(self.names)])
        self.at += 1
        ins.then_inc(self.sem, 1)

    def value(self, name, at, lead=0):
        n = len(self.names)
        return at.k * (n * at.mul) + ((at.off + lead + self.back) * n + self.names.index(name) + 1)

    def wait(self, eng, name, at, lead=0):
        eng.wait_ge(self.sem, self.value(name, at, lead))

    def skip(self, eng, names, at):
        i = self.names.index(names[0])
        assert self.names[i:i + len(names)] == list(names) and self.at % len(self.names) == i
        eng.wait_ge(self.sem, self.value(names[0], at) - 1)
        eng.sem_inc(self.sem, len(names))
        self.at += len(names)

    def credit(self, eng, ahead=()):
        full = self.back - bool(ahead)
        self.at = self.names.index(ahead[0]) if ahead else 0
        eng.sem_inc(self.sem, len(self.names) * full + self.at)

    def rest(self, eng, ahead, then=None):
        n, a = self.names.index(then[0]) if then else len(self.names), self.at
        assert self.names[a - len(ahead):a] == list(ahead)
        if a < n:
            eng.wait_ge(self.sem, len(self.names) * (self.back - 1) + a)
            eng.sem_inc(self.sem, n - a)
        self.at = n if then else 0


def build(nc, x, src_t, dst, dst_t, W, att_src, att_dst, g_bias, g_gamma, g_beta, Wr, br, W1, b1, W2, b2,
          f_gamma, f_beta, out, N, E):
    D = x.shape[1]
    H, C = att_src.shape
    NE, _, F = W1.shape
    KD, KF = D // P, F // P
    chunks, STEPS, BLOCKS, GROUPS = sizes(N, E)
    HC1 = H * (C + 1)
    ONE, AS, AD = HC1, HC1 + 1, HC1 + 1 + H
    TW = AD + H
    R5 = 1 + H
    SR = R5 * TILES
    SHIFT, HAS = HC1, HC1 + H
    AW = HAS + 1
    SCHED = 256
    assert STEPS + 3 <= SCHED and SR <= P and D == H * C
    QB = GROUP // P
    XO_ROWS = (GROUPS + 1) * GROUP

    with ExitStack() as ctx:
        def sb(name, shape, dt=F32):
            return ctx.enter_context(nc.sbuf_tensor(name, shape, dt))

        def sem(name):
            return ctx.enter_context(nc.semaphore(name))

        bank = [ctx.enter_context(nc.psum_tensor(f"bank{i}", [P, 512], F32)) for i in range(8)]
        table = nc.dram_tensor("table", [BLOCKS * P, TW], F32, kind="Internal").ap()
        x_mid = nc.dram_tensor("x_mid", [XO_ROWS, D], F32, kind="Internal").ap()
        sched = nc.dram_tensor("sched", [2, SCHED], I32, kind="Internal").ap()

        ident = sb("ident", [P, P])
        iota_row = sb("iota_row", [P, P])
        iota_b = sb("iota_b", [P, P], BF16)
        iota_col = sb("iota_col", [P, 1])
        ones = sb("ones", [P, P])
        eps = sb("eps", [P, 1])
        zeros = sb("zeros", [P, D])
        g_aff = sb("g_aff", [P, 3, D])
        f_aff = sb("f_aff", [P, 2, D])

        wx = sb("wx", [P, KD, D + 2 * H])
        att = sb("att", [P, 2, D])
        att_tmp = sb("att_tmp", [P, D])
        x_in = sb("x_in", [P, ROWS_RING, D])
        xT = sb("xT", [P, 2, KD, P])
        st1 = sb("st1", [P, ROWS_RING, 6])
        mv1 = sb("mv1", [P, ROWS_RING, 2])
        y1 = sb("y1", [P, ROWS_RING, 2])
        row_out = sb("row_out", [P, ROWS_RING, TW])

        first = sb("first", [1, 257], I32)
        gap = sb("gap", [1, 256], I32)
        lows = sb("lows", [1, 3, 256])
        s_both = sb("s_both", [P, 2, 256])
        s_cmp = sb("s_cmp", [P, 2, 256])
        s_col = sb("s_col", [P, 2, 4])
        s_out_i = sb("s_out_i", [P, 2, 2], I32)
        step_tab = sb("step_tab", [P, 2, SCHED], I32)
        w_tab = sb("w_tab", [P, SCHED])
        tot_i = sb("tot_i", [1, 2], I32)

        idx = [sb(f"idx{i}", [P, TILES], I32) for i in range(2)]
        dst_e = sb("dst_e", [P, 2, TILES], I32)
        dst_s = sb("dst_s", [SR, 2, P], I32)
        dst_b = sb("dst_b", [P, 2, CHUNK], I32)
        tab_w = sb("tab_w", [P, 2, TW])
        x_w = sb("x_w", [P, 2, D])
        rows = sb("rows", [P, 2, TILES, TW])
        msg = sb("msg", [P, 2, TILES, HC1])
        oh = sb("oh", [P, 2, TILES, P])
        oh_b = sb("oh_b", [P, 2, TILES, P], BF16)
        ohT = sb("ohT", [P, 2, TILES, P], BF16)
        wcur = sb("wcur", [P, 2, 2])
        node = sb("node", [P, 2])
        drel = sb("drel", [P, 2, TILES], BF16)
        sel = sb("sel", [P, 2])
        mask = sb("mask", [P, 2])
        newseg = sb("newseg", [SR, 2, P + 1])
        pen = sb("pen", [SR, 2, P])
        asrc = sb("asrc", [P, SR])
        runmax = sb("runmax", [SR, P])
        lastmax = sb("lastmax", [SR, P])
        last_p = sb("last_p", [P, TILES, 3, R5], BF16)
        last_r = sb("last_r", [P, TILES, R5])
        node_v = sb("node_v", [P, TILES, R5])
        nohas = sb("nohas", [P, TILES])
        mtile = sb("mtile", [P, TILES, H])
        mnode = sb("mnode", [P, H])
        zn = sb("zn", [P, H])
        adsh = sb("adsh", [P, 2, 2 * H])
        adsh_p = sb("adsh_p", [P, 3, 2 * H], BF16)
        adsh_r = sb("adsh_r", [P, 2 * H])
        edge_v = sb("edge_v", [P, TILES, 2 * H])
        ze = sb("ze", [P, TILES, H])
        le = sb("le", [P, TILES, H])
        we = sb("we", [P, 2, TILES, H])
        acc = sb("acc", [P, AW])
        carry = sb("carry", [1, AW])
        r_t = sb("r_t", [1, 1])
        r_sc = sb("r_sc", [1, H])
        r_mn = sb("r_mn", [1, H])
        r_d = sb("r_d", [1, 2 * H])
        r_f = sb("r_f", [1, 2 * H])
        r_c = sb("r_c", [1, HC1])
        zs = sb("zs", [P, H])
        ws = sb("ws", [P, H])
        num = sb("num", [P, HC1])
        rden = sb("rden", [P, H])
        o = sb("o", [P, D])
        st2 = sb("st2", [P, 6])
        mv2 = sb("mv2", [P, 4])
        ln2 = sb("ln2", [P, 4])
        vv = sb("vv", [P, 2])
        nt = sb("nt", [P, 3])
        m_lhs = sb("m_lhs", [P, 2])
        x_o = sb("x_o", [P, 2, D + 1])

        zrow = sb("zrow", [1, D + 1])
        zcol = sb("zcol", [P, KD])
        wr_sb = sb("wr_sb", [P, KD, NE])
        rt = sb("rt", [1, 16, NE])
        top_i = sb("top_i", [1, NE], U32)
        top_ii = sb("top_ii", [1, NE], I32)
        wtop = sb("wtop", [P, 2])
        w1_sb = sb("w1_sb", [P, 2, KD, F])
        w2_sb = sb("w2_sb", [P, 2, KF, D])
        b1_sb = sb("b1_sb", [P, 2, KF])
        b2_sb = sb("b2_sb", [P, 2, D])
        b2_w = sb("b2_w", [P, D])
        fx = sb("fx", [P, 3, QB, D])
        fst = sb("fst", [P, QB, 6])
        fmv = sb("fmv", [P, QB, 2])
        ft = sb("ft", [P, QB])
        fv = sb("fv", [P, QB])
        fh = sb("fh", [P, QB])
        fq = sb("fq", [P, QB])
        fxn = msg[:, :, :, :].rearrange("p a t c -> p (a t c)")[:, 0:2 * QB * D]\
            .rearrange("p (a q d) -> p a q d", a=2, q=QB)
        fxT = oh[:, :, :, :].rearrange("p a t c -> p (a t c)")[:, 0:2 * KD * GROUP]\
            .rearrange("p (a k n) -> p a k n", a=2, k=KD)
        hT = rows[:, :, :, :].rearrange("p a t c -> p (a t c)")[:, 0:2 * KF * GROUP]\
            .rearrange("p (f n) -> p f n", f=2 * KF)
        fo = sb("fo", [P, 2, QB, D])

        s_w = sem("s_w")
        s_x = [sem(f"s_x{i}") for i in range(ROWS_RING)]
        s_tab = [sem(f"s_tab{i}") for i in range(ROWS_RING)]
        s_pad = sem("s_pad")
        s_sched = sem("s_sched")
        s_idx = [sem(f"s_idx{i}") for i in range(2)]
        s_dst = [sem(f"s_dst{i}") for i in range(2)]
        s_rows = [sem(f"s_rows{i}") for i in range(2)]
        s_win = [sem(f"s_win{i}") for i in range(2)]
        s_mid = sem("s_mid")
        s_fwr = sem("s_fwr")
        s_fw = sem("s_fw")
        s_fx = [sem(f"s_fx{i}") for i in range(3)]
        s_out = sem("s_out")
        s_const = sem("s_const")
        s_pool = sem("s_pool")
        s_setup = sem("s_setup")
        s_once = sem("s_once")
        s_exp = sem("s_exp")
        s_granted = sem("s_granted")
        s_dve_held = sem("s_dve_held")
        s_sp_held = sem("s_sp_held")

        p1_pe = Ticks(sem("p1_pe"), "xT rows", 4)
        p1_dve = Ticks(sem("p1_dve"), "stats mv xT", 4)
        p1_act = Ticks(sem("p1_act"), "ln rstd rows logits", 4)
        DVE_A = "wcur node drel newseg pen".split()
        DVE_B = "ohT oh".split()
        DVE_F1 = "r_t r_sc r_mn r_d1 r_d".split()
        DVE_F2 = "accshift merged mergedshift self_z self_l self_d".split()
        DVE_F3 = "num den rden biased st mv v".split()
        DVE_F4 = "gam n1 n2 rstd normed xmid st_m mv_m v_m".split()
        DVE_F5 = "m1 m2 m_rstd lhs mu".split()
        MSGS = [f"msg{i}" for i in range(TILES // 2)]
        dve2 = Ticks(sem("dve2"), " ".join(
            DVE_A + ["runmax", "lastmax", "sel", "mask"] + DVE_F1 + "last_hi last_r last_mid last_lo".split() + DVE_B
            + "node_v nohas mtile mnode maxself ad zn shift adsh_hi adsh_r adsh_mid adsh_lo".split() + DVE_F2
            + "edge_v ze le d dmin".split() + DVE_F3
            + MSGS[:4] + DVE_F4 + MSGS[4:] + DVE_F5), 3)
        act2 = Ticks(sem("act2"), "asrc acc rexp carried oh wself carry we ln1 y1 ln2 y2", 3)
        pe2 = Ticks(sem("pe2"), "lT lastT nodemax expand carry agg router", 3)
        sp2 = Ticks(sem("sp2"), "stored", 3)
        ROOT = "v vh seed sq0 t0 r0 sq1 t1 r1 sq2 t2 rstd".split()
        DVE3_A = ["st", "mv"] + ROOT + ["xn", "xT"]
        ROOT2 = [n + "'" for n in ROOT]
        HID = [f"h{i}" for i in range(2 * KF)]
        dve3 = Ticks(sem("dve3"), " ".join(DVE3_A) + " res b2 st2 mv2 " + " ".join(ROOT2) + " gam normed out", 2)
        act3 = Ticks(sem("act3"), " ".join(HID), 2)
        pe3 = Ticks(sem("pe3"), " ".join(HID) + " half xT out", 2)
        sp3 = Ticks(sem("sp3"), "stored", 3)

        psX = [bank[i][:, 0:KD * P].rearrange("p (k n) -> p k n", k=KD) for i in (0, 1)]
        psH = [bank[i][:, 0:D + 2 * H] for i in (2, 3)]
        psW = bank[4][:, 0:D + 2 * H]
        psS = bank[5]
        psT, psR, psM = bank[0][0:SR, 0:P], bank[1][:, 0:SR], bank[2][:, 0:3 * SR]
        psE = bank[3][:, 0:3 * 2 * H * TILES]
        psA = [bank[i][:, 0:HC1] for i in (4, 5)]
        psC, psZ = bank[6][0:1, 0:AW], bank[7][0:1, 0:D + 1]
        psF = [bank[i][:, :] for i in (0, 1)]
        psU = [bank[i][:, :] for i in (2, 3, 4, 5)]
        psY = [bank[i][:, :].rearrange("p (q d) -> p q d", d=D) for i in (6, 7)]

        N_ATT = 1 + 4 * KD
        N_WX = N_ATT + KD
        N_LOWS = N_WX + 8
        N_SETUP = N_LOWS + 1 + 2 * 9
        N_MEAN = N_SETUP + 2 + 2
        N_EXP = [N_MEAN + 4, N_MEAN + 13, N_MEAN + 20]
        N_TOP = N_EXP[2] + 3
        N_EXPERT = N_TOP + 5
        WTOP = 9

        block = ctx.enter_context(nc.Block())

        def row(v):
            return v.rearrange("(a d) -> a d", a=1)

        def head_cols(ap):
            return ap.rearrange("p (h c) -> p h c", h=H)

        def over(ap, n):
            return ap.unsqueeze(len(ap.shape)).to_broadcast([*ap.shape, n])

        def hold(eng, counted):
            eng.sem_inc(counted, 1)

        def walk(eng, total, step):
            step(At(0, 2, 0), False)
            with eng.Fori(0, (STEPS - 1) // 2) as k:
                for j in (1, 2):
                    at = At(k, 2, j)
                    with eng.If(at.number() < total):
                        step(at, True)

        def steps_to_run(eng):
            eng.wait_ge(s_sched, 64)
            return eng.value_load(tot_i[0:1, 0:1], min_val=2, max_val=STEPS)

        @block.sync
        def _(sp):
            sp.dma_start(wx[:, :, 0:D], W.rearrange("(k p) n -> p k n", p=P)).then_inc(s_w, 16)
            for i, v in enumerate((att_src, att_dst)):
                sp.dma_start(att[:, i, :], v.rearrange("(a h) c -> a (h c)", a=1).to_broadcast([P, D])).then_inc(s_w, 16)
            for b in range(3):
                sp.dma_start(x_in[:, b, :], x[b * P:(b + 1) * P, :]).then_inc(s_x[b], 16)
            for i, v in enumerate((g_bias, g_gamma, g_beta)):
                sp.dma_start(g_aff[:, i, :], row(v).to_broadcast([P, D])).then_inc(s_w, 16)
            sp.wait_ge(s_setup, 1)
            sp.dma_start(first[:, 0:chunks],
                         dst[0:chunks * CHUNK].rearrange("(a c e) -> a c e", a=1, e=CHUNK)[:, :, 0],
                         allow_slow_non_contiguous=True).then_inc(s_sched, 16)
            sp.wait_ge(s_const, 7)
            pads = [(r, min(P, XO_ROWS - r)) for r in range(N, XO_ROWS, P)]
            for i, (r, n) in enumerate(pads):
                sp.dma_start(x_mid[r:r + n, :], zeros[0:n, :]).then_inc(s_tab[i] if i < ROWS_RING else s_pad, 16)
            with sp.Fori(0, BLOCKS // ROWS_RING) as k:
                for j in range(ROWS_RING):
                    at = At(k, ROWS_RING, j)
                    p1_dve.wait(sp, "stats", at, -1)
                    hold(sp, s_sp_held)
                    p1_pe.wait(sp, "xT", at, -2)
                    hold(sp, s_sp_held)
                    sp.dma_start(x_in[:, at.slot(3), :], x[bass.ds(at.number(3) * P, P), :])\
                      .then_inc(s_x[at.slot(3)], 16)
                    p1_act.wait(sp, "logits", at)
                    hold(sp, s_sp_held)
                    sp.dma_start(table[bass.ds(at.number() * P, P), :], row_out[:, j, :]).then_inc(s_tab[j], 16)
            for j in range(ROWS_RING):
                sp.wait_ge(s_tab[j], 16 * (BLOCKS // ROWS_RING + 1))
                sp.wait_ge(s_x[j], 16 * (BLOCKS // ROWS_RING + (j < 3)))
            sp.wait_ge(s_pad, 16 * (len(pads) - ROWS_RING))
            sp.wait_ge(s_setup, N_SETUP)
            for i in range(2):
                sp.dma_start(sched[i, :].rearrange("(b p) -> p b", p=P), s_out_i[:, i, :],
                             allow_slow_non_contiguous=True).then_inc(s_sched, 16)
            sp.wait_ge(s_sched, 48)
            sp.dma_start(step_tab[:, :, :].rearrange("p a s -> p (a s)"),
                         sched.rearrange("(o a) s -> o (a s)", o=1).to_broadcast([P, 2 * SCHED])).then_inc(s_sched, 16)
            total = steps_to_run(sp)

            def load_edges(at, lead):
                slot = at.slot(lead)
                c = sp.value_load(step_tab[0:1, 1, bass.ds(at.number(lead), 1)], min_val=0, max_val=chunks - 1)
                sp.dma_start(idx[slot][:, :], src_t[bass.ds(c * P, P), :]).then_inc(s_idx[slot], 16)
                sp.dma_start(dst_e[:, slot, :], dst_t[bass.ds(c * P, P), :]).then_inc(s_dst[slot], 16)
                sp.dma_start(dst_s[:, slot, :], dst.rearrange("(t o e) -> t o e", o=1, e=P)
                             [bass.ds(c * TILES, TILES), :, :].to_broadcast([TILES, R5, P])).then_inc(s_dst[slot], 16)
                sp.dma_start(dst_b[:, slot, :], dst.rearrange("(a e) -> a e", e=CHUNK)
                             [bass.ds(c, 1), :].to_broadcast([P, CHUNK])).then_inc(s_dst[slot], 16)

            def load_window(at, lead):
                slot = at.slot(lead)
                w = sp.value_load(step_tab[0:1, 0, bass.ds(at.number(lead), 1)], min_val=0, max_val=N + P)
                sp.dma_start(tab_w[:, slot, :], table[bass.ds(w, P), :]).then_inc(s_win[slot], 16)
                sp.dma_start(x_w[:, slot, :], x[bass.ds(w, P), :]).then_inc(s_win[slot], 16)

            def step(at, follows):
                sp.wait_ge(s_rows[at.slot()], at.landed(TILES))
                hold(sp, s_sp_held)
                dve2.wait(sp, "oh", at, -1)
                hold(sp, s_sp_held)
                load_edges(at, 2)
                if not follows:
                    load_window(at, 1)
                    sp2.skip(sp, ["stored"], at)
                    return
                dve2.wait(sp, "xmid", at)
                hold(sp, s_sp_held)
                w = sp.value_load(step_tab[0:1, 0, bass.ds(at.number(-1), 1)], min_val=0, max_val=N)
                sp.dma_start(x_mid[bass.ds(w, P), :], x_o[:, at.slot(-1), 0:D]).then_inc(s_mid, 16)
                load_window(at, 1)
                sp.wait_ge(s_mid, at.k * (16 * at.mul) + 16 * at.off)
                hold(sp, s_sp_held)
                sp2.skip(sp, ["stored"], at)

            sp2.credit(sp)
            load_edges(At(0, 2, 0), 0)
            load_edges(At(0, 2, 0), 1)
            load_window(At(0, 2, 0), 0)
            walk(sp, total, step)
            for slot in range(2):
                edges, windows = (total + (3 - slot)) // 2, (total + (2 - slot)) // 2
                for s, n in ((s_idx, edges * 16), (s_dst, edges * 48), (s_win, windows * 32)):
                    sp.wait_ge(s[slot], n)
                    hold(sp, s_sp_held)

            sp.dma_start(wr_sb[:, :, :], Wr.rearrange("(k p) e -> p k e", p=P)).then_inc(s_fwr, 16)
            sp.dma_start(rt[:, 0, :], row(br)).then_inc(s_fwr, 16)
            for i, v in enumerate((f_gamma, f_beta)):
                sp.dma_start(f_aff[:, i, :], row(v).to_broadcast([P, D])).then_inc(s_fwr, 16)

            def load_group(at, lead):
                sp.dma_start(fx[:, at.slot(lead), :, :],
                             x_mid[bass.ds(at.number(lead) * GROUP, GROUP), :].rearrange("(q p) d -> p q d", p=P))\
                  .then_inc(s_fx[at.slot(lead)], 16)

            load_group(At(0, 3, 0), 0)
            load_group(At(0, 3, 0), 1)
            sp.wait_ge(s_setup, N_TOP)
            for i in range(2):
                e = sp.value_load(top_ii[0:1, i:i + 1], min_val=0, max_val=NE - 1)
                sp.dma_start(w1_sb[:, i, :, :],
                             W1[bass.ds(e, 1), :, :].rearrange("o (k p) f -> p (o k) f", p=P)).then_inc(s_fw, 16)
                sp.dma_start(w2_sb[:, i, :, :],
                             W2[bass.ds(e, 1), :, :].rearrange("o (k p) f -> p (o k) f", p=P)).then_inc(s_fw, 16)
                sp.dma_start(b1_sb[:, i, :], b1[bass.ds(e, 1), :].rearrange("o (k p) -> p (o k)", p=P),
                             allow_slow_non_contiguous=True).then_inc(s_fw, 16)
                sp.dma_start(b2_sb[:, i, :], b2[bass.ds(e, 1), :].to_broadcast([P, D])).then_inc(s_fw, 16)
            sp3.credit(sp)
            with sp.Fori(0, (GROUPS - 1) // 6) as k:
                for j in range(6):
                    at3, at2 = At(k * 2, 3, j), At(k * 3, 2, j)
                    dve3.wait(sp, "out", at2, -1)
                    hold(sp, s_sp_held)
                    load_group(at3, 2)
                    dve3.wait(sp, "out", at2)
                    hold(sp, s_sp_held)
                    sp.dma_start(out[bass.ds(at2.number() * GROUP, GROUP), :].rearrange("(q p) d -> p q d", p=P),
                                 fo[:, at2.slot(), :, :]).then_inc(s_out, 16)
                    sp.wait_ge(s_out, at2.k * 32 + 16 * (j + 1))
                    hold(sp, s_sp_held)
                    sp3.skip(sp, ["stored"], at2)
            last = At(0, 2, GROUPS - 1)
            dve3.wait(sp, "out", last)
            hold(sp, s_sp_held)
            tail = [(r, min(P, N - r)) for r in range((GROUPS - 1) * GROUP, N, P)]
            for q, (r, n) in enumerate(tail):
                sp.dma_start(out[r:r + n, :], fo[0:n, last.slot(), q, :]).then_inc(s_out, 16)
            sp.wait_ge(s_out, 16 * (GROUPS - 1 + len(tail)))
            for j in range(3):
                sp.wait_ge(s_fx[j], 16 * len([g for g in range(GROUPS + 1) if g % 3 == j]))

        @block.gpsimd
        def _(pool):
            pool.iota(iota_row[:, :], [[1, P]], base=0, channel_multiplier=0,
                      allow_small_or_imprecise_dtypes=True).then_inc(s_const, 1)
            pool.iota(iota_col[:, :], [[0, 1]], base=0, channel_multiplier=1,
                      allow_small_or_imprecise_dtypes=True).then_inc(s_const, 1)
            pool.memset(ones[:, :], 1.0).then_inc(s_const, 1)
            pool.memset(eps[:, :], LN_EPS).then_inc(s_const, 1)
            pool.memset(zeros[:, :], 0.0).then_inc(s_const, 1)
            pool.memset(ident[:, :], 0.0).then_inc(s_const, 1)
            pool.wait_ge(s_const, 6)
            pool.affine_select(out=ident[:, :], in_=ident[:, :], compare_op=ALU.not_equal, fill=1.0, base=0,
                               pattern=[[-1, P]], channel_multiplier=1).then_inc(s_const, 1)
            pool.memset(row_out[:, :, :], 1.0).then_inc(s_pool, 1)
            pool.memset(newseg[:, :, :], 1.0).then_inc(s_pool, 1)
            pool.memset(acc[:, :], 1.0).then_inc(s_pool, 1)
            pool.memset(carry[:, :], 0.0).then_inc(s_pool, 1)
            for j in range(ROWS_RING):
                pool.wait_ge(s_tab[j], 16 * (BLOCKS // ROWS_RING + 1))
            total = steps_to_run(pool)
            bound = pool.to_reg(BLOCKS * P - 1)

            def gather(at, follows):
                slot = at.slot()
                pool.wait_ge(s_idx[slot], at.landed(1))
                dve2.wait(pool, MSGS[-1], at, -2)
                act2.wait(pool, "asrc", at, -2)
                hold(pool, s_granted)
                for t in range(TILES):
                    pool.indirect_dma_start(rows[:, slot, t, :], None, table,
                                            bass.IndirectOffsetOnAxis(ap=idx[slot][:, t:t + 1], axis=0),
                                            bounds_check=bound, oob_is_err=False).then_inc(s_rows[slot], 16)

            walk(pool, total, gather)

        @block.tensor
        def _(pe):
            pe.wait_ge(s_setup, N_ATT)
            for k in range(KD):
                mm = pe.matmul(psW, ones[:, :], wx[:, k, :], start=(k == 0), stop=(k == KD - 1))
            mm.then_inc(s_once, 1)
            p1_pe.credit(pe, ahead=["xT"])

            def transpose_x(at, lead):
                pe.wait_ge(s_x[at.slot(lead)], at.landed(1, lead))
                p1_dve.wait(pe, "xT", at, lead - 2)
                for k in range(KD):
                    mm = pe.transpose(psX[(at.off + lead) % 2][:, k, :], x_in[:, at.slot(lead), k * P:(k + 1) * P],
                                      ident[:, :])
                p1_pe.mark("xT", mm)

            transpose_x(At(0, ROWS_RING, 0), 0)
            p1_pe.rest(pe, ["xT"])
            pe.wait_ge(s_setup, N_WX)
            with pe.Fori(0, BLOCKS // ROWS_RING) as k:
                for j in range(ROWS_RING):
                    at = At(k, ROWS_RING, j)
                    transpose_x(at, 1)
                    p1_dve.wait(pe, "xT", at)
                    p1_act.wait(pe, "logits", at, -2)
                    for kk in range(KD):
                        mm = pe.matmul(psH[j % 2], xT[:, j % 2, kk, :], wx[:, kk, :], start=(kk == 0),
                                       stop=(kk == KD - 1))
                    p1_pe.mark("rows", mm)
            pe.wait_ge(s_setup, N_LOWS)
            pe.matmul(psS[:, 0:256], ones[0:1, :], lows[0:1, 1, :], start=True, stop=True)
            pe.matmul(psS[:, 256:512], ones[0:1, :], lows[0:1, 2, :], start=True, stop=True).then_inc(s_once, 1)
            pe.matmul(bank[7][0:1, 0:D], zeros[:, 0:1], zeros[:, :], start=True, stop=False, skip_group_check=True)
            pe.matmul(bank[7][0:1, D:D + 1], zeros[:, 0:1], zeros[:, 0:1], start=False, stop=False,
                      skip_group_check=True)
            pe2.credit(pe)
            p1_end = At(BLOCKS // ROWS_RING - 1, ROWS_RING, ROWS_RING - 1)
            p1_act.wait(pe, "logits", p1_end)
            total = steps_to_run(pe)

            def step(at, follows):
                s, q = at.slot(), at.slot(-1)
                act2.wait(pe, "asrc", at)
                dve2.wait(pe, "runmax", at, -1)
                pe2.mark("lT", pe.matmul(psT, asrc[:, :], ident[:, :], start=True, stop=True))
                dve2.wait(pe, "lastmax", at)
                dve2.wait(pe, "last_lo", at, -1)
                pe2.mark("lastT", pe.matmul(psR, lastmax[:, :], ident[0:SR, 0:SR], start=True, stop=True))
                dve2.wait(pe, "last_lo", at)
                dve2.wait(pe, "node_v", at, -1)
                for t in range(TILES):
                    mm = pe.matmul(psM[:, t * 3 * R5:(t + 1) * 3 * R5], oh_b[:, s, t, :],
                                   last_p[:, t, :, :].rearrange("p a r -> p (a r)"), start=True, stop=True)
                pe2.mark("nodemax", mm)
                dve2.wait(pe, "adsh_lo", at)
                dve2.wait(pe, "edge_v", at, -1)
                for t in range(TILES):
                    mm = pe.matmul(psE[:, t * 6 * H:(t + 1) * 6 * H], ohT[:, s, t, :],
                                   adsh_p[:, :, :].rearrange("p a r -> p (a r)"), start=True, stop=True)
                pe2.mark("expand", mm)
                if follows:
                    dve2.wait(pe, "mergedshift", at)
                    act2.wait(pe, "carry", at, -1)
                    pe2.mark("carry", pe.matmul(psC, sel[:, q:q + 1], acc[:, :], start=True, stop=True))
                else:
                    pe2.skip(pe, ["carry"], at)
                act2.wait(pe, "acc", at, -1)
                act2.wait(pe, "oh", at, -1)
                for t in range(TILES):
                    if t % 2 == 0:
                        dve2.wait(pe, MSGS[t // 2], at)
                    mm = pe.matmul(psA[s], oh[:, s, t, :], msg[:, s, t, :], start=(t == 0), stop=(t == TILES - 1))
                pe2.mark("agg", mm)
                if follows:
                    dve2.wait(pe, "mu", at)
                    pe2.mark("router", pe.matmul(psZ, m_lhs[:, q:q + 1], x_o[:, q, :], start=False, stop=False,
                                                 skip_group_check=True))
                else:
                    pe2.skip(pe, ["router"], at)

            walk(pe, total, step)
            pe.drain().then_inc(s_once, 1)
            pe.wait_ge(s_setup, N_MEAN)
            for k in range(KD):
                mm = pe.matmul(bank[0][:, k:k + 1], zrow[0:1, k * P:(k + 1) * P], ones[0:1, 0:1], start=True, stop=True)
            mm.then_inc(s_once, 1)
            pe.wait_ge(s_setup, N_MEAN + 1)
            pe.wait_ge(s_fwr, 64)
            for k in range(KD):
                mm = pe.matmul(bank[1][0:1, 0:NE], zcol[:, k:k + 1], wr_sb[:, k, :], start=(k == 0), stop=(k == KD - 1))
            mm.then_inc(s_once, 1)
            pe.wait_ge(s_setup, N_TOP)
            pe.matmul(bank[2][:, 0:2], ones[0:1, :], rt[0:1, WTOP, 0:2], start=True, stop=True).then_inc(s_once, 1)

            pe3.credit(pe, ahead=["xT"])

            def transpose_rows(at, lead):
                dve3.wait(pe, "xn", at, lead - 1)
                dve3.wait(pe, "xT", at, lead - 2)
                for k in range(KD):
                    for q in range(QB):
                        mm = pe.transpose(psF[k][:, q * P:(q + 1) * P],
                                          fxn[:, at.slot(lead), q, k * P:(k + 1) * P], ident[:, :])
                pe3.mark("xT", mm)

            def group(at):
                dve3.wait(pe, "xT", at, -1)
                for f in range(2 * KF):
                    e, fk = divmod(f, KF)
                    u = psU[f % len(psU)]
                    g = f - len(psU)
                    act3.wait(pe, HID[g], at, 0 if g >= 0 else -1)
                    for k in range(KD):
                        mm = pe.matmul(u, w1_sb[:, e, k, fk * P:(fk + 1) * P], fxT[:, at.slot(), k, :],
                                       start=(k == 0), stop=(k == KD - 1))
                    pe3.mark(HID[f], mm)
                dve3.wait(pe, "res", at, -1)
                for q in range(QB):
                    if q == QB // 2:
                        pe3.mark("half", mm)
                        transpose_rows(at, 1)
                    for f in range(2 * KF):
                        e, fk = divmod(f, KF)
                        if q == 0:
                            act3.wait(pe, HID[f], at)
                        mm = pe.matmul(psY[q // 2][:, q % 2, :], hT[:, f, q * P:(q + 1) * P], w2_sb[:, e, fk, :],
                                       start=(f == 0), stop=(f == 2 * KF - 1))
                pe3.mark("out", mm)

            pe.wait_ge(s_setup, N_EXPERT)
            transpose_rows(At(0, 2, 0), 0)
            pe3.rest(pe, ["xT"])
            with pe.Fori(0, (GROUPS - 1) // 2) as k:
                for j in range(2):
                    group(At(k, 2, j))
            group(At(0, 2, GROUPS - 1))

        @block.scalar
        def _(act):
            act.preload_act_table_set("natural_log_exp_and_others")
            p1_act.credit(act)
            act.wait_ge(s_const, 7)
            act.wait_ge(s_pool, 4)
            with act.Fori(0, BLOCKS // ROWS_RING) as k:
                for j in range(ROWS_RING):
                    at = At(k, ROWS_RING, j)
                    p1_dve.wait(act, "mv", at)
                    p1_mark = p1_act.mark
                    p1_mark("ln", act.activation(y1[:, j, 0:1], mv1[:, j, 1:2], ACT.Ln, bias=eps[:, 0:1]))
                    p1_act.wait(act, "ln", at)
                    p1_mark("rstd", act.activation(y1[:, j, 1:2], y1[:, j, 0:1], ACT.Exp, scale=-0.5))
                    p1_act.wait(act, "rstd", at)
                    p1_pe.wait(act, "rows", at)
                    act.wait_ge(s_tab[j], at.k * 16 + 16)
                    p1_mark("rows", act.activation(head_cols(row_out[:, j, 0:HC1])[:, :, 0:C],
                                                   head_cols(psH[j % 2][:, 0:D]), ACT.Copy, scale=y1[:, j, 1:2]))
                    p1_mark("logits", act.activation(row_out[:, j, AS:TW], psH[j % 2][:, D:D + 2 * H], ACT.Copy,
                                                     scale=y1[:, j, 1:2]))
            act2.credit(act, ahead=["oh"])
            total = steps_to_run(act)

            def convert_one_hots(at, lead):
                slot = at.slot(lead)
                dve2.wait(act, "oh", at, lead - 1)
                pe2.wait(act, "agg", at, lead - 2)
                act2.mark("oh", act.activation(oh[:, slot, :, :], oh_b[:, slot, :, :], ACT.Copy))

            convert_one_hots(At(0, 2, 0), 0)
            act2.rest(act, ["oh"])

            def step(at, follows):
                s, q = at.slot(), at.slot(-1)
                act.wait_ge(s_rows[s], at.landed(TILES))
                pe2.wait(act, "lT", at, -1)
                act2.mark("asrc", act.activation(asrc[:, :].rearrange("p (t r) -> p t r", r=R5),
                                                 rows[:, s, :, ONE:AD], ACT.Copy))
                if follows:
                    pe2.wait(act, "agg", at, -1)
                    dve2.wait(act, "num", at, -1)
                    pe2.wait(act, "carry", at, -1)
                    act2.mark("acc", act.activation(acc[:, 0:HC1], psA[q], ACT.Copy))
                else:
                    act2.skip(act, ["acc"], at)
                if follows:
                    dve2.wait(act, "r_d", at)
                    act2.mark("rexp", act.activation(r_f[:, :], r_d[:, :], ACT.Exp))
                    act2.wait(act, "rexp", at)
                    act2.wait(act, "carry", at, -1)
                    for h in range(H):
                        ins = act.activation(head_cols(r_c[:, :])[:, h, :], head_cols(carry[:, 0:HC1])[:, h, :],
                                             ACT.Copy, scale=r_f[:, h:h + 1])
                    act2.mark("carried", ins)
                else:
                    act2.skip(act, ["rexp", "carried"], at)
                convert_one_hots(at, 1)
                if follows:
                    dve2.wait(act, "self_d", at)
                    act2.mark("wself", act.activation(ws[:, :], zs[:, :], ACT.Exp))
                    pe2.wait(act, "carry", at)
                    act2.mark("carry", act.activation(carry[:, :], psC, ACT.Copy))
                else:
                    act2.skip(act, ["wself", "carry"], at)
                dve2.wait(act, "dmin", at)
                act2.mark("we", act.activation(we[:, s, :, :], le[:, :, :], ACT.Exp))
                if follows:
                    for n, src in (("1", "mv"), ("2", "mv_m")):
                        c = 2 * int(n) - 2
                        dve2.wait(act, src, at)
                        act2.mark("ln" + n, act.activation(ln2[:, c:c + 1], mv2[:, c + 1:c + 2], ACT.Ln,
                                                           bias=eps[:, 0:1]))
                        act2.wait(act, "ln" + n, at)
                        act2.mark("y" + n, act.activation(ln2[:, c + 1:c + 2], ln2[:, c:c + 1], ACT.Exp, scale=-0.5))
                else:
                    act2.skip(act, ["ln1", "y1", "ln2", "y2"], at)

            walk(act, total, step)

            for n in N_EXP:
                act.wait_ge(s_setup, n)
                act.activation(rt[:, 13, :], rt[:, 14, :], ACT.Exp).then_inc(s_exp, 1)

            act3.credit(act)

            def group(at):
                for f in range(2 * KF):
                    e, fk = divmod(f, KF)
                    pe3.wait(act, HID[f], at)
                    if f == 0:
                        pe3.wait(act, "out", at, -1)
                    act3.mark(HID[f], act.activation(hT[:, f, :], psU[f % len(psU)], ACT.Gelu,
                                                     bias=b1_sb[:, e, fk:fk + 1]))

            act.wait_ge(s_fw, 128)
            with act.Fori(0, (GROUPS - 1) // 2) as k:
                for j in range(2):
                    group(At(k, 2, j))
            group(At(0, 2, GROUPS - 1))

        @block.vector
        def _(dve):
            done = [0]

            def link(ins):
                done[0] += 1
                ins.then_inc(s_setup, 1)
                dve.wait_ge(s_setup, done[0])

            link(dve.memset(first[:, :], N))
            dve.wait_ge(s_w, 96)
            dve.wait_ge(s_const, 7)
            for k in range(KD):
                for i in range(2):
                    link(dve.tensor_tensor(att_tmp[:, :], wx[:, k, 0:D], att[:, i, :], ALU.mult))
                    link(dve.tensor_reduce(wx[:, k, D + i * H:D + (i + 1) * H], head_cols(att_tmp[:, :]), X, ALU.add))
            assert done[0] == N_ATT
            dve.wait_ge(s_once, 1)
            for k in range(KD):
                link(dve.scalar_tensor_tensor(out=wx[:, k, :], in0=psW, scalar=-1.0 / D, in1=wx[:, k, :],
                                              op0=ALU.mult, op1=ALU.add))
            assert done[0] == N_WX
            p1_dve.credit(dve)
            with dve.Fori(0, BLOCKS // ROWS_RING) as k:
                for j in range(ROWS_RING):
                    at = At(k, ROWS_RING, j)
                    dve.wait_ge(s_x[j], at.landed(1))
                    p1_dve.mark("stats", dve.bn_stats(st1[:, j, :], x_in[:, j, :]))
                    p1_dve.wait(dve, "stats", at)
                    p1_act.wait(dve, "ln", at, -4)
                    hold(dve, s_dve_held)
                    p1_dve.mark("mv", dve.bn_aggr(mv1[:, j, :], st1[:, j, :]))
                    p1_pe.wait(dve, "xT", at, -1)
                    p1_pe.wait(dve, "rows", at, -2)
                    p1_dve.mark("xT", dve.tensor_copy(xT[:, j % 2, :, :], psX[j % 2]))
            dve.wait_ge(s_sched, 16)
            link(dve.memset(first[:, 0:1], 0))
            link(dve.tensor_tensor(gap[:, :], first[:, 1:257], first[:, 0:256], ALU.subtract))
            link(dve.tensor_scalar(gap[:, :], gap[:, :], 7, None, ALU.arith_shift_right))
            link(dve.tensor_scalar(lows[:, 0, :], gap[:, :], 1.0, None, ALU.add))
            link(dve.memset(lows[:, 1, 0:1], 0.0))
            link(dve.tensor_tensor_scan(lows[:, 1, 1:256], lows[:, 0, 0:255], zeros[0:1, 0:255], 0.0, ALU.add, ALU.add))
            link(dve.scalar_tensor_tensor(out=lows[:, 2, :], in0=lows[:, 1, :], scalar=-float(P), in1=first[:, 0:256],
                                          op0=ALU.mult, op1=ALU.add))
            link(dve.tensor_scalar(tot_i[:, 0:1], lows[:, 1, chunks:chunks + 1], 1.0, None, ALU.add))
            assert done[0] == N_LOWS
            dve.wait_ge(s_once, 2)
            link(dve.tensor_copy(s_both[:, :, :], psS[:, :].rearrange("p (a s) -> p a s", a=2)))
            for half in range(2):
                col = s_col[:, half, :]
                link(dve.tensor_scalar(col[:, 0:1], iota_col[:, :], float(half * P), None, ALU.add))
                link(dve.tensor_scalar(s_cmp[:, half, 0:chunks], s_both[:, 0, 0:chunks], col[:, 0:1], None, ALU.is_le))
                link(dve.tensor_reduce(col[:, 1:2], s_cmp[:, half, 0:chunks], X, ALU.add))
                link(dve.tensor_scalar(s_out_i[:, 1, half:half + 1], col[:, 1:2], -1.0, None, ALU.add))
                link(dve.tensor_scalar(s_cmp[:, half, 0:chunks + 1], s_both[:, 0, 0:chunks + 1], col[:, 0:1], 1e9,
                                       ALU.is_gt, ALU.mult))
                link(dve.tensor_tensor(s_cmp[:, half, 0:chunks + 1], s_cmp[:, half, 0:chunks + 1],
                                       s_both[:, 1, 0:chunks + 1], ALU.add))
                link(dve.tensor_reduce(col[:, 2:3], s_cmp[:, half, 0:chunks + 1], X, ALU.min))
                link(dve.scalar_tensor_tensor(out=col[:, 3:4], in0=col[:, 0:1], scalar=float(P), in1=col[:, 2:3],
                                              op0=ALU.mult, op1=ALU.add))
                link(dve.tensor_scalar(s_out_i[:, 0, half:half + 1], col[:, 3:4], float(N + P), None, ALU.min))
            assert done[0] == N_SETUP
            total = steps_to_run(dve)
            link(dve.tensor_copy(w_tab[:, :], step_tab[:, 0, :]))
            link(dve.tensor_copy(iota_b[:, :], iota_row[:, :]))
            dve2.credit(dve, ahead=DVE_A)

            def one_hots(at, lead):
                s, b = at.slot(lead), lead - 1
                dve2.mark("wcur", dve.tensor_copy(wcur[:, s, :], w_tab[:, bass.ds(at.number(lead), 2)]))
                dve2.wait(dve, "wcur", at, b)
                dve2.mark("node", dve.tensor_tensor(node[:, s:s + 1], iota_col[:, :], wcur[:, s, 0:1], ALU.add))
                dve.wait_ge(s_dst[s], at.landed(3, lead))
                dve2.mark("drel", dve.tensor_scalar(drel[:, s, :], dst_e[:, s, :], wcur[:, s, 0:1], None, ALU.subtract))
                dve2.mark("newseg", dve.tensor_tensor(newseg[:, s, 1:P], dst_s[:, s, 1:P], dst_s[:, s, 0:P - 1],
                                                      ALU.not_equal))
                dve2.wait(dve, "newseg", at, b)
                dve2.mark("pen", dve.tensor_scalar(pen[:, s, :], newseg[:, s, 0:P], -BIG, None, ALU.mult))

            def more_one_hots(at, lead):
                s, b = at.slot(lead), lead - 1
                pe2.wait(dve, "expand", at, b - 1)
                dve2.mark("ohT", dve.tensor_scalar(ohT[:, s, :, :].rearrange("p t n -> p (t n)"), dst_b[:, s, :],
                                                   node[:, s:s + 1], None, ALU.is_equal))
                pe2.wait(dve, "nodemax", at, b - 1)
                act2.wait(dve, "oh", at, b - 2)
                dve2.wait(dve, "drel", at, b)
                dve2.mark("oh", dve.tensor_tensor(oh_b[:, s, :, :], over(drel[:, s, :], P),
                                                  iota_b[:, :].unsqueeze(1).to_broadcast([P, TILES, P]), ALU.is_equal))

            def step(at, follows):
                s, q = at.slot(), at.slot(-1)
                mark = dve2.mark

                def own(name, lead=0):
                    dve2.wait(dve, name, at, lead)

                def parts(p, value, rest, names):
                    mark(names[0], dve.tensor_copy(p(0), value))
                    own(names[0])
                    mark(names[1], dve.tensor_tensor(rest, value, p(0), ALU.subtract))
                    mark(names[2], dve.tensor_tensor(p(1), value, p(0), ALU.subtract))
                    own(names[2])
                    mark(names[3], dve.tensor_tensor(p(2), rest, p(1), ALU.subtract))

                one_hots(at, 1)
                pe2.wait(dve, "lT", at)
                mark("runmax", dve.tensor_tensor_scan(runmax[:, :], pen[:, s, :], psT, -BIG, ALU.add, ALU.max))
                own("runmax")
                mark("lastmax", dve.tensor_tensor(lastmax[:, :], runmax[:, :], newseg[:, s, 1:P + 1], ALU.mult))
                mark("sel", dve.tensor_tensor(sel[:, s:s + 1], node[:, s:s + 1], wcur[:, s, 1:2], ALU.is_equal))
                mark("mask", dve.tensor_tensor(mask[:, s:s + 1], node[:, s:s + 1], wcur[:, s, 1:2], ALU.is_lt))
                if follows:
                    mark("r_t", dve.tensor_scalar(r_t[:, :], carry[:, HAS:HAS + 1], BIG, -BIG, ALU.mult, ALU.add))
                    own("r_t")
                    mark("r_sc", dve.tensor_scalar(r_sc[:, :], carry[:, SHIFT:HAS], r_t[:, 0:1], None, ALU.add))
                    own("r_sc")
                    mark("r_mn", dve.tensor_tensor(r_mn[:, :], r_sc[:, :], adsh[0:1, q, H:], ALU.max))
                    own("r_mn")
                    mark("r_d1", dve.tensor_tensor(r_d[:, 0:H], r_sc[:, :], r_mn[:, :], ALU.subtract))
                    mark("r_d", dve.tensor_tensor(r_d[:, H:], adsh[0:1, q, H:], r_mn[:, :], ALU.subtract))
                else:
                    dve2.skip(dve, DVE_F1, at)
                pe2.wait(dve, "lastT", at)
                parts(lambda i: last_p[:, :, i, :], psR.rearrange("p (t r) -> p t r", r=R5), last_r[:, :, :],
                      "last_hi last_r last_mid last_lo".split())
                more_one_hots(at, 1)
                pe2.wait(dve, "nodemax", at)
                mark("node_v", dve.tensor_reduce(node_v[:, :, :], psM.rearrange("p (t a r) -> p t r a", a=3, r=R5),
                                                 X, ALU.add))
                own("node_v")
                mark("nohas", dve.tensor_scalar(nohas[:, :], node_v[:, :, 0], BIG, -BIG, ALU.mult, ALU.add))
                own("nohas")
                mark("mtile", dve.tensor_tensor(mtile[:, :, :], node_v[:, :, 1:R5], over(nohas[:, :], H), ALU.add))
                own("mtile")
                mark("mnode", dve.tensor_reduce(mnode[:, :], mtile[:, :, :].rearrange("p t h -> p h t"), X, ALU.max))
                dve.wait_ge(s_win[s], at.landed(2))
                own("mnode")
                mark("maxself", dve.tensor_tensor(mnode[:, :], mnode[:, :], tab_w[:, s, AS:AD], ALU.max))
                mark("ad", dve.tensor_copy(adsh[:, s, 0:H], tab_w[:, s, AD:TW]))
                own("maxself")
                mark("zn", dve.tensor_tensor(zn[:, :], mnode[:, :], tab_w[:, s, AD:TW], ALU.add))
                own("zn")
                mark("shift", dve.scalar_tensor_tensor(out=adsh[:, s, H:], in0=zn[:, :], scalar=NEG_SLOPE, in1=zn[:, :],
                                                       op0=ALU.mult, op1=ALU.max))
                own("shift")
                parts(lambda i: adsh_p[:, i, :], adsh[:, s, :], adsh_r[:, :], "adsh_hi adsh_r adsh_mid adsh_lo".split())
                if follows:
                    act2.wait(dve, "acc", at)
                    mark("accshift", dve.tensor_copy(acc[:, SHIFT:HAS], adsh[:, q, H:]))
                    act2.wait(dve, "carried", at)
                    for h in range(H):
                        a0 = head_cols(acc[0:1, 0:HC1])[:, h, :]
                        ins = dve.scalar_tensor_tensor(out=a0, in0=a0, scalar=r_f[:, H + h:H + h + 1],
                                                       in1=head_cols(r_c[:, :])[:, h, :], op0=ALU.mult, op1=ALU.add)
                    mark("merged", ins)
                    own("accshift")
                    mark("mergedshift", dve.tensor_copy(acc[0:1, SHIFT:HAS], r_mn[:, :]))
                    mark("self_z", dve.tensor_tensor(zs[:, :], tab_w[:, q, AS:AD], tab_w[:, q, AD:TW], ALU.add))
                    own("self_z")
                    mark("self_l", dve.scalar_tensor_tensor(out=zs[:, :], in0=zs[:, :], scalar=NEG_SLOPE,
                                                            in1=zs[:, :], op0=ALU.mult, op1=ALU.max))
                    own("self_l")
                    mark("self_d", dve.tensor_tensor(zs[:, :], zs[:, :], acc[:, SHIFT:HAS], ALU.subtract))
                else:
                    dve2.skip(dve, DVE_F2, at)
                pe2.wait(dve, "expand", at)
                act2.wait(dve, "we", at, -1)
                mark("edge_v", dve.tensor_reduce(edge_v[:, :, :], psE.rearrange("p (t a r) -> p t r a", a=3, r=2 * H),
                                                 X, ALU.add))
                own("edge_v")
                mark("ze", dve.tensor_tensor(ze[:, :, :], rows[:, s, :, AS:AD], edge_v[:, :, 0:H], ALU.add))
                own("ze")
                mark("le", dve.scalar_tensor_tensor(out=ze[:, :, :], in0=ze[:, :, :], scalar=NEG_SLOPE,
                                                    in1=ze[:, :, :], op0=ALU.mult, op1=ALU.max))
                own("le")
                mark("d", dve.tensor_tensor(le[:, :, :], ze[:, :, :], edge_v[:, :, H:], ALU.subtract))
                own("d")
                mark("dmin", dve.tensor_scalar(le[:, :, :], le[:, :, :], 0.0, None, ALU.min))
                if follows:
                    act2.wait(dve, "wself", at)
                    own("merged")
                    numh = head_cols(num[:, :])
                    for h in range(H):
                        ins = dve.scalar_tensor_tensor(out=numh[:, h, :], in0=head_cols(tab_w[:, q, 0:HC1])[:, h, :],
                                                       scalar=ws[:, h:h + 1], in1=head_cols(acc[:, 0:HC1])[:, h, :],
                                                       op0=ALU.mult, op1=ALU.add)
                    mark("num", ins)
                    own("num")
                    mark("den", dve.tensor_scalar(rden[:, :], numh[:, :, C], DEN_EPS, None, ALU.add))
                    own("den")
                    mark("rden", dve.reciprocal(rden[:, :], rden[:, :]))
                    own("rden")
                    for h in range(H):
                        ins = dve.scalar_tensor_tensor(out=o[:, h * C:(h + 1) * C], in0=numh[:, h, 0:C],
                                                       scalar=rden[:, h:h + 1], in1=g_aff[:, 0, h * C:(h + 1) * C],
                                                       op0=ALU.mult, op1=ALU.add)
                    mark("biased", ins)
                    own("biased")
                    mark("st", dve.bn_stats(st2[:, :], o[:, :]))
                    own("st")
                    hold(dve, s_dve_held)
                    mark("mv", dve.bn_aggr(mv2[:, 0:2], st2[:, :]))
                    own("mv")
                    mark("v", dve.tensor_scalar(vv[:, 0:1], mv2[:, 1:2], LN_EPS, None, ALU.add))
                else:
                    dve2.skip(dve, DVE_F3, at)

                def messages(names):
                    for name in names:
                        t = 2 * MSGS.index(name)
                        w = we[:, s, t:t + 2, :]
                        mark(name, dve.tensor_tensor(
                            msg[:, s, t:t + 2, :].rearrange("p t (h c) -> p t h c", h=H),
                            rows[:, s, t:t + 2, 0:HC1].rearrange("p t (h c) -> p t h c", h=H),
                            over(w, C + 1), ALU.mult))

                act2.wait(dve, "we", at)
                messages(MSGS[:4])
                if follows:
                    def refine(y, v, names):
                        mark(names[0], dve.scalar_tensor_tensor(out=nt[:, 0:1], in0=y, scalar=v, in1=y,
                                                                op0=ALU.mult, op1=ALU.mult))
                        own(names[0])
                        mark(names[1], dve.tensor_scalar(nt[:, 1:2], nt[:, 0:1], -0.5, 1.5, ALU.mult, ALU.add))
                        own(names[1])
                        mark(names[2], dve.tensor_tensor(nt[:, 2:3], nt[:, 1:2], y, ALU.mult))
                        own(names[2])

                    mark("gam", dve.scalar_tensor_tensor(out=o[:, :], in0=o[:, :], scalar=mv2[:, 0:1],
                                                         in1=g_aff[:, 1, :], op0=ALU.subtract, op1=ALU.mult))
                    act2.wait(dve, "y1", at)
                    own("v")
                    refine(ln2[:, 1:2], vv[:, 0:1], ("n1", "n2", "rstd"))
                    own("rstd")
                    mark("normed", dve.scalar_tensor_tensor(out=o[:, :], in0=o[:, :], scalar=nt[:, 2:3],
                                                            in1=g_aff[:, 2, :], op0=ALU.mult, op1=ALU.add))
                    own("normed")
                    sp2.wait(dve, "stored", at, -1)
                    pe2.wait(dve, "router", at, -2)
                    mark("xmid", dve.scalar_tensor_tensor(out=x_o[:, q, 0:D], in0=o[:, :], scalar=0.0,
                                                          in1=x_w[:, q, :], op0=ALU.max, op1=ALU.add))
                    own("xmid")
                    mark("st_m", dve.bn_stats(st2[:, :], x_o[:, q, 0:D]))
                    own("st_m")
                    hold(dve, s_dve_held)
                    mark("mv_m", dve.bn_aggr(mv2[:, 2:4], st2[:, :]))
                    own("mv_m")
                    mark("v_m", dve.tensor_scalar(vv[:, 1:2], mv2[:, 3:4], LN_EPS, None, ALU.add))
                else:
                    dve2.skip(dve, DVE_F4, at)
                messages(MSGS[4:])
                if follows:
                    act2.wait(dve, "y2", at)
                    own("v_m")
                    refine(ln2[:, 3:4], vv[:, 1:2], ("m1", "m2", "m_rstd"))
                    mark("lhs", dve.tensor_tensor(m_lhs[:, q:q + 1], nt[:, 2:3], mask[:, q:q + 1], ALU.mult))
                    mark("mu", dve.tensor_copy(x_o[:, q, D:D + 1], mv2[:, 2:3]))
                else:
                    dve2.skip(dve, DVE_F5, at)

            one_hots(At(0, 2, 0), 0)
            dve2.rest(dve, DVE_A, DVE_B)
            more_one_hots(At(0, 2, 0), 0)
            dve2.rest(dve, DVE_B)
            walk(dve, total, step)

            dve.wait_ge(s_once, 3)
            link(dve.tensor_copy(zrow[:, :], psZ))
            link(dve.tensor_scalar(zrow[:, 0:D], zrow[:, 0:D], zrow[:, D:D + 1], 1.0 / N, ALU.subtract, ALU.mult))
            assert done[0] == N_MEAN
            dve.wait_ge(s_once, 4)
            link(dve.tensor_copy(zcol[:, :], bank[0][:, 0:KD]))
            dve.wait_ge(s_once, 5)
            link(dve.tensor_tensor(rt[:, 1, :], bank[1][0:1, 0:NE], rt[:, 0, :], ALU.add))

            exps = [0]

            def softmax(src, to):
                link(dve.tensor_reduce(rt[:, 15, 0:1], rt[:, src, :], X, ALU.max))
                link(dve.tensor_scalar(rt[:, 14, :], rt[:, src, :], rt[:, 15, 0:1], None, ALU.subtract))
                assert done[0] == N_EXP[exps[0]]
                exps[0] += 1
                dve.wait_ge(s_exp, exps[0])
                link(dve.tensor_reduce(rt[:, 15, 1:2], rt[:, 13, :], X, ALU.add))
                link(dve.reciprocal(rt[:, 15, 2:3], rt[:, 15, 1:2]))
                link(dve.tensor_scalar(rt[:, to, :], rt[:, 13, :], rt[:, 15, 2:3], None, ALU.mult))

            softmax(1, 2)
            capacity = float(math.ceil(N * CAPACITY_FACTOR / NE))
            link(dve.tensor_scalar(rt[:, 3, :], rt[:, 2, :], float(N), 1e-30, ALU.mult, ALU.max))
            link(dve.reciprocal(rt[:, 4, :], rt[:, 3, :]))
            link(dve.tensor_scalar(rt[:, 5, :], rt[:, 4, :], capacity, 1.0, ALU.mult, ALU.min))
            link(dve.tensor_tensor(rt[:, 6, :], rt[:, 5, :], rt[:, 2, :], ALU.mult))
            softmax(6, 7)
            link(dve.max(rt[:, 8, :], rt[:, 7, :]))
            link(dve.max_index(top_i[:, :], rt[:, 8, :], rt[:, 7, :]))
            link(dve.tensor_copy(top_ii[:, :], top_i[:, :]))
            link(dve.tensor_scalar(rt[:, 14, :], rt[:, 8, :], rt[:, 8, 0:1], None, ALU.subtract))
            assert done[0] == N_EXP[exps[0]]
            dve.wait_ge(s_exp, exps[0] + 1)
            link(dve.tensor_reduce(rt[:, 15, 1:2], rt[:, 13, 0:2], X, ALU.add))
            link(dve.reciprocal(rt[:, 15, 2:3], rt[:, 15, 1:2]))
            link(dve.tensor_scalar(rt[:, WTOP, 0:2], rt[:, 13, 0:2], rt[:, 15, 2:3], None, ALU.mult))
            assert done[0] == N_TOP
            dve.wait_ge(s_once, 6)
            link(dve.tensor_copy(wtop[:, :], bank[2][:, 0:2]))
            dve.wait_ge(s_fw, 128)
            for i in range(2):
                flat = w2_sb[:, i, :, :].rearrange("p k d -> p (k d)")
                link(dve.tensor_scalar(flat, flat, wtop[:, i:i + 1], None, ALU.mult))
            link(dve.tensor_scalar(b2_w[:, :], b2_sb[:, 0, :], wtop[:, 0:1], None, ALU.mult))
            link(dve.scalar_tensor_tensor(out=b2_w[:, :], in0=b2_sb[:, 1, :], scalar=wtop[:, 1:2], in1=b2_w[:, :],
                                          op0=ALU.mult, op1=ALU.add))
            assert done[0] == N_EXPERT
            dve3.credit(dve, ahead=DVE3_A)

            def normalise(at, at3, lead):
                s = at.slot(lead)
                dve.wait_ge(s_fx[at3.slot(lead)], at3.landed(1, lead))
                rstd_of(at, lead - 1, ["st", "mv"] + ROOT, lambda q: fx[:, at3.slot(lead), q, :])
                for q in range(QB):
                    ins = dve.tensor_scalar(fxn[:, s, q, :], fx[:, at3.slot(lead), q, :], fmv[:, q, 0:1],
                                            ft[:, q:q + 1], ALU.subtract, ALU.mult)
                dve3.mark("xn", ins)
                pe3.wait(dve, "xT", at, lead - 1)
                for k in range(KD):
                    ins = dve.tensor_copy(fxT[:, s, k, :], psF[k])
                dve3.mark("xT", ins)

            def rstd_of(at, lead, names, rows_of):
                def own(name):
                    dve3.wait(dve, name, at, lead)

                for q in range(QB):
                    ins = dve.bn_stats(fst[:, q, :], rows_of(q))
                dve3.mark(names[0], ins)
                own(names[0])
                hold(dve, s_dve_held)
                for q in range(QB):
                    ins = dve.bn_aggr(fmv[:, q, :], fst[:, q, :])
                dve3.mark(names[1], ins)
                own(names[1])
                dve3.mark(names[2], dve.tensor_scalar(fv[:, :], fmv[:, :, 1], LN_EPS, None, ALU.add))
                dve3.mark(names[3], dve.tensor_scalar(fh[:, :], fmv[:, :, 1], LN_EPS, -0.5, ALU.add, ALU.mult))
                own(names[2])
                dve3.mark(names[4], dve.tensor_scalar(ft[:, :].bitcast(I32), fv[:, :].bitcast(I32), -0.5,
                                                      ROOT_SEED, ALU.mult, ALU.add))
                own(names[4])
                for n in range(5, 14, 3):
                    dve3.mark(names[n], dve.tensor_tensor(fq[:, :], ft[:, :], ft[:, :], ALU.mult))
                    own(names[n])
                    dve3.mark(names[n + 1], dve.tensor_tensor(fq[:, :], fq[:, :], fh[:, :], ALU.mult))
                    own(names[n + 1])
                    dve3.mark(names[n + 2], dve.scalar_tensor_tensor(out=ft[:, :], in0=fq[:, :], scalar=1.5,
                                                                     in1=ft[:, :], op0=ALU.add, op1=ALU.mult))
                    own(names[n + 2])

            def group(at, at3):
                s = at.slot()
                y = fo[:, s, :, :]

                def own(name):
                    dve3.wait(dve, name, at)

                normalise(at, at3, 1)
                pe3.wait(dve, "out", at)
                sp3.wait(dve, "stored", at, -2)
                for i in range(2):
                    ins = dve.tensor_tensor(y[:, 2 * i:2 * i + 2, :], psY[i], fxn[:, s, 2 * i:2 * i + 2, :], ALU.add)
                dve3.mark("res", ins)
                own("res")
                dve3.mark("b2", dve.tensor_tensor(y, y, b2_w[:, :].unsqueeze(1).to_broadcast([P, QB, D]), ALU.add))
                own("b2")
                rstd_of(at, 0, ["st2", "mv2"] + ROOT2, lambda q: y[:, q, :])
                for q in range(QB):
                    ins = dve.scalar_tensor_tensor(out=y[:, q, :], in0=y[:, q, :], scalar=fmv[:, q, 0:1],
                                                   in1=f_aff[:, 0, :], op0=ALU.subtract, op1=ALU.mult)
                dve3.mark("gam", ins)
                own("gam")
                for q in range(QB):
                    ins = dve.scalar_tensor_tensor(out=y[:, q, :], in0=y[:, q, :], scalar=ft[:, q:q + 1],
                                                   in1=f_aff[:, 1, :], op0=ALU.mult, op1=ALU.add)
                dve3.mark("normed", ins)
                own("normed")
                dve3.mark("out", dve.tensor_tensor(y, y, fx[:, at3.slot(), :, :], ALU.add))

            normalise(At(0, 2, 0), At(0, 3, 0), 0)
            dve3.rest(dve, DVE3_A)
            with dve.Fori(0, (GROUPS - 1) // 6) as k:
                for j in range(6):
                    group(At(k * 3, 2, j), At(k * 2, 3, j))
            group(At(0, 2, GROUPS - 1), At(0, 3, GROUPS - 1))


def kernel(**inputs):
    import numpy as _np
    import concourse.bacc as _bacc
    from concourse.bass_utils import run_bass_kernel_spmd as _run

    N, E = inputs["x"].shape[0], inputs["src"].shape[0]
    chunks, _, blocks, _ = sizes(N, E)
    padded = chunks * CHUNK
    host = {k: _np.ascontiguousarray(v) for k, v in inputs.items()}
    rows = _np.zeros(((blocks + ROWS_RING - 1) * P, host["x"].shape[1]), host["x"].dtype)
    rows[:N] = host["x"]
    src = _np.zeros(padded, host["src"].dtype)
    src[:E] = host["src"]
    dst = _np.full(padded, PAD_NODE, host["dst"].dtype)
    dst[:E] = host["dst"]

    def tiles(a):
        return _np.ascontiguousarray(a.reshape(chunks, TILES, P).transpose(0, 2, 1)).reshape(chunks * P, TILES)

    arrays = {"x_rows": rows, "src_tiles": tiles(src), "dst": dst, "dst_tiles": tiles(dst)}
    arrays.update((k, host[k]) for k in _WEIGHTS)
    nc = _bacc.Bacc("TRN2", target_bir_lowering=False, num_devices=1)
    args = [nc.dram_tensor(f"in_{k}", a.shape, mybir.dt.from_np(a.dtype), kind="ExternalInput").ap()
            for k, a in arrays.items()]
    args.append(nc.dram_tensor("out_0", (N, rows.shape[1]), F32, kind="ExternalOutput").ap())
    build(nc, *args, N, E)
    r = _run(nc, [{f"in_{k}": a for k, a in arrays.items()}], core_ids=[0])
    return r.results[0]["out_0"]


PAD_NODE = 1 << 20
_WEIGHTS = ["L0_gnn_W", "L0_gnn_att_src", "L0_gnn_att_dst", "L0_gnn_bias", "L0_gnn_ln_gamma", "L0_gnn_ln_beta",
            "L0_ffn_Wr", "L0_ffn_br", "L0_ffn_W1", "L0_ffn_b1", "L0_ffn_W2", "L0_ffn_b2", "L0_ffn_gamma",
            "L0_ffn_beta"]
```

```python
from contextlib import ExitStack
import math

import concourse.bass as bass
from concourse import mybir

F32 = mybir.dt.float32
BF16 = mybir.dt.bfloat16
I32 = mybir.dt.int32
U32 = mybir.dt.uint32
ALU = mybir.AluOpType
ACT = mybir.ActivationFunctionType
X = mybir.AxisListType.X

P = 128
TILES = 14
CUTS = (7, 11)
ACT_TILES = 4
CHUNK = TILES * P
ROWS_RING = 4
NEG_SLOPE, LN_EPS, DEN_EPS = 0.2, 1e-5, 1e-16
ROOT_SEED = 1597463007.0
BIG = 1e30
CAPACITY_FACTOR = 1.25
GROUP = 512


def sizes(N, E):
    chunks = -(-E // CHUNK)
    steps = chunks + N // P + 1 + 1
    steps += 1 - steps % 2
    blocks = -(-(N + 3 * P) // P)
    blocks = -(-blocks // ROWS_RING) * ROWS_RING
    groups = -(-N // GROUP)
    return chunks, steps, blocks, groups


class At:

    def __init__(self, k, mul, off):
        self.k, self.mul, self.off = k, mul, off

    def number(self, lead=0):
        return self.k * self.mul + (self.off + lead)

    def slot(self, lead=0):
        return (self.off + lead) % self.mul

    def landed(self, dmas, lead=0):
        return self.k * (16 * dmas) + 16 * dmas * ((self.off + lead) // self.mul + 1)


class Ticks:

    def __init__(self, sem, names, back):
        self.sem, self.names, self.back, self.at = sem, names.split(), back, 0
        assert len(set(self.names)) == len(self.names)

    def mark(self, name, ins):
        assert self.names[self.at % len(self.names)] == name, (name, self.names[self.at % len(self.names)])
        self.at += 1
        ins.then_inc(self.sem, 1)

    def value(self, name, at, lead=0):
        n = len(self.names)
        return at.k * (n * at.mul) + ((at.off + lead + self.back) * n + self.names.index(name) + 1)

    def wait(self, eng, name, at, lead=0):
        eng.wait_ge(self.sem, self.value(name, at, lead))

    def skip(self, eng, names, at):
        i = self.names.index(names[0])
        assert self.names[i:i + len(names)] == list(names) and self.at % len(self.names) == i
        eng.wait_ge(self.sem, self.value(names[0], at) - 1)
        eng.sem_inc(self.sem, len(names))
        self.at += len(names)

    def credit(self, eng, ahead=()):
        full = self.back - bool(ahead)
        self.at = self.names.index(ahead[0]) if ahead else 0
        eng.sem_inc(self.sem, len(self.names) * full + self.at)

    def rest(self, eng, ahead, then=None):
        n, a = self.names.index(then[0]) if then else len(self.names), self.at
        assert self.names[a - len(ahead):a] == list(ahead)
        if a < n:
            eng.wait_ge(self.sem, len(self.names) * (self.back - 1) + a)
            eng.sem_inc(self.sem, n - a)
        self.at = n if then else 0


def build(nc, x, src_t, dst, W, att_src, att_dst, g_bias, g_gamma, g_beta, Wr, br, W1, b1, W2, b2,
          f_gamma, f_beta, out, N, E):
    D = x.shape[1]
    H, C = att_src.shape
    NE, _, F = W1.shape
    KD, KF = D // P, F // P
    chunks, STEPS, BLOCKS, GROUPS = sizes(N, E)
    HC1 = H * (C + 1)
    ONE, AS, AD = HC1, HC1 + 1, HC1 + 1 + H
    TW = AD + H
    R5 = 1 + H
    SR = R5 * TILES
    SHIFT, HAS = HC1, HC1 + H
    AW = HAS + 1
    SCHED = 256
    assert STEPS + 3 <= SCHED and SR <= P and D == H * C
    QB = GROUP // P
    XO_ROWS = (GROUPS + 1) * GROUP

    with ExitStack() as ctx:
        def sb(name, shape, dt=F32):
            return ctx.enter_context(nc.sbuf_tensor(name, shape, dt))

        def sem(name):
            return ctx.enter_context(nc.semaphore(name))

        bank = [ctx.enter_context(nc.psum_tensor(f"bank{i}", [P, 512], F32)) for i in range(8)]
        table = nc.dram_tensor("table", [BLOCKS * P, TW], F32, kind="Internal").ap()
        x_mid = nc.dram_tensor("x_mid", [XO_ROWS, D], F32, kind="Internal").ap()
        sched = nc.dram_tensor("sched", [2, SCHED], I32, kind="Internal").ap()

        ident = sb("ident", [P, P])
        ident_b = sb("ident_b", [P, P], BF16)
        iota_col = sb("iota_col", [P, 1])
        ones = sb("ones", [P, P])
        eps = sb("eps", [P, 1])
        zeros = sb("zeros", [P, D])
        g_aff = sb("g_aff", [P, 3, D])
        f_aff = sb("f_aff", [P, 2, D])

        wx = sb("wx", [P, KD, D + 2 * H])
        att = sb("att", [P, 2, D])
        att_tmp = sb("att_tmp", [P, D])
        x_in = sb("x_in", [P, ROWS_RING, D])
        xT = sb("xT", [P, 2, KD, P])
        st1 = sb("st1", [P, ROWS_RING, 6])
        mv1 = sb("mv1", [P, ROWS_RING, 2])
        y1 = sb("y1", [P, ROWS_RING, 2])
        row_out = sb("row_out", [P, ROWS_RING, TW])

        first = sb("first", [1, 257], I32)
        gap = sb("gap", [1, 256], I32)
        lows = sb("lows", [1, 3, 256])
        s_both = sb("s_both", [P, 2, 256])
        s_cmp = sb("s_cmp", [P, 2, 256])
        s_col = sb("s_col", [P, 2, 4])
        s_out_i = sb("s_out_i", [P, 2, 2], I32)
        step_tab = sb("step_tab", [P, 2, SCHED], I32)
        w_tab = sb("w_tab", [P, SCHED])
        tot_i = sb("tot_i", [1, 2], I32)

        idx = [sb(f"idx{i}", [P, TILES], I32) for i in range(2)]
        dst_s = sb("dst_s", [SR, 2, P], I32)
        dst_b = sb("dst_b", [P, 2, CHUNK], I32)
        tab_w = sb("tab_w", [P, 2, TW])
        x_w = sb("x_w", [P, 2, D])
        rows = sb("rows", [P, 2, TILES, TW])
        msg = sb("msg", [P, 2, TILES, HC1])
        oh = sb("oh", [P, 2, TILES, P])
        oh_b = sb("oh_b", [P, 2, TILES, P], BF16)
        ohT = sb("ohT", [P, 2, TILES, P], BF16)
        wcur = sb("wcur", [P, 2, 2])
        node = sb("node", [P, 2])
        sel = sb("sel", [P, 2])
        mask = sb("mask", [P, 2])
        newseg = sb("newseg", [SR, 2, P + 1])
        pen = sb("pen", [SR, 2, P])
        asrc = sb("asrc", [P, SR])
        runmax = sb("runmax", [SR, P])
        lastmax = sb("lastmax", [SR, P])
        last_p = sb("last_p", [P, TILES, 3, R5], BF16)
        last_r = sb("last_r", [P, TILES, R5])
        node_v = sb("node_v", [P, TILES, R5])
        nohas = sb("nohas", [P, TILES])
        mtile = sb("mtile", [P, TILES, H])
        mnode = sb("mnode", [P, H])
        zn = sb("zn", [P, H])
        adsh = sb("adsh", [P, 2, 2 * H])
        adsh_p = sb("adsh_p", [P, 3, 2 * H], BF16)
        adsh_r = sb("adsh_r", [P, 2 * H])
        edge_v = sb("edge_v", [P, TILES, 2 * H])
        ze = sb("ze", [P, TILES, H])
        le = sb("le", [P, TILES, H])
        we = sb("we", [P, 2, TILES, H])
        acc = sb("acc", [P, AW])
        carry = sb("carry", [1, AW])
        r_t = sb("r_t", [1, 1])
        r_m = sb("r_m", [1, 2, H])
        r_d = sb("r_d", [1, 2 * H])
        r_f = sb("r_f", [1, 2 * H])
        r_c = sb("r_c", [1, HC1])
        zs = sb("zs", [P, H])
        ws = sb("ws", [P, H])
        num = sb("num", [P, HC1])
        rden = sb("rden", [P, H])
        o = sb("o", [P, D])
        st2 = sb("st2", [P, 6])
        mv2 = sb("mv2", [P, 2])
        ln2 = sb("ln2", [P, 4])
        m_lhs = sb("m_lhs", [P, 2])
        x_o = sb("x_o", [P, 2, D + 2])

        zrow = sb("zrow", [1, D + 1])
        zcol = sb("zcol", [P, KD])
        wr_sb = sb("wr_sb", [P, KD, NE])
        rt = sb("rt", [1, 16, NE])
        top_i = sb("top_i", [1, NE], U32)
        top_ii = sb("top_ii", [1, NE], I32)
        wtop = sb("wtop", [P, 2])
        w1_sb = sb("w1_sb", [P, 2, KD, F])
        w2_sb = sb("w2_sb", [P, 2, KF, D])
        b1_sb = sb("b1_sb", [P, 2, KF])
        b2_sb = sb("b2_sb", [P, 2, D])
        b2_w = sb("b2_w", [P, D])
        fx = sb("fx", [P, 3, QB, D])
        fst = sb("fst", [P, QB, 6])
        fmv = sb("fmv", [P, QB, 2])
        ft = sb("ft", [P, QB])
        fv = sb("fv", [P, QB])
        fh = sb("fh", [P, QB])
        fq = sb("fq", [P, QB])
        fxn = msg[:, :, :, :].rearrange("p a t c -> p (a t c)")[:, 0:2 * QB * D]\
            .rearrange("p (a q d) -> p a q d", a=2, q=QB)
        fxT = oh[:, :, :, :].rearrange("p a t c -> p (a t c)")[:, 0:2 * KD * GROUP]\
            .rearrange("p (a k n) -> p a k n", a=2, k=KD)
        hT = rows[:, :, :, :].rearrange("p a t c -> p (a t c)")[:, 0:2 * KF * GROUP]\
            .rearrange("p (f n) -> p f n", f=2 * KF)
        fo = sb("fo", [P, 2, QB, D])

        s_w = sem("s_w")
        s_x = [sem(f"s_x{i}") for i in range(ROWS_RING)]
        s_tab = [sem(f"s_tab{i}") for i in range(ROWS_RING)]
        s_pad = sem("s_pad")
        s_sched = sem("s_sched")
        s_idx = [sem(f"s_idx{i}") for i in range(2)]
        s_dst = [sem(f"s_dst{i}") for i in range(2)]
        s_rows = [sem(f"s_rows{i}") for i in range(2)]
        s_win = [sem(f"s_win{i}") for i in range(2)]
        s_mid = sem("s_mid")
        s_fwr = sem("s_fwr")
        s_fw = sem("s_fw")
        s_fx = [sem(f"s_fx{i}") for i in range(3)]
        s_out = sem("s_out")
        s_const = sem("s_const")
        s_pool = sem("s_pool")
        s_setup = sem("s_setup")
        s_once = sem("s_once")
        s_exp = sem("s_exp")
        s_walked = sem("s_walked")
        s_granted = sem("s_granted")
        s_dve_held = sem("s_dve_held")
        s_sp_held = sem("s_sp_held")

        p1_pe = Ticks(sem("p1_pe"), "xT rows", 4)
        p1_dve = Ticks(sem("p1_dve"), "stats mv xT", 4)
        p1_act = Ticks(sem("p1_act"), "ln rstd rows logits", 4)
        MSGS = [f"msg{i}" for i in range((TILES - ACT_TILES) // 2)]
        dve2 = Ticks(sem("dve2"), """
            wcur* r_t newseg* r_sc node* r_mn pen* r_d1 r_d RUNMAX self_z LASTMAX self_l ohT0*
            LAST_HI SEL LAST_R LAST_MID MASK LAST_LO ohT*
            NODE_V accshift NOHAS merged0 MTILE merged1 MNODE merged2 AD MAXSELF merged3 ZN mergedshift SHIFT self_d
            HI REST MID LO num0 num1 num2 num3 EDGE_V den ZE rden LE biased0 biased1 D biased2 DMIN biased3
            st msg0 mv msg1 gam msg2 normed msg3 xmid """ + " ".join(MSGS[4:]) + " st_m mv_m", 3)
        act2 = Ticks(sem("act2"), "asrc oh ln2 y2 lhs rexp carried acc wself oh_b* we carry msgs0 ln1 y1 msgs", 3)
        pe2 = Ticks(sem("pe2"), "agg0 lT agg1 lastT agg nodemax router turned* expand carry", 3)
        sp2 = Ticks(sem("sp2"), "stored", 3)
        ROOT = "v vh seed sq0 t0 r0 sq1 t1 r1 sq2 t2 rstd".split()
        DVE3_A = ["st", "mv"] + ROOT + ["xn", "xT"]
        ROOT2 = [n + "'" for n in ROOT]
        HID = [f"h{i}" for i in range(2 * KF)]
        dve3 = Ticks(sem("dve3"), " ".join(DVE3_A) + " res b2 st2 mv2 " + " ".join(ROOT2) + " gam normed out", 2)
        act3 = Ticks(sem("act3"), " ".join(HID), 2)
        pe3 = Ticks(sem("pe3"), " ".join(HID) + " half xT out", 2)
        sp3 = Ticks(sem("sp3"), "stored", 3)

        psX = [bank[i][:, 0:KD * P].rearrange("p (k n) -> p k n", k=KD) for i in (0, 1)]
        psH = [bank[i][:, 0:D + 2 * H] for i in (2, 3)]
        psW = bank[4][:, 0:D + 2 * H]
        psS = bank[5]
        psT, psR, psM = bank[0][0:SR, 0:P], bank[0][:, P:P + SR], bank[0][:, P + SR:P + 4 * SR]
        psO = [bank[i][:, :].bitcast(BF16)[:, 0:TILES // 2 * P] for i in (1, 2)]
        psE = bank[3][:, 0:3 * 2 * H * TILES]
        psA = [bank[i][:, 0:HC1] for i in (4, 5)]
        psC, psZ = bank[6][0:1, 0:AW], bank[7][0:1, 0:D + 1]
        psF = [bank[i][:, :] for i in (0, 1)]
        psU = [bank[i][:, :] for i in (2, 3, 4, 5)]
        psY = [bank[i][:, :].rearrange("p (q d) -> p q d", d=D) for i in (6, 7)]

        N_ATT = 1 + 4 * KD
        N_WX = N_ATT + KD
        N_LOWS = N_WX + 9
        N_SETUP = N_LOWS + 1 + 2 * 9
        N_WALKED = N_SETUP + 2 + 1
        N_MEAN = N_WALKED + 2
        N_EXP = [N_MEAN + 4, N_MEAN + 13, N_MEAN + 20]
        N_TOP = N_EXP[2] + 3
        N_EXPERT = N_TOP + 5
        WTOP = 9

        block = ctx.enter_context(nc.Block())

        def row(v):
            return v.rearrange("(a d) -> a d", a=1)

        def head_cols(ap):
            return ap.rearrange("p (h c) -> p h c", h=H)

        def over(ap, n):
            return ap.unsqueeze(len(ap.shape)).to_broadcast([*ap.shape, n])

        def hold(eng, counted):
            eng.sem_inc(counted, 1)

        def walk(eng, total, step):
            step(At(0, 2, 0), False)
            with eng.Fori(0, (STEPS - 1) // 2) as k:
                with eng.If(k * 2 + 1 < total):
                    for j in (1, 2):
                        step(At(k, 2, j), True)

        def steps_to_run(eng):
            eng.wait_ge(s_sched, 64)
            return eng.value_load(tot_i[0:1, 0:1], min_val=2, max_val=STEPS)

        @block.sync
        def _(sp):
            sp.dma_start(wx[:, :, 0:D], W.rearrange("(k p) n -> p k n", p=P)).then_inc(s_w, 16)
            for i, v in enumerate((att_src, att_dst)):
                sp.dma_start(att[:, i, :], v.rearrange("(a h) c -> a (h c)", a=1).to_broadcast([P, D])).then_inc(s_w, 16)
            for b in range(3):
                sp.dma_start(x_in[:, b, :], x[b * P:(b + 1) * P, :]).then_inc(s_x[b], 16)
            for i, v in enumerate((g_bias, g_gamma, g_beta)):
                sp.dma_start(g_aff[:, i, :], row(v).to_broadcast([P, D])).then_inc(s_w, 16)
            sp.wait_ge(s_setup, 1)
            sp.dma_start(first[:, 0:chunks],
                         dst[0:chunks * CHUNK].rearrange("(a c e) -> a c e", a=1, e=CHUNK)[:, :, 0],
                         allow_slow_non_contiguous=True).then_inc(s_sched, 16)
            sp.wait_ge(s_const, 6)
            pads = [(r, min(P, XO_ROWS - r)) for r in range(N, XO_ROWS, P)]
            for i, (r, n) in enumerate(pads):
                sp.dma_start(x_mid[r:r + n, :], zeros[0:n, :]).then_inc(s_tab[i] if i < ROWS_RING else s_pad, 16)
            with sp.Fori(0, BLOCKS // ROWS_RING) as k:
                for j in range(ROWS_RING):
                    at = At(k, ROWS_RING, j)
                    p1_dve.wait(sp, "stats", at, -1)
                    hold(sp, s_sp_held)
                    p1_pe.wait(sp, "xT", at, -2)
                    hold(sp, s_sp_held)
                    sp.dma_start(x_in[:, at.slot(3), :], x[bass.ds(at.number(3) * P, P), :])\
                      .then_inc(s_x[at.slot(3)], 16)
                    p1_act.wait(sp, "logits", at)
                    hold(sp, s_sp_held)
                    sp.dma_start(table[bass.ds(at.number() * P, P), :], row_out[:, j, :]).then_inc(s_tab[j], 16)
            for j in range(ROWS_RING):
                sp.wait_ge(s_tab[j], 16 * (BLOCKS // ROWS_RING + 1))
                sp.wait_ge(s_x[j], 16 * (BLOCKS // ROWS_RING + (j < 3)))
            sp.wait_ge(s_pad, 16 * (len(pads) - ROWS_RING))
            sp.wait_ge(s_setup, N_SETUP)
            for i in range(2):
                sp.dma_start(sched[i, :].rearrange("(b p) -> p b", p=P), s_out_i[:, i, :],
                             allow_slow_non_contiguous=True).then_inc(s_sched, 16)
            sp.wait_ge(s_sched, 48)
            sp.dma_start(step_tab[:, :, :].rearrange("p a s -> p (a s)"),
                         sched.rearrange("(o a) s -> o (a s)", o=1).to_broadcast([P, 2 * SCHED])).then_inc(s_sched, 16)
            total = steps_to_run(sp)

            def load_edges(at, lead):
                slot = at.slot(lead)
                c = sp.value_load(step_tab[0:1, 1, bass.ds(at.number(lead), 1)], min_val=0, max_val=chunks - 1)
                sp.dma_start(idx[slot][:, :], src_t[bass.ds(c * P, P), :]).then_inc(s_idx[slot], 16)
                sp.dma_start(dst_s[:, slot, :], dst.rearrange("(t o e) -> t o e", o=1, e=P)
                             [bass.ds(c * TILES, TILES), :, :].to_broadcast([TILES, R5, P])).then_inc(s_dst[slot], 16)
                sp.dma_start(dst_b[:, slot, :], dst.rearrange("(a e) -> a e", e=CHUNK)
                             [bass.ds(c, 1), :].to_broadcast([P, CHUNK])).then_inc(s_dst[slot], 16)

            def load_window(at, lead):
                slot = at.slot(lead)
                w = sp.value_load(step_tab[0:1, 0, bass.ds(at.number(lead), 1)], min_val=0, max_val=N)
                sp.dma_start(tab_w[:, slot, :], table[bass.ds(w, P), :]).then_inc(s_win[slot], 16)
                sp.dma_start(x_w[:, slot, :], x[bass.ds(w, P), :]).then_inc(s_win[slot], 16)

            def step(at, follows):
                sp.wait_ge(s_rows[at.slot()], at.landed(TILES))
                hold(sp, s_sp_held)
                dve2.wait(sp, "ohT*", at, -1)
                hold(sp, s_sp_held)
                load_edges(at, 2)
                if not follows:
                    load_window(at, 1)
                    sp2.skip(sp, ["stored"], at)
                    return
                dve2.wait(sp, "xmid", at)
                hold(sp, s_sp_held)
                w = sp.value_load(step_tab[0:1, 0, bass.ds(at.number(-1), 1)], min_val=0, max_val=N)
                sp.dma_start(x_mid[bass.ds(w, P), :], x_o[:, at.slot(-1), 0:D]).then_inc(s_mid, 16)
                load_window(at, 1)
                sp.wait_ge(s_mid, at.k * (16 * at.mul) + 16 * at.off)
                hold(sp, s_sp_held)
                sp2.skip(sp, ["stored"], at)

            sp2.credit(sp)
            load_edges(At(0, 2, 0), 0)
            load_edges(At(0, 2, 0), 1)
            load_window(At(0, 2, 0), 0)
            walk(sp, total, step)
            for slot in range(2):
                edges, windows = (total + (3 - slot)) // 2, (total + (2 - slot)) // 2
                for s, n in ((s_idx, edges * 16), (s_dst, edges * 32), (s_win, windows * 32)):
                    sp.wait_ge(s[slot], n)
                    hold(sp, s_sp_held)

            sp.dma_start(wr_sb[:, :, :], Wr.rearrange("(k p) e -> p k e", p=P)).then_inc(s_fwr, 16)
            sp.dma_start(rt[:, 0, :], row(br)).then_inc(s_fwr, 16)
            for i, v in enumerate((f_gamma, f_beta)):
                sp.dma_start(f_aff[:, i, :], row(v).to_broadcast([P, D])).then_inc(s_fwr, 16)

            def load_group(at, lead):
                sp.dma_start(fx[:, at.slot(lead), :, :],
                             x_mid[bass.ds(at.number(lead) * GROUP, GROUP), :].rearrange("(q p) d -> p q d", p=P))\
                  .then_inc(s_fx[at.slot(lead)], 16)

            load_group(At(0, 3, 0), 0)
            load_group(At(0, 3, 0), 1)
            sp.wait_ge(s_setup, N_TOP)
            for i in range(2):
                e = sp.value_load(top_ii[0:1, i:i + 1], min_val=0, max_val=NE - 1)
                sp.dma_start(w1_sb[:, i, :, :],
                             W1[bass.ds(e, 1), :, :].rearrange("o (k p) f -> p (o k) f", p=P)).then_inc(s_fw, 16)
                sp.dma_start(w2_sb[:, i, :, :],
                             W2[bass.ds(e, 1), :, :].rearrange("o (k p) f -> p (o k) f", p=P)).then_inc(s_fw, 16)
                sp.dma_start(b1_sb[:, i, :], b1[bass.ds(e, 1), :].rearrange("o (k p) -> p (o k)", p=P),
                             allow_slow_non_contiguous=True).then_inc(s_fw, 16)
                sp.dma_start(b2_sb[:, i, :], b2[bass.ds(e, 1), :].to_broadcast([P, D])).then_inc(s_fw, 16)
            sp3.credit(sp)
            with sp.Fori(0, (GROUPS - 1) // 6) as k:
                for j in range(6):
                    at3, at2 = At(k * 2, 3, j), At(k * 3, 2, j)
                    dve3.wait(sp, "out", at2, -1)
                    hold(sp, s_sp_held)
                    load_group(at3, 2)
                    dve3.wait(sp, "out", at2)
                    hold(sp, s_sp_held)
                    sp.dma_start(out[bass.ds(at2.number() * GROUP, GROUP), :].rearrange("(q p) d -> p q d", p=P),
                                 fo[:, at2.slot(), :, :]).then_inc(s_out, 16)
                    sp.wait_ge(s_out, at2.k * 32 + 16 * (j + 1))
                    hold(sp, s_sp_held)
                    sp3.skip(sp, ["stored"], at2)
            last = At(0, 2, GROUPS - 1)
            dve3.wait(sp, "out", last)
            hold(sp, s_sp_held)
            tail = [(r, min(P, N - r)) for r in range((GROUPS - 1) * GROUP, N, P)]
            for q, (r, n) in enumerate(tail):
                sp.dma_start(out[r:r + n, :], fo[0:n, last.slot(), q, :]).then_inc(s_out, 16)
            sp.wait_ge(s_out, 16 * (GROUPS - 1 + len(tail)))
            for j in range(3):
                sp.wait_ge(s_fx[j], 16 * len([g for g in range(GROUPS + 1) if g % 3 == j]))

        @block.gpsimd
        def _(pool):
            pool.iota(iota_col[:, :], [[0, 1]], base=0, channel_multiplier=1,
                      allow_small_or_imprecise_dtypes=True).then_inc(s_const, 1)
            pool.memset(ones[:, :], 1.0).then_inc(s_const, 1)
            pool.memset(eps[:, :], LN_EPS).then_inc(s_const, 1)
            pool.memset(zeros[:, :], 0.0).then_inc(s_const, 1)
            pool.memset(ident[:, :], 0.0).then_inc(s_const, 1)
            pool.wait_ge(s_const, 5)
            pool.affine_select(out=ident[:, :], in_=ident[:, :], compare_op=ALU.not_equal, fill=1.0, base=0,
                               pattern=[[-1, P]], channel_multiplier=1).then_inc(s_const, 1)
            pool.memset(row_out[:, :, :], 1.0).then_inc(s_pool, 1)
            pool.memset(newseg[:, :, :], 1.0).then_inc(s_pool, 1)
            pool.memset(acc[:, :], 1.0).then_inc(s_pool, 1)
            pool.memset(carry[:, :], 0.0).then_inc(s_pool, 1)
            pool.memset(mask[:, :], 0.0).then_inc(s_pool, 1)
            pool.memset(x_o[:, :, :], 0.0).then_inc(s_pool, 1)
            for j in range(ROWS_RING):
                pool.wait_ge(s_tab[j], 16 * (BLOCKS // ROWS_RING + 1))
            total = steps_to_run(pool)
            bound = pool.to_reg(BLOCKS * P - 1)

            def gather(at, follows):
                slot = at.slot()
                pool.wait_ge(s_idx[slot], at.landed(1))
                act2.wait(pool, "asrc", at, -2)
                for t in range(TILES):
                    if t % 2 == 0 and t // 2 < len(MSGS):
                        dve2.wait(pool, MSGS[t // 2], at, -2)
                        hold(pool, s_granted)
                    elif t == 2 * len(MSGS):
                        act2.wait(pool, "msgs", at, -2)
                        hold(pool, s_granted)
                    pool.indirect_dma_start(rows[:, slot, t, :], None, table,
                                            bass.IndirectOffsetOnAxis(ap=idx[slot][:, t:t + 1], axis=0),
                                            bounds_check=bound, oob_is_err=False).then_inc(s_rows[slot], 16)

            walk(pool, total, gather)

        @block.tensor
        def _(pe):
            pe.wait_ge(s_setup, N_ATT)
            for k in range(KD):
                mm = pe.matmul(psW, ones[:, :], wx[:, k, :], start=(k == 0), stop=(k == KD - 1))
            mm.then_inc(s_once, 1)
            p1_pe.credit(pe, ahead=["xT"])

            def transpose_x(at, lead):
                pe.wait_ge(s_x[at.slot(lead)], at.landed(1, lead))
                p1_dve.wait(pe, "xT", at, lead - 2)
                for k in range(KD):
                    mm = pe.transpose(psX[(at.off + lead) % 2][:, k, :], x_in[:, at.slot(lead), k * P:(k + 1) * P],
                                      ident[:, :])
                p1_pe.mark("xT", mm)

            transpose_x(At(0, ROWS_RING, 0), 0)
            p1_pe.rest(pe, ["xT"])
            pe.wait_ge(s_setup, N_WX)
            with pe.Fori(0, BLOCKS // ROWS_RING) as k:
                for j in range(ROWS_RING):
                    at = At(k, ROWS_RING, j)
                    transpose_x(at, 1)
                    p1_dve.wait(pe, "xT", at)
                    p1_act.wait(pe, "logits", at, -2)
                    for kk in range(KD):
                        mm = pe.matmul(psH[j % 2], xT[:, j % 2, kk, :], wx[:, kk, :], start=(kk == 0),
                                       stop=(kk == KD - 1))
                    p1_pe.mark("rows", mm)
            pe.wait_ge(s_setup, N_LOWS)
            pe.matmul(psS[:, 0:256], ones[0:1, :], lows[0:1, 1, :], start=True, stop=True)
            pe.matmul(psS[:, 256:512], ones[0:1, :], lows[0:1, 2, :], start=True, stop=True).then_inc(s_once, 1)
            pe.matmul(bank[7][0:1, 0:D], zeros[:, 0:1], zeros[:, :], start=True, stop=False, skip_group_check=True)
            pe.matmul(bank[7][0:1, D:D + 1], zeros[:, 0:1], zeros[:, 0:1], start=False, stop=False,
                      skip_group_check=True)
            pe2.credit(pe, ahead=["turned*"])
            p1_end = At(BLOCKS // ROWS_RING - 1, ROWS_RING, ROWS_RING - 1)
            p1_act.wait(pe, "logits", p1_end)
            total = steps_to_run(pe)

            def turn_one_hots(at, lead):
                dve2.wait(pe, "ohT*", at, lead - 1)
                act2.wait(pe, "oh", at, lead - 1)
                for t in range(TILES):
                    ps, c = psO[2 * t // TILES], t % (TILES // 2) * P
                    mm = pe.transpose(ps[:, c:c + P], ohT[:, at.slot(lead), t, :], ident_b[:, :])
                pe2.mark("turned*", mm)

            turn_one_hots(At(0, 2, 0), 0)
            pe2.rest(pe, ["turned*"])

            def step(at, follows):
                s, q = at.slot(), at.slot(-1)
                def sums(tiles, name):
                    if not follows:
                        pe2.skip(pe, [name], at)
                        return
                    for t in tiles:
                        if t == 0:
                            act2.wait(pe, "acc", at, -1)
                            act2.wait(pe, "oh", at, -1)
                        if t == TILES - ACT_TILES:
                            act2.wait(pe, "msgs0", at, -1)
                        elif t == TILES - ACT_TILES // 2:
                            act2.wait(pe, "msgs", at, -1)
                        elif t % 2 == 0 and t // 2 < len(MSGS):
                            dve2.wait(pe, MSGS[t // 2], at, -1)
                        mm = pe.matmul(psA[q], oh[:, q, t, :], msg[:, q, t, :], start=(t == 0), stop=(t == TILES - 1))
                    pe2.mark(name, mm)

                sums(range(0, CUTS[0]), "agg0")
                act2.wait(pe, "asrc", at)
                dve2.wait(pe, "NODE_V", at, -1)
                pe2.mark("lT", pe.matmul(psT, asrc[:, :], ident[:, :], start=True, stop=True))
                sums(range(CUTS[0], CUTS[1]), "agg1")
                dve2.wait(pe, "LASTMAX", at)
                pe2.mark("lastT", pe.matmul(psR, lastmax[:, :], ident[0:SR, 0:SR], start=True, stop=True))
                sums(range(CUTS[1], TILES), "agg")
                dve2.wait(pe, "LAST_LO", at)
                act2.wait(pe, "oh_b*", at, -1)
                for t in range(TILES):
                    mm = pe.matmul(psM[:, t * 3 * R5:(t + 1) * 3 * R5], oh_b[:, s, t, :],
                                   last_p[:, t, :, :].rearrange("p a r -> p (a r)"), start=True, stop=True)
                pe2.mark("nodemax", mm)
                if follows:
                    act2.wait(pe, "lhs", at)
                    dve2.wait(pe, "mv_m", at, -1)
                    pe2.mark("router", pe.matmul(psZ, m_lhs[:, s:s + 1], x_o[:, s, 0:D + 1], start=False, stop=False,
                                                 skip_group_check=True))
                else:
                    pe2.skip(pe, ["router"], at)
                turn_one_hots(at, 1)
                dve2.wait(pe, "LO", at)
                dve2.wait(pe, "EDGE_V", at, -1)
                for t in range(TILES):
                    mm = pe.matmul(psE[:, t * 6 * H:(t + 1) * 6 * H], ohT[:, s, t, :],
                                   adsh_p[:, :, :].rearrange("p a r -> p (a r)"), start=True, stop=True)
                pe2.mark("expand", mm)
                if follows:
                    dve2.wait(pe, "mergedshift", at)
                    act2.wait(pe, "carry", at, -1)
                    pe2.mark("carry", pe.matmul(psC, sel[:, q:q + 1], acc[:, :], start=True, stop=True))
                else:
                    pe2.skip(pe, ["carry"], at)

            walk(pe, total, step)
            pe.wait_ge(s_setup, N_WALKED)
            pe.wait_ge(s_walked, 3)
            pe.matmul(psZ, m_lhs[:, 1:2], x_o[:, 1, 0:D + 1], start=False, stop=False, skip_group_check=True)
            pe.drain().then_inc(s_once, 1)
            pe.wait_ge(s_setup, N_MEAN)
            for k in range(KD):
                mm = pe.matmul(bank[0][:, k:k + 1], zrow[0:1, k * P:(k + 1) * P], ones[0:1, 0:1], start=True, stop=True)
            mm.then_inc(s_once, 1)
            pe.wait_ge(s_setup, N_MEAN + 1)
            pe.wait_ge(s_fwr, 64)
            for k in range(KD):
                mm = pe.matmul(bank[1][0:1, 0:NE], zcol[:, k:k + 1], wr_sb[:, k, :], start=(k == 0), stop=(k == KD - 1))
            mm.then_inc(s_once, 1)
            pe.wait_ge(s_setup, N_TOP)
            pe.matmul(bank[2][:, 0:2], ones[0:1, :], rt[0:1, WTOP, 0:2], start=True, stop=True).then_inc(s_once, 1)

            pe3.credit(pe, ahead=["xT"])

            def transpose_rows(at, lead):
                dve3.wait(pe, "xn", at, lead - 1)
                dve3.wait(pe, "xT", at, lead - 2)
                for k in range(KD):
                    for q in range(QB):
                        mm = pe.transpose(psF[k][:, q * P:(q + 1) * P],
                                          fxn[:, at.slot(lead), q, k * P:(k + 1) * P], ident[:, :])
                pe3.mark("xT", mm)

            def group(at):
                dve3.wait(pe, "xT", at, -1)
                for f in range(2 * KF):
                    e, fk = divmod(f, KF)
                    u = psU[f % len(psU)]
                    g = f - len(psU)
                    act3.wait(pe, HID[g], at, 0 if g >= 0 else -1)
                    for k in range(KD):
                        mm = pe.matmul(u, w1_sb[:, e, k, fk * P:(fk + 1) * P], fxT[:, at.slot(), k, :],
                                       start=(k == 0), stop=(k == KD - 1))
                    pe3.mark(HID[f], mm)
                dve3.wait(pe, "res", at, -1)
                for q in range(QB):
                    if q == QB // 2:
                        pe3.mark("half", mm)
                        transpose_rows(at, 1)
                    for f in range(2 * KF):
                        e, fk = divmod(f, KF)
                        if q == 0:
                            act3.wait(pe, HID[f], at)
                        mm = pe.matmul(psY[q // 2][:, q % 2, :], hT[:, f, q * P:(q + 1) * P], w2_sb[:, e, fk, :],
                                       start=(f == 0), stop=(f == 2 * KF - 1))
                pe3.mark("out", mm)

            pe.wait_ge(s_setup, N_EXPERT)
            transpose_rows(At(0, 2, 0), 0)
            pe3.rest(pe, ["xT"])
            with pe.Fori(0, (GROUPS - 1) // 2) as k:
                for j in range(2):
                    group(At(k, 2, j))
            group(At(0, 2, GROUPS - 1))

        @block.scalar
        def _(act):
            act.preload_act_table_set("natural_log_exp_and_others")
            p1_act.credit(act)
            act.wait_ge(s_const, 6)
            act.wait_ge(s_pool, 6)
            with act.Fori(0, BLOCKS // ROWS_RING) as k:
                for j in range(ROWS_RING):
                    at = At(k, ROWS_RING, j)
                    p1_dve.wait(act, "mv", at)
                    p1_mark = p1_act.mark
                    p1_mark("ln", act.activation(y1[:, j, 0:1], mv1[:, j, 1:2], ACT.Ln, bias=eps[:, 0:1]))
                    p1_act.wait(act, "ln", at)
                    p1_mark("rstd", act.activation(y1[:, j, 1:2], y1[:, j, 0:1], ACT.Exp, scale=-0.5))
                    p1_act.wait(act, "rstd", at)
                    p1_pe.wait(act, "rows", at)
                    act.wait_ge(s_tab[j], at.k * 16 + 16)
                    p1_mark("rows", act.activation(head_cols(row_out[:, j, 0:HC1])[:, :, 0:C],
                                                   head_cols(psH[j % 2][:, 0:D]), ACT.Copy, scale=y1[:, j, 1:2]))
                    p1_mark("logits", act.activation(row_out[:, j, AS:TW], psH[j % 2][:, D:D + 2 * H], ACT.Copy,
                                                     scale=y1[:, j, 1:2]))
            act2.credit(act, ahead=["oh_b*"])
            total = steps_to_run(act)

            def copy_one_hots(to, at, lead, name):
                half = TILES // 2
                for i in range(2):
                    ins = act.activation(to[:, at.slot(lead), i * half:(i + 1) * half, :],
                                         psO[i].rearrange("p (t n) -> p t n", n=P), ACT.Copy)
                act2.mark(name, ins)

            def one_hots_b(at, lead):
                pe2.wait(act, "turned*", at, lead - 1)
                copy_one_hots(oh_b, at, lead, "oh_b*")

            one_hots_b(At(0, 2, 0), 0)
            act2.rest(act, ["oh_b*"])

            def step(at, follows):
                s, q = at.slot(), at.slot(-1)

                def of_last(name, issue):
                    if follows:
                        act2.mark(name, issue())
                    else:
                        act2.skip(act, [name], at)

                def carried():
                    for h in range(H):
                        ins = act.activation(head_cols(r_c[:, :])[:, h, :], head_cols(carry[:, 0:HC1])[:, h, :],
                                             ACT.Copy, scale=r_f[:, h:h + 1])
                    return ins

                def root(c, var):
                    n = str(c // 2 + 1)
                    of_last("ln" + n, lambda: act.activation(ln2[:, c:c + 1], var, ACT.Ln, bias=eps[:, 0:1]))
                    act2.wait(act, "ln" + n, at)
                    of_last("y" + n, lambda: act.activation(ln2[:, c + 1:c + 2], ln2[:, c:c + 1], ACT.Exp, scale=-0.5))

                act.wait_ge(s_rows[s], at.landed(TILES))
                pe2.wait(act, "lT", at, -1)
                act2.mark("asrc", act.activation(asrc[:, :].rearrange("p (t r) -> p t r", r=R5),
                                                 rows[:, s, :, ONE:AD], ACT.Copy))
                pe2.wait(act, "agg", at, -1)
                copy_one_hots(oh, at, 0, "oh")
                dve2.wait(act, "mv_m", at, -1)
                root(2, x_o[:, s, D + 1:D + 2])
                act2.wait(act, "y2", at)
                pe2.wait(act, "router", at, -1)
                of_last("lhs", lambda: act.activation(m_lhs[:, s:s + 1], mask[:, s:s + 1], ACT.Copy, scale=ln2[:, 3:4]))
                dve2.wait(act, "r_d", at)
                of_last("rexp", lambda: act.activation(r_f[:, :], r_d[:, :], ACT.Exp))
                act2.wait(act, "rexp", at)
                act2.wait(act, "carry", at, -1)
                of_last("carried", carried)
                pe2.wait(act, "agg", at)
                dve2.wait(act, "num3", at, -1)
                pe2.wait(act, "carry", at, -1)
                of_last("acc", lambda: act.activation(acc[:, 0:HC1], psA[q], ACT.Copy))
                dve2.wait(act, "self_d", at)
                of_last("wself", lambda: act.activation(ws[:, :], zs[:, :], ACT.Exp))
                one_hots_b(at, 1)
                dve2.wait(act, "DMIN", at)
                act2.mark("we", act.activation(we[:, s, :, :], le[:, :, :], ACT.Exp))
                pe2.wait(act, "carry", at)
                of_last("carry", lambda: act.activation(carry[:, :], psC, ACT.Copy))
                act2.wait(act, "we", at)
                def messages(tiles, name):
                    for t in tiles:
                        for h in range(H):
                            ins = act.activation(head_cols(msg[:, s, t, :])[:, h, :],
                                                 head_cols(rows[:, s, t, 0:HC1])[:, h, :], ACT.Copy,
                                                 scale=we[:, s, t, h:h + 1])
                    act2.mark(name, ins)

                middle = TILES - ACT_TILES // 2
                messages(range(TILES - ACT_TILES, middle), "msgs0")
                dve2.wait(act, "mv", at)
                root(0, mv2[:, 1:2])
                messages(range(middle, TILES), "msgs")

            walk(act, total, step)

            act.wait_ge(s_setup, N_WALKED)
            act.activation(ln2[:, 2:3], x_o[:, 1, D + 1:D + 2], ACT.Ln, bias=eps[:, 0:1]).then_inc(s_walked, 1)
            act.wait_ge(s_walked, 1)
            act.activation(ln2[:, 3:4], ln2[:, 2:3], ACT.Exp, scale=-0.5).then_inc(s_walked, 1)
            act.wait_ge(s_walked, 2)
            act.activation(m_lhs[:, 1:2], mask[:, 1:2], ACT.Copy, scale=ln2[:, 3:4]).then_inc(s_walked, 1)
            for n in N_EXP:
                act.wait_ge(s_setup, n)
                act.activation(rt[:, 13, :], rt[:, 14, :], ACT.Exp).then_inc(s_exp, 1)

            act3.credit(act)

            def group(at):
                for f in range(2 * KF):
                    e, fk = divmod(f, KF)
                    pe3.wait(act, HID[f], at)
                    if f == 0:
                        pe3.wait(act, "out", at, -1)
                    act3.mark(HID[f], act.activation(hT[:, f, :], psU[f % len(psU)], ACT.Gelu,
                                                     bias=b1_sb[:, e, fk:fk + 1]))

            act.wait_ge(s_fw, 128)
            with act.Fori(0, (GROUPS - 1) // 2) as k:
                for j in range(2):
                    group(At(k, 2, j))
            group(At(0, 2, GROUPS - 1))

        @block.vector
        def _(dve):
            done = [0]

            def link(ins):
                done[0] += 1
                ins.then_inc(s_setup, 1)
                dve.wait_ge(s_setup, done[0])

            link(dve.memset(first[:, :], N))
            dve.wait_ge(s_w, 96)
            dve.wait_ge(s_const, 6)
            for k in range(KD):
                for i in range(2):
                    link(dve.tensor_tensor(att_tmp[:, :], wx[:, k, 0:D], att[:, i, :], ALU.mult))
                    link(dve.tensor_reduce(wx[:, k, D + i * H:D + (i + 1) * H], head_cols(att_tmp[:, :]), X, ALU.add))
            assert done[0] == N_ATT
            dve.wait_ge(s_once, 1)
            for k in range(KD):
                link(dve.scalar_tensor_tensor(out=wx[:, k, :], in0=psW, scalar=-1.0 / D, in1=wx[:, k, :],
                                              op0=ALU.mult, op1=ALU.add))
            assert done[0] == N_WX
            p1_dve.credit(dve)
            with dve.Fori(0, BLOCKS // ROWS_RING) as k:
                for j in range(ROWS_RING):
                    at = At(k, ROWS_RING, j)
                    dve.wait_ge(s_x[j], at.landed(1))
                    p1_dve.mark("stats", dve.bn_stats(st1[:, j, :], x_in[:, j, :]))
                    p1_dve.wait(dve, "stats", at)
                    p1_act.wait(dve, "ln", at, -4)
                    hold(dve, s_dve_held)
                    p1_dve.mark("mv", dve.bn_aggr(mv1[:, j, :], st1[:, j, :]))
                    p1_pe.wait(dve, "xT", at, -1)
                    p1_pe.wait(dve, "rows", at, -2)
                    p1_dve.mark("xT", dve.tensor_copy(xT[:, j % 2, :, :], psX[j % 2]))
            dve.wait_ge(s_sched, 16)
            link(dve.memset(first[:, 0:1], 0))
            link(dve.tensor_tensor(gap[:, :], first[:, 1:257], first[:, 0:256], ALU.subtract))
            link(dve.tensor_scalar(gap[:, :], gap[:, :], 7, None, ALU.arith_shift_right))
            link(dve.tensor_scalar(lows[:, 0, :], gap[:, :], 1.0, None, ALU.add))
            link(dve.memset(lows[:, 1, 0:1], 0.0))
            link(dve.tensor_tensor_scan(lows[:, 1, 1:256], lows[:, 0, 0:255], zeros[0:1, 0:255], 0.0, ALU.add, ALU.add))
            link(dve.scalar_tensor_tensor(out=lows[:, 2, :], in0=lows[:, 1, :], scalar=-float(P), in1=first[:, 0:256],
                                          op0=ALU.mult, op1=ALU.add))
            link(dve.tensor_scalar(tot_i[:, 0:1], lows[:, 1, chunks:chunks + 1], 1.0, None, ALU.add))
            link(dve.tensor_scalar(tot_i[:, 0:1], tot_i[:, 0:1], 1, None, ALU.bitwise_or))
            assert done[0] == N_LOWS
            dve.wait_ge(s_once, 2)
            link(dve.tensor_copy(s_both[:, :, :], psS[:, :].rearrange("p (a s) -> p a s", a=2)))
            for half in range(2):
                col = s_col[:, half, :]
                link(dve.tensor_scalar(col[:, 0:1], iota_col[:, :], float(half * P), None, ALU.add))
                link(dve.tensor_scalar(s_cmp[:, half, 0:chunks], s_both[:, 0, 0:chunks], col[:, 0:1], None, ALU.is_le))
                link(dve.tensor_reduce(col[:, 1:2], s_cmp[:, half, 0:chunks], X, ALU.add))
                link(dve.tensor_scalar(s_out_i[:, 1, half:half + 1], col[:, 1:2], -1.0, None, ALU.add))
                link(dve.tensor_scalar(s_cmp[:, half, 0:chunks + 1], s_both[:, 0, 0:chunks + 1], col[:, 0:1], 1e9,
                                       ALU.is_gt, ALU.mult))
                link(dve.tensor_tensor(s_cmp[:, half, 0:chunks + 1], s_cmp[:, half, 0:chunks + 1],
                                       s_both[:, 1, 0:chunks + 1], ALU.add))
                link(dve.tensor_reduce(col[:, 2:3], s_cmp[:, half, 0:chunks + 1], X, ALU.min))
                link(dve.scalar_tensor_tensor(out=col[:, 3:4], in0=col[:, 0:1], scalar=float(P), in1=col[:, 2:3],
                                              op0=ALU.mult, op1=ALU.add))
                link(dve.tensor_scalar(s_out_i[:, 0, half:half + 1], col[:, 3:4], float(N), None, ALU.min))
            assert done[0] == N_SETUP
            total = steps_to_run(dve)
            link(dve.tensor_copy(w_tab[:, :], step_tab[:, 0, :]))
            link(dve.tensor_copy(ident_b[:, :], ident[:, :]))
            dve2.credit(dve, ahead=["wcur*"])

            def next_wcur(at, lead):
                dve2.mark("wcur*", dve.tensor_copy(wcur[:, at.slot(lead), :], w_tab[:, bass.ds(at.number(lead), 2)]))

            def next_newseg(at, lead):
                s = at.slot(lead)
                dve.wait_ge(s_dst[s], at.landed(2, lead))
                dve2.mark("newseg*", dve.tensor_tensor(newseg[:, s, 1:P], dst_s[:, s, 1:P], dst_s[:, s, 0:P - 1],
                                                       ALU.not_equal))

            def next_node(at, lead):
                s = at.slot(lead)
                dve2.wait(dve, "wcur*", at, lead - 1)
                dve2.mark("node*", dve.tensor_tensor(node[:, s:s + 1], iota_col[:, :], wcur[:, s, 0:1], ALU.add))

            def next_pen(at, lead):
                s = at.slot(lead)
                dve2.wait(dve, "newseg*", at, lead - 1)
                dve2.mark("pen*", dve.tensor_scalar(pen[:, s, :], newseg[:, s, 0:P], -BIG, None, ALU.mult))

            def next_ohT(at, lead, half):
                s, c = at.slot(lead), slice(half * TILES // 2 * P, (half + 1) * TILES // 2 * P)
                pe2.wait(dve, "expand", at, lead - 2)
                dve2.wait(dve, "node*", at, lead - 1)
                dve2.mark(("ohT0*", "ohT*")[half],
                          dve.tensor_scalar(ohT[:, s, :, :].rearrange("p t n -> p (t n)")[:, c], dst_b[:, s, c],
                                            node[:, s:s + 1], None, ALU.is_equal))

            def step(at, follows):
                s, q = at.slot(), at.slot(-1)
                mark = dve2.mark

                def own(name, lead=0):
                    dve2.wait(dve, name, at, lead)

                def of_last(name, issue):
                    if follows:
                        mark(name, issue())
                    else:
                        dve2.skip(dve, [name], at)

                def head(ap, h):
                    return head_cols(ap)[:, h, :]

                def merge(h):
                    first_row = head(acc[0:1, 0:HC1], h)
                    of_last(f"merged{h}", lambda: dve.scalar_tensor_tensor(
                        out=first_row, in0=first_row, scalar=r_f[:, H + h:H + h + 1], in1=head(r_c[:, :], h),
                        op0=ALU.mult, op1=ALU.add))

                def num_of(h):
                    of_last(f"num{h}", lambda: dve.scalar_tensor_tensor(
                        out=head(num[:, :], h), in0=head(tab_w[:, q, 0:HC1], h), scalar=ws[:, h:h + 1],
                        in1=head(acc[:, 0:HC1], h), op0=ALU.mult, op1=ALU.add))

                def biased(h):
                    c = slice(h * C, (h + 1) * C)
                    of_last(f"biased{h}", lambda: dve.scalar_tensor_tensor(
                        out=o[:, c], in0=head(num[:, :], h)[:, 0:C], scalar=rden[:, h:h + 1], in1=g_aff[:, 0, c],
                        op0=ALU.mult, op1=ALU.add))

                def message(name):
                    t = 2 * MSGS.index(name)
                    mark(name, dve.tensor_tensor(
                        msg[:, s, t:t + 2, :].rearrange("p t (h c) -> p t h c", h=H),
                        rows[:, s, t:t + 2, 0:HC1].rearrange("p t (h c) -> p t h c", h=H),
                        over(we[:, s, t:t + 2, :], C + 1), ALU.mult))

                r_sc, r_mn = r_m[:, 0, :], r_m[:, 1, :]
                next_wcur(at, 1)
                act2.wait(dve, "carry", at, -1)
                of_last("r_t", lambda: dve.tensor_scalar(r_t[:, :], carry[:, HAS:HAS + 1], BIG, -BIG, ALU.mult, ALU.add))
                next_newseg(at, 1)
                own("r_t")
                of_last("r_sc", lambda: dve.tensor_scalar(r_sc, carry[:, SHIFT:HAS], r_t[:, 0:1], None, ALU.add))
                next_node(at, 1)
                own("r_sc")
                of_last("r_mn", lambda: dve.tensor_tensor(r_mn, r_sc, adsh[0:1, q, H:], ALU.max))
                next_pen(at, 1)
                own("r_mn")
                of_last("r_d1", lambda: dve.tensor_tensor(r_d[:, 0:H], r_sc, r_mn, ALU.subtract))
                of_last("r_d", lambda: dve.tensor_tensor(r_d[:, H:], adsh[0:1, q, H:], r_mn, ALU.subtract))
                pe2.wait(dve, "lT", at)
                mark("RUNMAX", dve.tensor_tensor_scan(runmax[:, :], pen[:, s, :], psT, -BIG, ALU.add, ALU.max))
                of_last("self_z", lambda: dve.tensor_tensor(zs[:, :], tab_w[:, q, AS:AD], tab_w[:, q, AD:TW], ALU.add))
                own("RUNMAX")
                mark("LASTMAX", dve.tensor_tensor(lastmax[:, :], runmax[:, :], newseg[:, s, 1:P + 1], ALU.mult))
                own("self_z")
                of_last("self_l", lambda: dve.scalar_tensor_tensor(out=zs[:, :], in0=zs[:, :], scalar=NEG_SLOPE,
                                                                   in1=zs[:, :], op0=ALU.mult, op1=ALU.max))
                next_ohT(at, 1, 0)
                pr, part = psR.rearrange("p (t r) -> p t r", r=R5), [last_p[:, :, i, :] for i in range(3)]
                pe2.wait(dve, "lastT", at)
                mark("LAST_HI", dve.tensor_copy(part[0], pr))
                pe2.wait(dve, "carry", at, -1)
                mark("SEL", dve.tensor_tensor(sel[:, s:s + 1], node[:, s:s + 1], wcur[:, s, 1:2], ALU.is_equal))
                own("LAST_HI")
                mark("LAST_R", dve.tensor_tensor(last_r[:, :, :], pr, part[0], ALU.subtract))
                mark("LAST_MID", dve.tensor_tensor(part[1], pr, part[0], ALU.subtract))
                act2.wait(dve, "lhs", at)
                mark("MASK", dve.tensor_tensor(mask[:, s:s + 1], node[:, s:s + 1], wcur[:, s, 1:2], ALU.is_lt))
                own("LAST_MID")
                mark("LAST_LO", dve.tensor_tensor(part[2], last_r[:, :, :], part[1], ALU.subtract))
                next_ohT(at, 1, 1)
                pe2.wait(dve, "nodemax", at)
                mark("NODE_V", dve.tensor_reduce(node_v[:, :, :], psM.rearrange("p (t a r) -> p t r a", a=3, r=R5),
                                                 X, ALU.add))
                act2.wait(dve, "acc", at)
                of_last("accshift", lambda: dve.tensor_copy(acc[:, SHIFT:HAS], adsh[:, q, H:]))
                own("NODE_V")
                mark("NOHAS", dve.tensor_scalar(nohas[:, :], node_v[:, :, 0], BIG, -BIG, ALU.mult, ALU.add))
                act2.wait(dve, "carried", at)
                merge(0)
                own("NOHAS")
                mark("MTILE", dve.tensor_tensor(mtile[:, :, :], node_v[:, :, 1:R5], over(nohas[:, :], H), ALU.add))
                merge(1)
                own("MTILE")
                mark("MNODE", dve.tensor_reduce(mnode[:, :], mtile[:, :, :].rearrange("p t h -> p h t"), X, ALU.max))
                merge(2)
                dve.wait_ge(s_win[s], at.landed(2))
                mark("AD", dve.tensor_copy(adsh[:, s, 0:H], tab_w[:, s, AD:TW]))
                own("MNODE")
                mark("MAXSELF", dve.tensor_tensor(mnode[:, :], mnode[:, :], tab_w[:, s, AS:AD], ALU.max))
                merge(3)
                own("MAXSELF")
                mark("ZN", dve.tensor_tensor(zn[:, :], mnode[:, :], tab_w[:, s, AD:TW], ALU.add))
                own("accshift")
                of_last("mergedshift", lambda: dve.tensor_copy(acc[0:1, SHIFT:HAS], r_mn))
                own("ZN")
                mark("SHIFT", dve.scalar_tensor_tensor(out=adsh[:, s, H:], in0=zn[:, :], scalar=NEG_SLOPE, in1=zn[:, :],
                                                       op0=ALU.mult, op1=ALU.max))
                own("mergedshift")
                of_last("self_d", lambda: dve.tensor_tensor(zs[:, :], zs[:, :], acc[:, SHIFT:HAS], ALU.subtract))
                part = [adsh_p[:, i, :] for i in range(3)]
                own("SHIFT")
                mark("HI", dve.tensor_copy(part[0], adsh[:, s, :]))
                own("HI")
                mark("REST", dve.tensor_tensor(adsh_r[:, :], adsh[:, s, :], part[0], ALU.subtract))
                mark("MID", dve.tensor_tensor(part[1], adsh[:, s, :], part[0], ALU.subtract))
                own("MID")
                mark("LO", dve.tensor_tensor(part[2], adsh_r[:, :], part[1], ALU.subtract))
                act2.wait(dve, "wself", at)
                own("merged3")
                for h in range(H):
                    num_of(h)
                pe2.wait(dve, "expand", at)
                mark("EDGE_V", dve.tensor_reduce(edge_v[:, :, :], psE.rearrange("p (t a r) -> p t r a", a=3, r=2 * H),
                                                 X, ALU.add))
                own("num3")
                of_last("den", lambda: dve.tensor_scalar(rden[:, :], head_cols(num[:, :])[:, :, C], DEN_EPS, None, ALU.add))
                own("EDGE_V")
                mark("ZE", dve.tensor_tensor(ze[:, :, :], rows[:, s, :, AS:AD], edge_v[:, :, 0:H], ALU.add))
                own("den")
                of_last("rden", lambda: dve.reciprocal(rden[:, :], rden[:, :]))
                own("ZE")
                mark("LE", dve.scalar_tensor_tensor(out=ze[:, :, :], in0=ze[:, :, :], scalar=NEG_SLOPE,
                                                    in1=ze[:, :, :], op0=ALU.mult, op1=ALU.max))
                own("rden")
                biased(0)
                biased(1)
                own("LE")
                act2.wait(dve, "we", at, -1)
                mark("D", dve.tensor_tensor(le[:, :, :], ze[:, :, :], edge_v[:, :, H:], ALU.subtract))
                biased(2)
                own("D")
                mark("DMIN", dve.tensor_scalar(le[:, :, :], le[:, :, :], 0.0, None, ALU.min))
                biased(3)
                own("biased3")
                of_last("st", lambda: dve.bn_stats(st2[:, :], o[:, :]))
                act2.wait(dve, "we", at)
                pe2.wait(dve, "agg", at, -1)
                message(MSGS[0])
                own("st")
                hold(dve, s_dve_held)
                of_last("mv", lambda: dve.bn_aggr(mv2[:, 0:2], st2[:, :]))
                message(MSGS[1])
                own("mv")
                of_last("gam", lambda: dve.scalar_tensor_tensor(out=o[:, :], in0=o[:, :], scalar=mv2[:, 0:1],
                                                                in1=g_aff[:, 1, :], op0=ALU.subtract, op1=ALU.mult))
                message(MSGS[2])
                act2.wait(dve, "y1", at)
                own("gam")
                of_last("normed", lambda: dve.scalar_tensor_tensor(out=o[:, :], in0=o[:, :], scalar=ln2[:, 1:2],
                                                                   in1=g_aff[:, 2, :], op0=ALU.mult, op1=ALU.add))
                message(MSGS[3])
                own("normed")
                sp2.wait(dve, "stored", at, -1)
                pe2.wait(dve, "router", at, -1)
                of_last("xmid", lambda: dve.scalar_tensor_tensor(out=x_o[:, q, 0:D], in0=o[:, :], scalar=0.0,
                                                                 in1=x_w[:, q, :], op0=ALU.max, op1=ALU.add))
                for name in MSGS[4:]:
                    message(name)
                own("xmid")
                of_last("st_m", lambda: dve.bn_stats(st2[:, :], x_o[:, q, 0:D]))
                act2.wait(dve, "ln2", at)
                own("st_m")
                hold(dve, s_dve_held)
                of_last("mv_m", lambda: dve.bn_aggr(x_o[:, q, D:D + 2], st2[:, :]))

            start = At(0, 2, 0)
            for stage, name, then in ((next_wcur, "wcur*", "newseg*"), (next_newseg, "newseg*", "node*"),
                                      (next_node, "node*", "pen*"), (next_pen, "pen*", "ohT0*"),
                                      (lambda at, lead: next_ohT(at, lead, 0), "ohT0*", "ohT*"),
                                      (lambda at, lead: next_ohT(at, lead, 1), "ohT*", None)):
                stage(start, 0)
                dve2.rest(dve, [name], [then] if then else None)
            walk(dve, total, step)

            link(dve.drain())
            assert done[0] == N_WALKED
            dve.wait_ge(s_once, 3)
            link(dve.tensor_copy(zrow[:, :], psZ))
            link(dve.tensor_scalar(zrow[:, 0:D], zrow[:, 0:D], zrow[:, D:D + 1], 1.0 / N, ALU.subtract, ALU.mult))
            assert done[0] == N_MEAN
            dve.wait_ge(s_once, 4)
            link(dve.tensor_copy(zcol[:, :], bank[0][:, 0:KD]))
            dve.wait_ge(s_once, 5)
            link(dve.tensor_tensor(rt[:, 1, :], bank[1][0:1, 0:NE], rt[:, 0, :], ALU.add))

            exps = [0]

            def softmax(src, to):
                link(dve.tensor_reduce(rt[:, 15, 0:1], rt[:, src, :], X, ALU.max))
                link(dve.tensor_scalar(rt[:, 14, :], rt[:, src, :], rt[:, 15, 0:1], None, ALU.subtract))
                assert done[0] == N_EXP[exps[0]]
                exps[0] += 1
                dve.wait_ge(s_exp, exps[0])
                link(dve.tensor_reduce(rt[:, 15, 1:2], rt[:, 13, :], X, ALU.add))
                link(dve.reciprocal(rt[:, 15, 2:3], rt[:, 15, 1:2]))
                link(dve.tensor_scalar(rt[:, to, :], rt[:, 13, :], rt[:, 15, 2:3], None, ALU.mult))

            softmax(1, 2)
            capacity = float(math.ceil(N * CAPACITY_FACTOR / NE))
            link(dve.tensor_scalar(rt[:, 3, :], rt[:, 2, :], float(N), 1e-30, ALU.mult, ALU.max))
            link(dve.reciprocal(rt[:, 4, :], rt[:, 3, :]))
            link(dve.tensor_scalar(rt[:, 5, :], rt[:, 4, :], capacity, 1.0, ALU.mult, ALU.min))
            link(dve.tensor_tensor(rt[:, 6, :], rt[:, 5, :], rt[:, 2, :], ALU.mult))
            softmax(6, 7)
            link(dve.max(rt[:, 8, :], rt[:, 7, :]))
            link(dve.max_index(top_i[:, :], rt[:, 8, :], rt[:, 7, :]))
            link(dve.tensor_copy(top_ii[:, :], top_i[:, :]))
            link(dve.tensor_scalar(rt[:, 14, :], rt[:, 8, :], rt[:, 8, 0:1], None, ALU.subtract))
            assert done[0] == N_EXP[exps[0]]
            dve.wait_ge(s_exp, exps[0] + 1)
            link(dve.tensor_reduce(rt[:, 15, 1:2], rt[:, 13, 0:2], X, ALU.add))
            link(dve.reciprocal(rt[:, 15, 2:3], rt[:, 15, 1:2]))
            link(dve.tensor_scalar(rt[:, WTOP, 0:2], rt[:, 13, 0:2], rt[:, 15, 2:3], None, ALU.mult))
            assert done[0] == N_TOP
            dve.wait_ge(s_once, 6)
            link(dve.tensor_copy(wtop[:, :], bank[2][:, 0:2]))
            dve.wait_ge(s_fw, 128)
            for i in range(2):
                flat = w2_sb[:, i, :, :].rearrange("p k d -> p (k d)")
                link(dve.tensor_scalar(flat, flat, wtop[:, i:i + 1], None, ALU.mult))
            link(dve.tensor_scalar(b2_w[:, :], b2_sb[:, 0, :], wtop[:, 0:1], None, ALU.mult))
            link(dve.scalar_tensor_tensor(out=b2_w[:, :], in0=b2_sb[:, 1, :], scalar=wtop[:, 1:2], in1=b2_w[:, :],
                                          op0=ALU.mult, op1=ALU.add))
            assert done[0] == N_EXPERT
            dve3.credit(dve, ahead=DVE3_A)

            def normalise(at, at3, lead):
                s = at.slot(lead)
                dve.wait_ge(s_fx[at3.slot(lead)], at3.landed(1, lead))
                rstd_of(at, lead - 1, ["st", "mv"] + ROOT, lambda q: fx[:, at3.slot(lead), q, :])
                for q in range(QB):
                    ins = dve.tensor_scalar(fxn[:, s, q, :], fx[:, at3.slot(lead), q, :], fmv[:, q, 0:1],
                                            ft[:, q:q + 1], ALU.subtract, ALU.mult)
                dve3.mark("xn", ins)
                pe3.wait(dve, "xT", at, lead - 1)
                for k in range(KD):
                    ins = dve.tensor_copy(fxT[:, s, k, :], psF[k])
                dve3.mark("xT", ins)

            def rstd_of(at, lead, names, rows_of):
                def own(name):
                    dve3.wait(dve, name, at, lead)

                for q in range(QB):
                    ins = dve.bn_stats(fst[:, q, :], rows_of(q))
                dve3.mark(names[0], ins)
                own(names[0])
                hold(dve, s_dve_held)
                for q in range(QB):
                    ins = dve.bn_aggr(fmv[:, q, :], fst[:, q, :])
                dve3.mark(names[1], ins)
                own(names[1])
                dve3.mark(names[2], dve.tensor_scalar(fv[:, :], fmv[:, :, 1], LN_EPS, None, ALU.add))
                dve3.mark(names[3], dve.tensor_scalar(fh[:, :], fmv[:, :, 1], LN_EPS, -0.5, ALU.add, ALU.mult))
                own(names[2])
                dve3.mark(names[4], dve.tensor_scalar(ft[:, :].bitcast(I32), fv[:, :].bitcast(I32), -0.5,
                                                      ROOT_SEED, ALU.mult, ALU.add))
                own(names[4])
                for n in range(5, 14, 3):
                    dve3.mark(names[n], dve.tensor_tensor(fq[:, :], ft[:, :], ft[:, :], ALU.mult))
                    own(names[n])
                    dve3.mark(names[n + 1], dve.tensor_tensor(fq[:, :], fq[:, :], fh[:, :], ALU.mult))
                    own(names[n + 1])
                    dve3.mark(names[n + 2], dve.scalar_tensor_tensor(out=ft[:, :], in0=fq[:, :], scalar=1.5,
                                                                     in1=ft[:, :], op0=ALU.add, op1=ALU.mult))
                    own(names[n + 2])

            def group(at, at3):
                s = at.slot()
                y = fo[:, s, :, :]

                def own(name):
                    dve3.wait(dve, name, at)

                normalise(at, at3, 1)
                pe3.wait(dve, "out", at)
                sp3.wait(dve, "stored", at, -2)
                for i in range(2):
                    ins = dve.tensor_tensor(y[:, 2 * i:2 * i + 2, :], psY[i], fxn[:, s, 2 * i:2 * i + 2, :], ALU.add)
                dve3.mark("res", ins)
                own("res")
                dve3.mark("b2", dve.tensor_tensor(y, y, b2_w[:, :].unsqueeze(1).to_broadcast([P, QB, D]), ALU.add))
                own("b2")
                rstd_of(at, 0, ["st2", "mv2"] + ROOT2, lambda q: y[:, q, :])
                for q in range(QB):
                    ins = dve.scalar_tensor_tensor(out=y[:, q, :], in0=y[:, q, :], scalar=fmv[:, q, 0:1],
                                                   in1=f_aff[:, 0, :], op0=ALU.subtract, op1=ALU.mult)
                dve3.mark("gam", ins)
                own("gam")
                for q in range(QB):
                    ins = dve.scalar_tensor_tensor(out=y[:, q, :], in0=y[:, q, :], scalar=ft[:, q:q + 1],
                                                   in1=f_aff[:, 1, :], op0=ALU.mult, op1=ALU.add)
                dve3.mark("normed", ins)
                own("normed")
                dve3.mark("out", dve.tensor_tensor(y, y, fx[:, at3.slot(), :, :], ALU.add))

            normalise(At(0, 2, 0), At(0, 3, 0), 0)
            dve3.rest(dve, DVE3_A)
            with dve.Fori(0, (GROUPS - 1) // 6) as k:
                for j in range(6):
                    group(At(k * 3, 2, j), At(k * 2, 3, j))
            group(At(0, 2, GROUPS - 1), At(0, 3, GROUPS - 1))


def kernel(**inputs):
    import numpy as _np
    import concourse.bacc as _bacc
    from concourse.bass_utils import run_bass_kernel_spmd as _run

    N, E = inputs["x"].shape[0], inputs["src"].shape[0]
    chunks, _, blocks, _ = sizes(N, E)
    padded = chunks * CHUNK
    host = {k: _np.ascontiguousarray(v) for k, v in inputs.items()}
    rows = _np.zeros(((blocks + ROWS_RING - 1) * P, host["x"].shape[1]), host["x"].dtype)
    rows[:N] = host["x"]
    src = _np.zeros(padded, host["src"].dtype)
    src[:E] = host["src"]
    dst = _np.full(padded, PAD_NODE, host["dst"].dtype)
    dst[:E] = host["dst"]

    def tiles(a):
        return _np.ascontiguousarray(a.reshape(chunks, TILES, P).transpose(0, 2, 1)).reshape(chunks * P, TILES)

    arrays = {"x_rows": rows, "src_tiles": tiles(src), "dst": dst}
    arrays.update((k, host[k]) for k in _WEIGHTS)
    nc = _bacc.Bacc("TRN2", target_bir_lowering=False, num_devices=1)
    args = [nc.dram_tensor(f"in_{k}", a.shape, mybir.dt.from_np(a.dtype), kind="ExternalInput").ap()
            for k, a in arrays.items()]
    args.append(nc.dram_tensor("out_0", (N, rows.shape[1]), F32, kind="ExternalOutput").ap())
    build(nc, *args, N, E)
    r = _run(nc, [{f"in_{k}": a for k, a in arrays.items()}], core_ids=[0])
    return r.results[0]["out_0"]


PAD_NODE = 1 << 20
_WEIGHTS = ["L0_gnn_W", "L0_gnn_att_src", "L0_gnn_att_dst", "L0_gnn_bias", "L0_gnn_ln_gamma", "L0_gnn_ln_beta",
            "L0_ffn_Wr", "L0_ffn_br", "L0_ffn_W1", "L0_ffn_b1", "L0_ffn_W2", "L0_ffn_b2", "L0_ffn_gamma",
            "L0_ffn_beta"]
```
